# Optimizing a Trainium2 kernel written in Bass

```python
import numpy as np
import jax
import jax.numpy as jnp

def _softmax(x, axis=-1):
    return jax.nn.softmax(x, axis=axis)

def _gelu(x):
    return jax.nn.gelu(x, approximate=True)

def _silu(x):
    return jax.nn.silu(x)

def _sigmoid(x):
    return jax.nn.sigmoid(x)

def _layernorm(x, axis=-1, eps=1e-05):
    m = jnp.mean(x, axis=axis, keepdims=True)
    v = jnp.var(x, axis=axis, keepdims=True)
    return (x - m) / jnp.sqrt(v + eps)

def _scatter_add(tgt, idx, src, axis=0):
    return tgt.at[idx].add(src)

def _segment_sum(src, seg, n):
    return jax.ops.segment_sum(src, seg, n)
kernel_name = 'mk_hybrid_d1_jaxref_r8_0bd564'

def setup_inputs(seed: int=0):
    np.random.seed(seed)
    _w = jnp.asarray

    def _L0_attn_a_setup():
        import jax, jax.numpy as jnp
        import numpy as np
        DIM = 256
        HEADS = 16
        HEAD_DIM = DIM // HEADS
        RANK = 16
        ALPHA = 8.0
        SCALING = ALPHA / RANK
        SCALE = HEAD_DIM ** (-0.5)

        def lora_linear(x, W, b, Bm, Am):
            out = jnp.einsum('bld,od->blo', x, W) + b
            upd = jnp.einsum('blr,or->blo', jnp.einsum('bld,rd->blr', x, Bm), Am)
            return out + SCALING * upd

        def _split(t):
            B, L, D = t.shape
            return t.reshape(B, L, HEADS, HEAD_DIM).transpose(0, 2, 1, 3)
        key = jax.random.key(seed)
        ks = jax.random.split(key, 20)
        B, L = (4, 256)
        x = jax.random.normal(ks[0], (B, L, DIM), dtype=jnp.float32)
        s = 0.02
        inp = {'x': x}
        for i, name in enumerate(['q', 'k', 'v', 'o']):
            inp[f'W{name}'] = jax.random.normal(ks[1 + 4 * i], (DIM, DIM), jnp.float32) * s
            inp[f'b{name}'] = jax.random.normal(ks[2 + 4 * i], (DIM,), jnp.float32) * s
            inp[f'B{name}'] = jax.random.normal(ks[3 + 4 * i], (RANK, DIM), jnp.float32) * s
            inp[f'A{name}'] = jax.random.uniform(ks[4 + 4 * i], (DIM, RANK), jnp.float32, -0.1, 0.1)
        return inp
    _L0_attn_a_in = _L0_attn_a_setup()

    def _L0_attn_b_setup():
        import jax, jax.numpy as jnp
        import numpy as np
        H = 8
        DK = 32
        DV = 64
        EPS = 1e-05
        ROPE_BASE = 10000.0

        def _rope(x):
            B, T, h, d = x.shape
            inv_freq = 1.0 / ROPE_BASE ** (jnp.arange(0, d, 2, dtype=jnp.float32) / d)
            t = jnp.arange(T, dtype=jnp.float32)
            freqs = t[:, None] * inv_freq[None, :]
            cos = jnp.cos(freqs)[None, :, None, :]
            sin = jnp.sin(freqs)[None, :, None, :]
            x1, x2 = (x[..., :d // 2], x[..., d // 2:])
            return jnp.concatenate([x1 * cos - x2 * sin, x2 * cos + x1 * sin], axis=-1)
        key = jax.random.key(seed)
        ks = jax.random.split(key, 7)
        hidden = 256
        B, T = (2, 256)
        w = 0.02
        return {'hidden_states': jax.random.normal(ks[0], (B, T, hidden), jnp.float32), 'Wq': jax.random.normal(ks[1], (hidden, H * DK), jnp.float32) * w, 'Wk': jax.random.normal(ks[2], (hidden, H * DK), jnp.float32) * w, 'Wv': jax.random.normal(ks[3], (hidden, H * DV), jnp.float32) * w, 'Wg': jax.random.normal(ks[4], (hidden, H * DV), jnp.float32) * w, 'Wo': jax.random.normal(ks[5], (H * DV, hidden), jnp.float32) * w, 'g_norm_weight': jnp.ones((DV,), jnp.float32)}
    _L0_attn_b_in = _L0_attn_b_setup()

    def _L0_ffn_setup():
        import jax, jax.numpy as jnp
        import numpy as np
        DIM = 256
        EXPERT_DIM = 128
        N_EXPERTS = 16
        TOPK = 2
        N_SHARED = 1
        B, T = (4, 256)
        key = jax.random.key(seed)
        ks = jax.random.split(key, 9)
        s = 0.02
        return {'x': jax.random.normal(ks[0], (B, T, DIM), jnp.float32), 'router_w': jax.random.normal(ks[1], (N_EXPERTS, DIM), jnp.float32) * s, 'router_bias': jnp.zeros((N_EXPERTS,), jnp.float32), 'Wu': jax.random.normal(ks[2], (N_EXPERTS, DIM, EXPERT_DIM), jnp.float32) * s, 'Wg': jax.random.normal(ks[3], (N_EXPERTS, DIM, EXPERT_DIM), jnp.float32) * s, 'Wd': jax.random.normal(ks[4], (N_EXPERTS, EXPERT_DIM, DIM), jnp.float32) * s, 'Su': jax.random.normal(ks[5], (N_SHARED, DIM, EXPERT_DIM * TOPK), jnp.float32) * s, 'Sg': jax.random.normal(ks[6], (N_SHARED, DIM, EXPERT_DIM * TOPK), jnp.float32) * s, 'Sd': jax.random.normal(ks[7], (N_SHARED, EXPERT_DIM * TOPK, DIM), jnp.float32) * s}
    _L0_ffn_in = _L0_ffn_setup()
    _d = {'L0_attn_a_x': _L0_attn_a_in['x'], 'L0_attn_a_Wq': _L0_attn_a_in['Wq'], 'L0_attn_a_bq': _L0_attn_a_in['bq'], 'L0_attn_a_Bq': _L0_attn_a_in['Bq'], 'L0_attn_a_Aq': _L0_attn_a_in['Aq'], 'L0_attn_a_Wk': _L0_attn_a_in['Wk'], 'L0_attn_a_bk': _L0_attn_a_in['bk'], 'L0_attn_a_Bk': _L0_attn_a_in['Bk'], 'L0_attn_a_Ak': _L0_attn_a_in['Ak'], 'L0_attn_a_Wv': _L0_attn_a_in['Wv'], 'L0_attn_a_bv': _L0_attn_a_in['bv'], 'L0_attn_a_Bv': _L0_attn_a_in['Bv'], 'L0_attn_a_Av': _L0_attn_a_in['Av'], 'L0_attn_a_Wo': _L0_attn_a_in['Wo'], 'L0_attn_a_bo': _L0_attn_a_in['bo'], 'L0_attn_a_Bo': _L0_attn_a_in['Bo'], 'L0_attn_a_Ao': _L0_attn_a_in['Ao'], 'L0_attn_b_Wq': _L0_attn_b_in['Wq'], 'L0_attn_b_Wk': _L0_attn_b_in['Wk'], 'L0_attn_b_Wv': _L0_attn_b_in['Wv'], 'L0_attn_b_Wg': _L0_attn_b_in['Wg'], 'L0_attn_b_Wo': _L0_attn_b_in['Wo'], 'L0_attn_b_g_norm_weight': _L0_attn_b_in['g_norm_weight'], 'L0_ffn_router_w': _L0_ffn_in['router_w'], 'L0_ffn_router_bias': _L0_ffn_in['router_bias'], 'L0_ffn_Wu': _L0_ffn_in['Wu'], 'L0_ffn_Wg': _L0_ffn_in['Wg'], 'L0_ffn_Wd': _L0_ffn_in['Wd'], 'L0_ffn_Su': _L0_ffn_in['Su'], 'L0_ffn_Sg': _L0_ffn_in['Sg'], 'L0_ffn_Sd': _L0_ffn_in['Sd']}
    _x0 = _d['L0_attn_a_x']
    _d['L0_attn_a_x'] = jax.random.normal(jax.random.fold_in(jax.random.key(seed), 1), (2, 1024, 256), dtype=_x0.dtype)
    del _x0
    return _d

def reference(L0_attn_a_x, L0_attn_a_Wq, L0_attn_a_bq, L0_attn_a_Bq, L0_attn_a_Aq, L0_attn_a_Wk, L0_attn_a_bk, L0_attn_a_Bk, L0_attn_a_Ak, L0_attn_a_Wv, L0_attn_a_bv, L0_attn_a_Bv, L0_attn_a_Av, L0_attn_a_Wo, L0_attn_a_bo, L0_attn_a_Bo, L0_attn_a_Ao, L0_attn_b_Wq, L0_attn_b_Wk, L0_attn_b_Wv, L0_attn_b_Wg, L0_attn_b_Wo, L0_attn_b_g_norm_weight, L0_ffn_router_w, L0_ffn_router_bias, L0_ffn_Wu, L0_ffn_Wg, L0_ffn_Wd, L0_ffn_Su, L0_ffn_Sg, L0_ffn_Sd):

    def _L0_attn_a_ref(x, Wq, bq, Bq, Aq, Wk, bk, Bk, Ak, Wv, bv, Bv, Av, Wo, bo, Bo, Ao):
        import jax, jax.numpy as jnp
        import numpy as np
        DIM = 256
        HEADS = 16
        HEAD_DIM = DIM // HEADS
        RANK = 16
        ALPHA = 8.0
        SCALING = ALPHA / RANK
        SCALE = HEAD_DIM ** (-0.5)

        def lora_linear(x, W, b, Bm, Am):
            out = jnp.einsum('bld,od->blo', x, W) + b
            upd = jnp.einsum('blr,or->blo', jnp.einsum('bld,rd->blr', x, Bm), Am)
            return out + SCALING * upd

        def _split(t):
            B, L, D = t.shape
            return t.reshape(B, L, HEADS, HEAD_DIM).transpose(0, 2, 1, 3)
        q = _split(lora_linear(x, Wq, bq, Bq, Aq))
        k = _split(lora_linear(x, Wk, bk, Bk, Ak))
        v = _split(lora_linear(x, Wv, bv, Bv, Av))
        scores = jnp.einsum('bhqd,bhkd->bhqk', q, k) * SCALE
        attn = jax.nn.softmax(scores, axis=-1)
        out = jnp.einsum('bhqk,bhkd->bhqd', attn, v)
        B, H, L, hd = out.shape
        out = out.transpose(0, 2, 1, 3).reshape(B, L, H * hd)
        return lora_linear(out, Wo, bo, Bo, Ao)

    def _L0_attn_b_ref(hidden_states, Wq, Wk, Wv, Wg, Wo, g_norm_weight):
        import jax, jax.numpy as jnp
        import numpy as np
        H = 8
        DK = 32
        DV = 64
        EPS = 1e-05
        ROPE_BASE = 10000.0

        def _rope(x):
            B, T, h, d = x.shape
            inv_freq = 1.0 / ROPE_BASE ** (jnp.arange(0, d, 2, dtype=jnp.float32) / d)
            t = jnp.arange(T, dtype=jnp.float32)
            freqs = t[:, None] * inv_freq[None, :]
            cos = jnp.cos(freqs)[None, :, None, :]
            sin = jnp.sin(freqs)[None, :, None, :]
            x1, x2 = (x[..., :d // 2], x[..., d // 2:])
            return jnp.concatenate([x1 * cos - x2 * sin, x2 * cos + x1 * sin], axis=-1)
        B, T, _ = hidden_states.shape
        q = (hidden_states @ Wq).reshape(B, T, H, DK)
        k = (hidden_states @ Wk).reshape(B, T, H, DK)
        v = (hidden_states @ Wv).reshape(B, T, H, DV)
        g = (hidden_states @ Wg).reshape(B, T, H, DV)
        q = _rope(q)
        k = _rope(k)
        gamma = 1.0 - jnp.exp2(-5.0 - jnp.arange(H, dtype=jnp.float32))
        idx = jnp.arange(T)
        diff = idx[:, None] - idx[None, :]
        causal = diff >= 0
        log2g = jnp.log2(gamma)[:, None, None]
        D = jnp.where(causal[None], jnp.exp2(log2g * jnp.where(causal, diff, 0)[None]), 0.0)
        scale = DK ** (-0.5)
        scores = jnp.einsum('bihd,bjhd->bhij', q * scale, k) * D[None]
        o = jnp.einsum('bhij,bjhd->bihd', scores, v)
        rms = jax.lax.rsqrt(jnp.mean(o * o, axis=-1, keepdims=True) + EPS)
        o = o * rms * g_norm_weight
        o = o * (g * jax.nn.sigmoid(g))
        return o.reshape(B, T, H * DV) @ Wo

    def _L0_ffn_ref(x, router_w, router_bias, Wu, Wg, Wd, Su, Sg, Sd):
        import jax, jax.numpy as jnp
        import numpy as np
        DIM = 256
        EXPERT_DIM = 128
        N_EXPERTS = 16
        TOPK = 2
        N_SHARED = 1
        B, T = (4, 256)
        Bx, Tx, D = x.shape
        flat = x.reshape(Bx * Tx, D)
        logits = flat @ router_w.T
        scores = jax.nn.softmax(logits, axis=-1)
        _, topk_idx = jax.lax.top_k(logits + router_bias, TOPK)
        topk_scores = jnp.take_along_axis(scores, topk_idx, axis=-1)
        topk_scores = topk_scores / topk_scores.sum(-1, keepdims=True)
        combine = jnp.einsum('nk,nke->ne', topk_scores, jax.nn.one_hot(topk_idx, N_EXPERTS, dtype=scores.dtype))
        out = jnp.zeros_like(flat)
        for e in range(N_EXPERTS):
            h = jax.nn.silu(flat @ Wu[e]) * (flat @ Wg[e])
            out = out + combine[:, e:e + 1] * (h @ Wd[e])
        for s in range(N_SHARED):
            out = out + jax.nn.silu(flat @ Su[s]) * (flat @ Sg[s]) @ Sd[s]
        return out.reshape(Bx, Tx, D)
    x = L0_attn_a_x
    x = x + _L0_attn_a_ref(_layernorm(x, axis=-1), L0_attn_a_Wq, L0_attn_a_bq, L0_attn_a_Bq, L0_attn_a_Aq, L0_attn_a_Wk, L0_attn_a_bk, L0_attn_a_Bk, L0_attn_a_Ak, L0_attn_a_Wv, L0_attn_a_bv, L0_attn_a_Bv, L0_attn_a_Av, L0_attn_a_Wo, L0_attn_a_bo, L0_attn_a_Bo, L0_attn_a_Ao)
    x = x + _L0_ffn_ref(_layernorm(x, axis=-1), L0_ffn_router_w, L0_ffn_router_bias, L0_ffn_Wu, L0_ffn_Wg, L0_ffn_Wd, L0_ffn_Su, L0_ffn_Sg, L0_ffn_Sd)
    x = x + _L0_attn_b_ref(_layernorm(x, axis=-1), L0_attn_b_Wq, L0_attn_b_Wk, L0_attn_b_Wv, L0_attn_b_Wg, L0_attn_b_Wo, L0_attn_b_g_norm_weight)
    x = x + _L0_ffn_ref(_layernorm(x, axis=-1), L0_ffn_router_w, L0_ffn_router_bias, L0_ffn_Wu, L0_ffn_Wg, L0_ffn_Wd, L0_ffn_Su, L0_ffn_Sg, L0_ffn_Sd)
    return x

_drawn_inputs = setup_inputs


def setup_inputs(seed=0):
    import zlib

    import numpy as np

    out = dict(_drawn_inputs(seed))
    spreads = {'L0_attn_b_g_norm_weight': (1.0, 0.6), 'L0_ffn_router_bias': (0.0, 2.0)}
    factors = {'L0_attn_a_Wq': 8.0,
     'L0_attn_a_bq': 8.0,
     'L0_attn_a_Bq': 8.0,
     'L0_attn_a_Aq': 8.0,
     'L0_attn_a_Wk': 8.0,
     'L0_attn_a_bk': 200.0,
     'L0_attn_a_Bk': 8.0,
     'L0_attn_a_Ak': 8.0,
     'L0_attn_a_Wv': 8.0,
     'L0_attn_a_bv': 8.0,
     'L0_attn_a_Bv': 8.0,
     'L0_attn_a_Av': 8.0,
     'L0_attn_a_Wo': 7.924,
     'L0_attn_a_bo': 23.064,
     'L0_attn_a_Bo': 8.0,
     'L0_attn_a_Ao': 8.0,
     'L0_ffn_router_w': 3.651,
     'L0_ffn_Wu': 3.397,
     'L0_ffn_Wg': 3.359,
     'L0_ffn_Wd': 3.359,
     'L0_attn_b_Wq': 5.244,
     'L0_attn_b_Wk': 5.309,
     'L0_attn_b_Wv': 5.193,
     'L0_attn_b_Wg': 5.324,
     'L0_attn_b_Wo': 5.268,
     'L0_ffn_Su': 8.0,
     'L0_ffn_Sg': 8.0,
     'L0_ffn_Sd': 8.0}
    for name, (base, spread) in spreads.items():
        noise = np.random.default_rng([zlib.crc32(name.encode()), seed]).standard_normal(out[name].shape)
        drawn = base * np.exp(spread * noise) if base else spread * noise
        out[name] = jnp.asarray(drawn.astype(out[name].dtype))
    for name, factor in factors.items():
        out[name] = (out[name] * factor).astype(out[name].dtype)
    return out
```

```python
from contextlib import ExitStack

import numpy as np
import concourse.bass as bass
from concourse import mybir

F32 = mybir.dt.float32
F32R = mybir.dt.float32r
BF16 = mybir.dt.bfloat16
U32 = mybir.dt.uint32
ALU = mybir.AluOpType
ACT = mybir.ActivationFunctionType
AX_X = mybir.AxisListType.X

P = 128
B, L, D = 2, 1024, 256
N = B * L
NT = N // P
BLK = 512
NB = N // BLK
TPB = BLK // P
DH = D // P
EPS = 1e-5

HA, HDA, RANK = 16, 16, 16
SCALING = 8.0 / RANK
SCALE_A = HDA ** -0.5
HPG = 4
KT = L // P
TERMS = [(0, 0), (0, 1), (1, 0), (1, 1), (0, 2), (2, 0)]
KROWS = len(TERMS) * HDA
KEXP = KROWS + 3
JOBS = HPG * (BLK // P) * 2
RING = 3
RPS = JOBS + 1
SKEW = 3
TJ = 4

NE, ED = 16, 128
NU = NE + 2

HB, DK, DV = 8, 32, 64
QK = 2 * HB * DK
DVT = HB * DV


class Ctx:

    def __init__(self, nc, es, tag):
        self.nc, self.es, self.tag = nc, es, tag

    def sb(self, name, shape, dt=F32):
        return self.es.enter_context(self.nc.sbuf_tensor(f"{self.tag}_{name}", shape, dt))

    def ps(self, name, shape, dt=F32):
        return self.es.enter_context(self.nc.psum_tensor(f"{self.tag}_{name}", shape, dt))

    def sem(self, name):
        return self.es.enter_context(self.nc.semaphore(f"{self.tag}_{name}"))


def products(eng, out, lhs, rhs, first, last):
    pairs = [(0, 0), (0, 1), (1, 0)]
    for n, (a, b) in enumerate(pairs):
        mm = eng.matmul(out, lhs[a], rhs[b], start=first and n == 0, stop=last and n == 2)
    return mm


def normalise(nc, tag, x, ident, xt):
    with ExitStack() as es:
        c = Ctx(nc, es, tag)
        stats = c.sb("stats", [P, NT, 6])
        mv = c.sb("mv", [P, NT, 2])
        ve, nhalf, rstd = (c.sb(n, [P, NT, 1]) for n in ("ve", "nhalf", "rstd"))
        xn = c.sb("xn", [P, 2, TPB, D])
        pt = [c.ps(f"pt{n}", [P, BLK]) for n in range(4)]
        s_stats, s_mv, s_var, s_rstd = c.sem("stats"), c.sem("mv"), c.sem("var"), c.sem("rstd")
        s_half = c.sem("half")
        s_xn, s_t, s_hi, s_lo = c.sem("xn"), c.sem("transposed"), c.sem("hi"), c.sem("lo")
        block = es.enter_context(nc.Block())

        @block.vector
        def _(dve):
            for t in range(NT):
                dve.bn_stats(stats[:, t, :], x[:, t, :]).then_inc(s_stats, 1)
            for t in range(NT):
                dve.wait_ge(s_stats, t + 1)
                dve.bn_aggr(mv[:, t, :], stats[:, t, :]).then_inc(s_mv, 1)
            dve.wait_ge(s_mv, NT)
            dve.tensor_scalar(ve[:, :, :], mv[:, :, 1:2], EPS, None, ALU.add).then_inc(s_var, 1)
            dve.wait_ge(s_rstd, 1)

            def scale(b):
                if b >= 2:
                    dve.wait_ge(s_t, 2 * (b - 1))
                for j in range(TPB):
                    t = b * TPB + j
                    dve.tensor_scalar(xn[:, b % 2, j, :], x[:, t, :], mv[:, t, 0:1], rstd[:, t, :],
                                      ALU.subtract, ALU.mult).then_inc(s_xn, 1)

            scale(0)
            for b in range(NB):
                if b + 1 < NB:
                    scale(b + 1)
                for h in range(DH):
                    n = DH * b + h
                    dve.wait_ge(s_hi, n + 1)
                    dve.tensor_tensor(xt[1][:, h, b * BLK:(b + 1) * BLK], pt[n % 4][:, :],
                                      xt[0][:, h, b * BLK:(b + 1) * BLK].bitcast(F32),
                                      ALU.subtract).then_inc(s_lo, 1)

        @block.gpsimd
        def _(pool):
            pool.memset(nhalf[:, :, :], -0.5).then_inc(s_half, 1)
            pool.wait_ge(s_half, 1)
            pool.wait_ge(s_var, 1)
            pool.tensor_tensor(rstd[:, :, :], ve[:, :, :], nhalf[:, :, :], ALU.pow).then_inc(s_rstd, 1)

        @block.tensor
        def _(pe):
            for b in range(NB):
                pe.wait_ge(s_xn, TPB * (b + 1))
                for h in range(DH):
                    n = DH * b + h
                    if n >= 4:
                        pe.wait_ge(s_lo, n - 3)
                    for j in range(TPB):
                        mm = pe.transpose(pt[n % 4][:, j * P:(j + 1) * P],
                                          xn[:, b % 2, j, h * P:(h + 1) * P], ident[:, :])
                    mm.then_inc(s_t, 1)

        @block.scalar
        def _(act):
            for n in range(DH * NB):
                b, h = n // DH, n % DH
                act.wait_ge(s_t, n + 1)
                act.activation(xt[0][:, h, b * BLK:(b + 1) * BLK], pt[n % 4][:, :], ACT.Copy).then_inc(s_hi, 1)


def project_qkv(nc, io, x, xt, scratch, vaug, vb, bo, wo):
    with ExitStack() as es:
        c = Ctx(nc, es, "pj")
        wt = c.sb("wt", [P, 4, DH, D])
        bm = c.sb("bm", [RANK, 4, D])
        am = c.sb("am", [RANK, 4, D])
        bias = c.sb("bias", [P, 3, DH])
        biass = c.sb("biass", [P, 3, DH])
        weff = c.sb("weff", [P, 3, DH, D])
        whi = c.sb("whi", [P, 3, DH, D], F32R)
        wlo = c.sb("wlo", [P, 3, DH, D], F32R)
        xf = c.sb("xf", [P, 2, BLK])
        rf = c.sb("rf", [P, 2, BLK])
        parts = c.sb("parts", [P, 2, 3, BLK], BF16)
        pw = [c.ps(f"pw{n}", [P, BLK]) for n in range(2)]
        pp = [c.ps(f"pp{n}", [P, BLK]) for n in range(3)]
        pv = [c.ps(f"pv{n}", [P, BLK]) for n in range(2)]
        s_w, s_lora, s_weff, s_hi, s_lo, s_bias = (c.sem(n) for n in ("w", "lora", "weff", "whi", "wlo", "bias"))
        s_mm, s_xf, s_h, s_r, s_m, s_l = (c.sem(n) for n in ("mm", "xf", "h", "r", "m", "l"))
        s_st = [c.sem(f"stored{n}") for n in range(2)]
        s_vm, s_va, s_xb = c.sem("vmm"), c.sem("vadd"), c.sem("x_bias")
        JQ = 2 * DH * NB
        block = es.enter_context(nc.Block())

        @block.sync
        def _(sp):
            for n in range(4):
                sp.dma_start(wt[:, n, :, :], io["WT"][n].rearrange("(h p) o -> p h o", p=P)).then_inc(s_w, 16)
            sp.dma_start(bm[:, :, :], io["Bm"].rearrange("n r d -> r n d")).then_inc(s_w, 16)
            sp.dma_start(am[:, :, :], io["AmT"].rearrange("n r o -> r n o")).then_inc(s_w, 16)
            sp.dma_start(bias[:, :, :], io["biasT"]).then_inc(s_w, 16)
            for n in range(JQ):
                side, half, tb = n // (DH * NB), n // NB % DH, n % NB
                bb, off = tb * BLK // L, tb * BLK % L
                sp.wait_ge(s_l, n + 1)
                for k in range(3):
                    sp.dma_start(scratch[side, k, bb * DH + half].rearrange("u h r t -> (u h r) t")[:, off:off + BLK],
                                 parts[:, n % 2, k, :]).then_inc(s_st[n % 2], 16)
            for s_ in s_st:
                sp.wait_ge(s_, 16 * 3 * JQ // 2)

        @block.tensor
        def _(pe):
            pe.wait_ge(s_w, 16 * 7)
            for n in range(4):
                if n >= 2:
                    pe.wait_ge(s_weff, n - 1)
                for h in range(DH):
                    mm = pe.matmul(pw[n % 2][:, h * D:(h + 1) * D], bm[:, n, h * P:(h + 1) * P], am[:, n, :],
                                   start=True, stop=True)
                mm.then_inc(s_lora, 1)
            pe.wait_ge(s_hi, 3)
            pe.wait_ge(s_lo, 3)
            w = (whi, wlo)
            for n in range(JQ):
                side, half, tb = n // (DH * NB), n // NB % DH, n % NB
                if n >= 3:
                    pe.wait_ge(s_xf, n - 2)
                for h in range(DH):
                    mm = products(pe, pp[n % 3][:, :], [a[:, side, h, half * P:(half + 1) * P] for a in w],
                                  [a[:, h, tb * BLK:(tb + 1) * BLK] for a in xt], h == 0, h == DH - 1)
                mm.then_inc(s_mm, 1)
                t = n
                if t >= 2:
                    pe.wait_ge(s_va, t - 1)
                for h in range(DH):
                    mm = products(pe, pv[t % 2][:, 0:D], [a[:, h, t * P:(t + 1) * P] for a in xt],
                                  [a[:, 2, h, :] for a in w], h == 0, h == DH - 1)
                mm.then_inc(s_vm, 1)

        @block.gpsimd
        def _(pool):
            for t in range(NT):
                pool.tensor_tensor(x[:, t, :], x[:, t, :], bo[:, :], ALU.add).then_inc(s_xb, 1)

        @block.scalar
        def _(act):
            act.wait_ge(s_w, 16 * 7)
            act.mul(biass[:, :, :], bias[:, :, :], SCALE_A).then_inc(s_bias, 1)
            for n in range(3):
                act.wait_ge(s_weff, n + 1)
                act.activation(whi[:, n, :, :], weff[:, n, :, :], ACT.Copy).then_inc(s_hi, 1)
            act.wait_ge(s_bias, 1)
            for n in range(JQ):
                side, half = n // (DH * NB), n // NB % DH
                act.wait_ge(s_mm, n + 1)
                if n >= 2:
                    act.wait_ge(s_r, n - 1)
                    act.wait_ge(s_st[n % 2], 16 * 3 * (n // 2))
                b = biass if side == 0 else bias
                act.activation(xf[:, n % 2, :], pp[n % 3][:, :], ACT.Identity, bias=b[:, side, half:half + 1],
                               scale=SCALE_A if side == 0 else 1.0).then_inc(s_xf, 1)
                act.wait_ge(s_xf, n + 1)
                act.activation(parts[:, n % 2, 0, :], xf[:, n % 2, :], ACT.Copy).then_inc(s_h, 1)
                act.wait_ge(s_r, n + 1)
                act.activation(parts[:, n % 2, 1, :], rf[:, n % 2, :], ACT.Copy).then_inc(s_m, 1)

        @block.vector
        def _(dve):
            dve.wait_ge(s_w, 16 * 7)
            for n in range(4):
                dve.wait_ge(s_lora, n + 1)
                dve.scalar_tensor_tensor(out=weff[:, n, :, :] if n < 3 else wo[:, :, :], in0=pw[n % 2][:, :].rearrange("p (h o) -> p h o", h=DH),
                                         scalar=SCALING, in1=wt[:, n, :, :], op0=ALU.mult,
                                         op1=ALU.add).then_inc(s_weff, 1)
            for n in range(3):
                dve.wait_ge(s_hi, n + 1)
                dve.tensor_tensor(wlo[:, n, :, :], weff[:, n, :, :], whi[:, n, :, :].bitcast(F32),
                                  ALU.subtract).then_inc(s_lo, 1)
            for n in range(JQ):
                dve.wait_ge(s_h, n + 1)
                dve.tensor_tensor(rf[:, n % 2, :], xf[:, n % 2, :], parts[:, n % 2, 0, :], ALU.subtract).then_inc(s_r, 1)
                t = n
                dve.wait_ge(s_vm, t + 1)
                dve.tensor_tensor(vaug[:, t // KT, :, t % KT, :, 0:HDA],
                                  pv[t % 2][:, 0:D].rearrange("p (a h r) -> p a h r", a=DH, r=HDA),
                                  vb[:, :].rearrange("p (a h r) -> p a h r", a=DH, r=HDA), ALU.add).then_inc(s_va, 1)
                dve.wait_ge(s_m, n + 1)
                dve.tensor_tensor(parts[:, n % 2, 2, :], rf[:, n % 2, :], parts[:, n % 2, 1, :],
                                  ALU.subtract).then_inc(s_l, 1)


def attend(nc, scratch, vaug, oall, identb):
    STEPS = B * DH
    SUBS = 4
    with ExitStack() as es:
        c = Ctx(nc, es, "at")
        kst = [c.sb(f"kst{u}", [KEXP, HPG, L], BF16) for u in range(2)]
        qst = [c.sb(f"qst{u}", [KEXP, 2, HPG, BLK], BF16) for u in range(2)]
        vst = [c.sb(f"vst{u}", [P, KT, HPG, 32]) for u in range(2)]
        prob = [c.sb(f"prob{n}", [P, HPG, BLK]) for n in range(4)]
        mx = c.sb("mx", [P, JOBS])
        mrow = c.sb("mrow", [P, 2, JOBS // 2])
        mneg = c.sb("mneg", [P, JOBS // 2])
        mres = c.sb("mres", [P, JOBS // 2])
        zero = c.sb("zero", [P, JOBS // 2])
        msplit = c.sb("msplit", [P, P], BF16)
        mT = [c.sb(f"mT{n}", [P, P], BF16) for n in range(2)]
        ps_s = [c.ps(f"score{n}", [P, 2, BLK]) for n in range(2)]
        ps_m = [c.ps(f"max{n}", [P, BLK]) for n in range(RING)]
        ps_o = c.ps("out", [P, BLK])
        s_stack = [c.sem(f"stack_loaded{u}") for u in range(2)]
        s_rows, s_ones = c.sem("max_rows_loaded"), c.sem("ones")
        s_vst = c.sem("v_staged")
        s_score = [c.sem(f"scores_ready{n}") for n in range(2)]
        s_exp = [c.sem(f"exp_done{n}") for n in range(2)]
        s_pv, s_oev = c.sem("sub_values_done"), c.sem("out_evacuated")
        s_mm, s_free, s_chain, s_split = (c.sem(n) for n in ("max_ready", "max_bank_free", "max_chain", "max_split"))
        s_comb, s_zero = c.sem("max_combined"), c.sem("zero")
        SLOTS = SUBS * KT
        JPS = JOBS // KT
        UNIT_DMAS = 3 * len(TERMS)
        CH = 4
        block = es.enter_context(nc.Block())

        def sub(i, s):
            return SUBS * i + s

        def job_slot(n, j):
            if type(n) is int and n == 0:
                return j, j % RING
            k = j if j < TJ else j + 1
            return RPS * n + k - 1, (k - 1) % RING

        def turn_slot(n):
            k = TJ if type(n) is not int or n < SUBS * STEPS - 1 else 0
            return RPS * (n + 1) + k - 1, (k - 1) % RING

        @block.sync
        def _(sp):
            def load_unit(i, u):
                for n, (ck, cq) in enumerate(TERMS):
                    rows = slice(n * HDA, (n + 1) * HDA)
                    sp.dma_start(kst[u][rows, :, :], scratch[1, ck, i, u].rearrange("h r t -> r h t")).then_inc(s_stack[u], 16)
                    for qh in range(2):
                        sp.dma_start(qst[u][rows, qh, :, :],
                                     scratch[0, cq, i, u].rearrange("h r t -> r h t")[:, :, qh * BLK:(qh + 1) * BLK]
                                     ).then_inc(s_stack[u], 16)

            def load_rows(n, s):
                sp.wait_ge(s_free, turn_slot(n)[0] + 1)
                for k in range(3):
                    sp.dma_start(qst[s // 2][KROWS + k:KROWS + k + 1, s % 2, :, :].rearrange("o h (t j) -> o (h t) j", j=P),
                                 mT[s % 2][k * (JOBS // 2):(k + 1) * (JOBS // 2), :]).then_inc(s_rows, 16)

            load_unit(0, 0)
            load_unit(0, 1)
            load_rows(0, 0)

            def step(i, last):
                for s in range(SUBS):
                    if not (last and s == SUBS - 1):
                        load_rows(sub(i, s) + 1, (s + 1) % SUBS)
                    if s % 2 and not last:
                        sp.wait_ge(s_score[1], KT * (sub(i, s) + 1))
                        load_unit(i + 1, s // 2)

            with sp.Fori(0, STEPS - 1) as i:
                step(i, False)
            step(STEPS - 1, True)

        @block.gpsimd
        def _(pool):
            def stage(i, u):
                pool.tensor_copy(vst[u][:, :, :, :],
                                 vaug[:, :, :, :, :, :].rearrange("p b a k h r -> p (b a) k h r")
                                 [:, i, :, u * HPG:(u + 1) * HPG, :]).then_inc(s_vst, 1)

            def split(n, s):
                h, m, l = (msplit[:, k * JOBS // 2:(k + 1) * JOBS // 2] for k in range(3))
                pool.wait_ge(s_comb, n + 1)
                if type(n) is not int or n > 0:
                    pool.wait_ge(s_mm, turn_slot(n - 1)[0] + 1)
                pool.tensor_tensor(mneg[:, :], zero[:, :], mrow[:, s % 2, :], ALU.subtract).then_inc(s_chain, 1)
                pool.wait_ge(s_chain, CH * n + 1)
                pool.tensor_tensor(h, mneg[:, :], zero[:, :], ALU.add).then_inc(s_chain, 1)
                pool.wait_ge(s_chain, CH * n + 2)
                pool.tensor_tensor(mres[:, :], mneg[:, :], h, ALU.subtract).then_inc(s_chain, 1)
                pool.wait_ge(s_chain, CH * n + 3)
                pool.tensor_tensor(m, mres[:, :], zero[:, :], ALU.add).then_inc(s_chain, 1)
                pool.wait_ge(s_chain, CH * n + 4)
                pool.tensor_tensor(l, mres[:, :], m, ALU.subtract).then_inc(s_split, 1)

            pool.memset(zero[:, :], 0.0).then_inc(s_zero, 1)
            pool.wait_ge(s_zero, 1)
            split(0, 0)
            stage(0, 0)
            stage(0, 1)
            with pool.Fori(0, STEPS - 1) as i:
                for s in range(SUBS):
                    split(sub(i, s) + 1, s + 1)
                    if s % 2:
                        pool.wait_ge(s_pv, sub(i, s) + 1)
                        stage(i + 1, s // 2)
            for s in range(SUBS - 1):
                split(sub(STEPS - 1, s) + 1, s + 1)

        @block.tensor
        def _(pe):
            def max_job(i, s, j):
                i, s = i + s // SUBS, s % SUBS
                n = sub(i, s)
                slot, bank = job_slot(n, j)
                if type(n) is not int or slot >= RING:
                    pe.wait_ge(s_free, slot - RING + 1)
                if j == 0 and s % 2 == 0:
                    pe.wait_ge(s_stack[s // 2], UNIT_DMAS * 16 * (i + 1))
                h, qt, kh = j // 8, j // 2 % 4, j % 2
                pe.matmul(ps_m[bank][:, :], qst[s // 2][0:KROWS, s % 2, h, qt * P:(qt + 1) * P],
                          kst[s // 2][0:KROWS, h, kh * BLK:(kh + 1) * BLK], start=True, stop=True).then_inc(s_mm, 1)

            def max_turn(n, s):
                slot, bank = turn_slot(n)
                pe.wait_ge(s_split, n + 1)
                pe.wait_ge(s_free, slot - RING + 1)
                pe.transpose(ps_m[bank][:, 0:P // 2].bitcast(BF16), msplit[:, :], identb[:, :]).then_inc(s_mm, 1)

            def scores(n, s, kt, pair):
                if kt == 0 and pair == 0:
                    pe.wait_ge(s_rows, 16 * 3 * (n + 1))
                pe.wait_ge(s_exp[pair], KT * n + kt + 1)
                for k in range(2):
                    h = 2 * pair + k
                    mm = pe.matmul(ps_s[pair][:, k, :], kst[s // 2][:, h, kt * P:(kt + 1) * P],
                                   qst[s // 2][:, s % 2, h, :], start=True, stop=True)
                mm.then_inc(s_score[pair], 1)

            def values(i, s, kt):
                n = sub(i, s)
                for pair in range(2):
                    pe.wait_ge(s_exp[pair], KT * n + kt + 2)
                if kt == 0:
                    pe.wait_ge(s_oev, n + 1)
                    if s % 2 == 0:
                        pe.wait_ge(s_vst, 2 * i + s // 2 + 1)
                for h in range(HPG):
                    mm = pe.matmul(ps_o[32 * h:32 * h + 32, :], vst[s // 2][:, kt, h, :], prob[kt % 4][:, h, :],
                                   start=(kt == 0), stop=(kt == KT - 1))
                if kt == KT - 1:
                    mm.then_inc(s_pv, 1)

            def slot(i, r, last):
                i, r = i + r // SLOTS, r % SLOTS
                s, kt = r // KT, r % KT

                def job(q):
                    j = JPS * (kt + SKEW) + q
                    ahead = s + 1 + j // JOBS
                    if j % JOBS == TJ and j >= JOBS and not (last and s + 1 >= SUBS):
                        max_turn(sub(i, s) + 1, (s + 1) % SUBS)
                    if not (last and ahead >= SUBS):
                        max_job(i, ahead, j % JOBS)

                scores(sub(i, s), s, kt, 0)
                job(0)
                scores(sub(i, s), s, kt, 1)
                job(1)
                job(2)
                if type(i) is not int or i > 0 or r > 0:
                    p = r - 1
                    values(i if p >= 0 else i - 1, p % SLOTS // KT, p % KT)
                job(3)

            pe.wait_ge(s_ones, 3)
            for j in range(JOBS):
                max_job(0, 0, j)
            for j in range(TJ):
                max_job(0, 1, j)
            max_turn(0, 0)
            for j in range(TJ, JPS * SKEW):
                max_job(0, 1, j)
            slot(0, 0, False)
            with pe.Fori(0, STEPS - 1) as i:
                for r in range(1, SLOTS + 1):
                    slot(i, r, False)
            for r in range(1, SLOTS):
                slot(STEPS - 1, r, True)
            values(STEPS - 1, SUBS - 1, KT - 1)

        @block.scalar
        def _(act):
            def evacuate(i, s):
                n = sub(i, s)
                act.wait_ge(s_pv, n + 1)
                act.activation(oall[:, i, s // 2, s % 2, :], ps_o[:, :], ACT.Copy).then_inc(s_oev, 1)

            def slot(i, r):
                i, r = i + r // SLOTS, r % SLOTS
                s, kt = r // KT, r % KT
                for pair in range(2):
                    act.wait_ge(s_score[pair], KT * sub(i, s) + kt + 1)
                    act.activation(prob[kt % 4][:, 2 * pair:2 * pair + 2, :], ps_s[pair][:, :, :],
                                   ACT.Exp).then_inc(s_exp[pair], 1)

            for sem in (*s_exp, s_oev):
                act.sem_inc(sem, 1)
            slot(0, 0)
            with act.Fori(0, STEPS - 1) as i:
                for r in range(1, SLOTS + 1):
                    slot(i, r)
                    if r % KT == 0:
                        evacuate(i, r // KT - 1)
            for r in range(1, SLOTS):
                slot(STEPS - 1, r)
                if r % KT == 0:
                    evacuate(STEPS - 1, r // KT - 1)
            evacuate(STEPS - 1, SUBS - 1)

        @block.vector
        def _(dve):
            def reduce(n, j):
                slot, bank = job_slot(n, j)
                dve.wait_ge(s_mm, slot + 1)
                dve.tensor_reduce(mx[:, j:j + 1], ps_m[bank][:, :], AX_X, ALU.max).then_inc(s_free, 1)

            def combine(n, s):
                dve.wait_ge(s_free, job_slot(n, JOBS - 1)[0] + 1)
                if type(n) is not int or n > 1:
                    dve.wait_ge(s_split, n - 1)
                dve.tensor_reduce(mrow[:, s % 2, :], mx[:, :].rearrange("p (n k) -> p n k", k=2), AX_X,
                                  ALU.max).then_inc(s_comb, 1)
                dve.wait_ge(s_comb, n + 1)

            def turned(n, s):
                slot, bank = turn_slot(n)
                dve.wait_ge(s_mm, slot + 1)
                dve.tensor_copy(mT[s % 2][:, :], ps_m[bank][:, 0:P // 2].bitcast(BF16)).then_inc(s_free, 1)

            def step(i, last):
                for s in range(SUBS):
                    n = sub(i, s)
                    if last and s + 1 >= SUBS:
                        continue
                    for j in range(JPS * SKEW, JOBS):
                        reduce(n + 1, j)
                    combine(n + 1, s + 1)
                    for j in range(JPS * SKEW):
                        if j == TJ:
                            turned(n + 1, (s + 1) % SUBS)
                        if not (last and s + 2 >= SUBS):
                            reduce(n + 2, j)

            dve.memset(msplit[:, :], 0.0).then_inc(s_ones, 1)
            for u in range(2):
                dve.memset(kst[u][KROWS:KEXP, :, :], 1.0).then_inc(s_ones, 1)
            for j in range(JOBS):
                reduce(0, j)
            combine(0, 0)
            for j in range(JPS * SKEW):
                if j == TJ:
                    turned(0, 0)
                reduce(1, j)
            with dve.Fori(0, STEPS - 1) as i:
                step(i, False)
            step(STEPS - 1, True)


def project_out(nc, x, oall, wo, ident):
    with ExitStack() as es:
        c = Ctx(nc, es, "po")
        rec = c.sb("rec", [P, 2, HA, 1])
        at = c.sb("at", [P, 2, D])
        atT = c.sb("atT", [P, 2, D])
        p_h = [c.ps(f"heads{n}", [P, BLK]) for n in range(2)]
        p_t = [c.ps(f"turned{n}", [P, BLK]) for n in range(2)]
        p_y = [c.ps(f"y{n}", [P, BLK]) for n in range(2)]
        s_h, s_rec, s_at, s_t, s_tc, s_y, s_x = (c.sem(n) for n in ("heads", "rec", "at", "t", "tc", "y", "x"))
        block = es.enter_context(nc.Block())

        @block.tensor
        def _(pe):
            def heads(t):
                b, qh, j = t // KT, t % KT // TPB, t % TPB
                if t >= 2:
                    pe.wait_ge(s_at, t - 1)
                for g in range(4):
                    mm = pe.transpose(p_h[t % 2][:, g * P:(g + 1) * P],
                                      oall[:, DH * b + g // 2, g % 2, qh, j * P:(j + 1) * P], ident[:, :])
                mm.then_inc(s_h, 1)

            def project(t):
                pe.wait_ge(s_tc, t + 1)
                if t >= 2:
                    pe.wait_ge(s_x, t - 1)
                for h in range(DH):
                    mm = pe.matmul(p_y[t % 2][:, 0:D], atT[:, t % 2, h * P:(h + 1) * P], wo[:, h, :],
                                   start=(h == 0), stop=(h == DH - 1))
                mm.then_inc(s_y, 1)

            heads(0)
            for t in range(NT):
                if t + 1 < NT:
                    heads(t + 1)
                pe.wait_ge(s_at, t + 1)
                if t >= 2:
                    pe.wait_ge(s_tc, t - 1)
                for h in range(DH):
                    mm = pe.transpose(p_t[t % 2][:, h * P:(h + 1) * P], at[:, t % 2, h * P:(h + 1) * P], ident[:, :])
                mm.then_inc(s_t, 1)
                if t >= 1:
                    project(t - 1)
            project(NT - 1)

        @block.scalar
        def _(act):
            for t in range(NT):
                act.wait_ge(s_t, t + 1)
                if t >= 2:
                    act.wait_ge(s_y, t - 1)
                act.activation(atT[:, t % 2, :], p_t[t % 2][:, 0:D], ACT.Copy).then_inc(s_tc, 1)

        @block.vector
        def _(dve):
            def add(t):
                dve.wait_ge(s_y, t + 1)
                dve.tensor_tensor(x[:, t, :], p_y[t % 2][:, 0:D], x[:, t, :], ALU.add).then_inc(s_x, 1)

            for t in range(NT):
                heads = p_h[t % 2][:, :].rearrange("p (h r) -> p h r", r=2 * HDA)
                dve.wait_ge(s_h, t + 1)
                dve.reciprocal(rec[:, t % 2, :, :], heads[:, :, HDA:HDA + 1]).then_inc(s_rec, 1)
                dve.wait_ge(s_rec, t + 1)
                if t >= 2:
                    dve.wait_ge(s_t, t - 1)
                dve.tensor_tensor(at[:, t % 2, :].rearrange("p (h r) -> p h r", r=HDA), heads[:, :, 0:HDA],
                                  rec[:, t % 2, :, :].broadcast_to([P, HA, HDA]), ALU.mult).then_inc(s_at, 1)
                if t >= 2:
                    add(t - 2)
            add(NT - 2)
            add(NT - 1)


def route(nc, io, tag, xt, comb, rbias, iota):
    with ExitStack() as es:
        c = Ctx(nc, es, tag)
        rw = c.sb("rw", [P, DH, NE])
        rhi, rlo = c.sb("rhi", [P, DH, NE], F32R), c.sb("rlo", [P, DH, NE], F32R)
        lg = c.sb("lg", [P, NT, NE])
        lb = c.sb("lb", [P, NT, NE])
        m8 = c.sb("m8", [P, NT, 8])
        i8 = c.sb("i8", [P, NT, 8], U32)
        idx = c.sb("idx", [P, NT, 2])
        oh = c.sb("oh", [P, 2, NT, NE])
        sel = c.sb("sel", [P, NT, NE])
        mraw = c.sb("mraw", [P, NT, 1])
        sh = c.sb("sh", [P, NT, NE])
        ex = c.sb("ex", [P, NT, NE])
        w = c.sb("w", [P, NT, NE])
        tot = c.sb("tot", [P, NT, 1])
        rt = c.sb("rt", [P, NT, 1])
        pl = c.ps("logits", [P, BLK])
        s_w, s_hi, s_lo, s_l, s_lg, s_e, s_c = (c.sem(n) for n in ("w", "hi", "lo", "logits", "lg", "exp", "chain"))
        block = es.enter_context(nc.Block())
        shape = [P, NT, NE]

        @block.sync
        def _(sp):
            sp.dma_start(rw[:, :, :], io["RwT"].rearrange("(h p) e -> p h e", p=P)).then_inc(s_w, 16)

        @block.tensor
        def _(pe):
            pe.wait_ge(s_lo, 1)
            for t in range(NT):
                for h in range(DH):
                    mm = products(pe, pl[:, t * NE:(t + 1) * NE], [a[:, h, t * P:(t + 1) * P] for a in xt],
                                  [rhi[:, h, :], rlo[:, h, :]], h == 0, h == DH - 1)
            mm.then_inc(s_l, 1)

        @block.scalar
        def _(act):
            act.wait_ge(s_w, 16)
            act.activation(rhi[:, :, :], rw[:, :, :], ACT.Copy).then_inc(s_hi, 1)
            act.wait_ge(s_l, 1)
            act.activation(lg[:, :, :], pl[:, 0:NT * NE].rearrange("p (t e) -> p t e", e=NE), ACT.Copy).then_inc(s_lg, 1)
            act.wait_ge(s_c, 2)
            act.activation(ex[:, :, :], sh[:, :, :], ACT.Exp).then_inc(s_e, 1)

        @block.vector
        def _(dve):
            done = [0]

            def link(ins):
                done[0] += 1
                ins.then_inc(s_c, 1)
                dve.wait_ge(s_c, done[0])

            dve.wait_ge(s_hi, 1)
            dve.tensor_tensor(rlo[:, :, :], rw[:, :, :], rhi[:, :, :].bitcast(F32), ALU.subtract).then_inc(s_lo, 1)
            dve.wait_ge(s_lg, 1)
            link(dve.tensor_reduce(mraw[:, :, :], lg[:, :, :], AX_X, ALU.max))
            link(dve.tensor_tensor(sh[:, :, :], lg[:, :, :], mraw[:, :, :].broadcast_to(shape), ALU.subtract))
            link(dve.tensor_tensor(lb[:, :, :], lg[:, :, :], rbias[:, :].rearrange("p (o e) -> p o e", o=1)
                                   .broadcast_to(shape), ALU.add))
            for t in range(NT):
                dve.max(m8[:, t, :], lb[:, t, :]).then_inc(s_c, 1)
                done[0] += 1
            for t in range(NT):
                dve.wait_ge(s_c, done[0])
                dve.max_index(i8[:, t, :], m8[:, t, :], lb[:, t, :]).then_inc(s_c, 1)
                done[0] += 1
            dve.wait_ge(s_c, done[0])
            link(dve.tensor_copy(idx[:, :, :], i8[:, :, 0:2]))
            for k in range(2):
                link(dve.tensor_tensor(oh[:, k, :, :], iota[:, :].rearrange("p (o e) -> p o e", o=1).broadcast_to(shape),
                                       idx[:, :, k:k + 1].broadcast_to(shape), ALU.is_equal))
            link(dve.tensor_tensor(sel[:, :, :], oh[:, 0, :, :], oh[:, 1, :, :], ALU.add))
            dve.wait_ge(s_e, 1)
            link(dve.tensor_tensor(w[:, :, :], ex[:, :, :], sel[:, :, :], ALU.mult))
            link(dve.tensor_reduce(tot[:, :, :], w[:, :, :], AX_X, ALU.add))
            link(dve.reciprocal(rt[:, :, :], tot[:, :, :]))
            link(dve.memset(comb[:, NE:NU, :], 1.0))
            link(dve.tensor_tensor(comb[:, 0:NE, :].rearrange("p e t -> p t e"), w[:, :, :],
                                   rt[:, :, :].broadcast_to(shape), ALU.mult))


def experts(nc, io, tag, x, xt, comb):
    WC = DH * 2 * ED
    WN = WC + D
    with ExitStack() as es:
        c = Ctx(nc, es, tag)
        raw = [c.sb(f"raw{u}", [P, WN]) for u in range(2)]
        whi = [c.sb(f"whi{u}", [P, WN], F32R) for u in range(2)]
        wlo = [c.sb(f"wlo{u}", [P, WN], F32R) for u in range(2)]
        su = c.sb("su", [P, 2, BLK])
        hf = c.sb("hf", [P, 2, BLK])
        hhi = c.sb("hhi", [P, 4, BLK], F32R)
        hlo = c.sb("hlo", [P, 4, BLK], F32R)
        pu = [c.ps(f"up{n}", [P, BLK]) for n in range(2)]
        pg = [c.ps(f"gate{n}", [P, BLK]) for n in range(2)]
        pd = [c.ps(f"down{n}", [P, TPB, D]) for n in range(2)]
        s_w = [c.sem(f"weights{u}") for u in range(2)]
        s_whi, s_wlo = c.sem("weights_hi"), c.sem("weights_lo")
        s_ug, s_su, s_hf, s_hh, s_hl = (c.sem(n) for n in ("up_gate", "silu", "hidden", "hidden_hi", "hidden_lo"))
        s_d, s_x = c.sem("down"), c.sem("x_added")
        block = es.enter_context(nc.Block())
        STEPS = NU // 2

        @block.sync
        def _(sp):
            def load(i, u):
                sp.dma_start(raw[u][:, 0:WC].rearrange("p (h n) -> p h n", h=DH),
                             io["Wup"][i, u].rearrange("(h p) n -> p h n", p=P)).then_inc(s_w[u], 16)
                sp.dma_start(raw[u][:, WC:WN], io["Wdn"][i, u]).then_inc(s_w[u], 16)

            load(0, 0)
            load(0, 1)
            with sp.Fori(0, STEPS - 1) as i:
                for u in range(2):
                    sp.wait_ge(s_wlo, 2 * i + u + 1)
                    load(i + 1, u)

        @block.tensor
        def _(pe):
            def up(i, u, tb, m):
                k = NB * m + tb
                if tb == 0:
                    pe.wait_ge(s_whi, m + 1)
                    pe.wait_ge(s_wlo, m + 1)
                if type(m) is not int or k >= 2:
                    pe.wait_ge(s_hf, k - 1)
                w = (whi[u], wlo[u])
                for p_, off in ((pu, 0), (pg, ED)):
                    for h in range(DH):
                        mm = products(pe, p_[tb % 2][:, :], [a[:, h * 2 * ED + off:h * 2 * ED + off + ED] for a in w],
                                      [a[:, h, tb * BLK:(tb + 1) * BLK] for a in xt], h == 0, h == DH - 1)
                mm.then_inc(s_ug, 1)

            def down(i, u, tb):
                k = NB * (2 * i + u) + tb
                pe.wait_ge(s_hh, k + 1)
                pe.wait_ge(s_hl, k + 1)
                if type(k) is not int or k >= 2:
                    pe.wait_ge(s_x, k - 1)
                n = (NB * u + tb) % 4
                for j in range(TPB):
                    mm = products(pe, pd[tb % 2][:, j, :], [a[:, n, j * P:(j + 1) * P] for a in (hhi, hlo)],
                                  [a[:, WC:WN] for a in (whi[u], wlo[u])], True, True)
                mm.then_inc(s_d, 1)

            def step(i, last):
                for u in range(2):
                    for tb in range(NB):
                        down(i, u, tb)
                        if tb < 2:
                            up(i, u, tb + 2, 2 * i + u)
                        elif u == 0:
                            up(i, 1, tb - 2, 2 * i + 1)
                        elif not last:
                            up(i + 1, 0, tb - 2, 2 * i + 2)

            up(0, 0, 0, 0)
            up(0, 0, 1, 0)
            step(0, False)
            with pe.Fori(1, STEPS - 1) as i:
                step(i, False)
            step(STEPS - 1, True)

        @block.scalar
        def _(act):
            def weights(i, u):
                act.wait_ge(s_w[u], 32 * (i + 1))
                act.activation(whi[u][:, :], raw[u][:, :], ACT.Copy).then_inc(s_whi, 1)

            def step(i, last):
                for u in range(2):
                    for tb in range(NB):
                        k = NB * (2 * i + u) + tb
                        act.wait_ge(s_ug, k + 1)
                        act.activation(su[:, tb % 2, :], pu[tb % 2][:, :], ACT.Silu).then_inc(s_su, 1)
                        if tb == 1 and not (last and u == 1):
                            weights(i + u, 1 - u)
                        act.wait_ge(s_hf, k + 1)
                        act.activation(hhi[:, (NB * u + tb) % 4, :], hf[:, tb % 2, :], ACT.Copy).then_inc(s_hh, 1)

            weights(0, 0)
            with act.Fori(0, STEPS - 1) as i:
                step(i, False)
            step(STEPS - 1, True)

        @block.gpsimd
        def _(pool):
            def weights(m, u):
                pool.wait_ge(s_whi, m + 1)
                pool.tensor_tensor(wlo[u][:, :], raw[u][:, :], whi[u][:, :].bitcast(F32), ALU.subtract).then_inc(s_wlo, 1)

            def step(i, last):
                for u in range(2):
                    for tb in range(NB):
                        k = NB * (2 * i + u) + tb
                        if tb == 1 and not (last and u == 1):
                            weights(2 * i + u + 1, 1 - u)
                        pool.wait_ge(s_hh, k + 1)
                        n = (NB * u + tb) % 4
                        pool.tensor_tensor(hlo[:, n, :], hf[:, tb % 2, :], hhi[:, n, :].bitcast(F32),
                                           ALU.subtract).then_inc(s_hl, 1)

            weights(0, 0)
            with pool.Fori(0, STEPS - 1) as i:
                step(i, False)
            step(STEPS - 1, True)

        @block.vector
        def _(dve):
            def hidden(k, tb, first=False):
                dve.wait_ge(s_su, k + 1)
                if not first:
                    dve.wait_ge(s_hl, k - 1)
                dve.tensor_tensor(hf[:, tb % 2, :], su[:, tb % 2, :], pg[tb % 2][:, :], ALU.mult).then_inc(s_hf, 1)

            def add(i, u, tb):
                dve.wait_ge(s_d, NB * (2 * i + u) + tb + 1)
                for j in range(TPB):
                    t = TPB * tb + j
                    ins = dve.scalar_tensor_tensor(out=x[:, t, :], in0=pd[tb % 2][:, j, :],
                                                   scalar=comb[:, 2 * i + u, t:t + 1], in1=x[:, t, :],
                                                   op0=ALU.mult, op1=ALU.add)
                ins.then_inc(s_x, 1)

            def step(i, last):
                for u in range(2):
                    for tb in range(NB):
                        add(i, u, tb)
                        if not (last and u == 1 and tb >= 2):
                            hidden(NB * (2 * i + u) + tb + 2, tb)

            hidden(0, 0, True)
            hidden(1, 1, True)
            with dve.Fori(0, STEPS - 1) as i:
                step(i, False)
            step(STEPS - 1, True)


def retain(nc, io, x, xt, ident):
    G = 2
    H4 = HB // G
    W3 = QK + 2 * DVT
    with ExitStack() as es:
        c = Ctx(nc, es, "rt")
        wst = c.sb("wst", [P, DH, W3])
        whi = c.sb("whi", [P, DH, W3], F32R)
        wlo = c.sb("wlo", [P, DH, W3], F32R)
        wo = c.sb("wo", [P, DVT // P, D])
        xs = [[c.sb(f"xs{w}{k}", [P, DH, P], F32R) for k in range(2)] for w in range(2)]
        cos = c.sb("cos", [P, NT, DK])
        sin = c.sb("sin", [P, NT, DK])
        dec = c.sb("dec", [P, 2 * HB, 1])
        mask = c.sb("mask", [P, 1, P])
        bd = c.sb("bd", [P, 1, H4, 1])
        gdec = c.sb("gdec", [P, G, NT])
        gw = c.sb("gw", [P, 1, DV])
        nhalf = c.sb("nhalf", [P, HB, 1])
        ra, rb, rr = (c.sb(n, [P, 2 * HB, DK]) for n in ("ra", "rb", "rr"))
        qk = c.sb("qk", [P, 2, QK])
        v = c.sb("v", [P, 2, DVT])
        sg = c.sb("sg", [P, HB, DV])
        gate = c.sb("gate", [P, 2, HB, DV])
        qkT = c.sb("qkT", [P, 2 * G, P])
        qbd = c.sb("qbd", [P, G, H4, P])
        sc = c.sb("sc", [P, G, H4, P])
        st, sm, sa = (c.sb(n, [P, G, H4, DV]) for n in ("st", "sm", "sa"))
        sq, on = (c.sb(n, [P, HB, DV]) for n in ("sq", "on"))
        ms, mv, rs = (c.sb(n, [P, HB, 1]) for n in ("ms", "mv", "rs"))
        og = c.sb("og", [P, DVT])
        oT = c.sb("oT", [P, DVT // P, P])
        p_qk, p_v, p_g, p_t, p_o, p_y = (c.ps("p_" + n, [P, BLK]) for n in ("qk", "v", "g", "t", "o", "y"))
        p_s = [c.ps(f"p_s{g}", [P, BLK]) for g in range(G)]
        s_w, s_whi, s_wlo, s_const, s_zero, s_half = (c.sem(n) for n in ("w", "whi", "wlo", "const", "zero", "half"))
        s_xs = [c.sem(f"x_staged{w}") for w in range(2)]
        s_qk, s_v, s_g, s_o, s_st, s_y = (c.sem("mm_" + n) for n in ("qk", "v", "g", "o", "state", "y"))
        s_s = [c.sem(f"mm_scores{g}") for g in range(G)]
        s_tr, s_ot = c.sem("qk_transposed"), c.sem("o_transposed")
        s_rope, s_sum, s_dk, s_gate = (c.sem(n) for n in ("rope_products", "rope_sum", "qk_decayed", "gate"))
        s_vc, s_sg, s_tc, s_bd, s_otc = (c.sem(n) for n in ("v_copied", "silu", "qkT_copied", "q_block_diag", "oT_copied"))
        s_sc = [c.sem(f"scores_masked{g}") for g in range(G)]
        s_sm, s_sa, s_state = c.sem("update_masked"), c.sem("state_sum"), c.sem("state_ready")
        s_sq, s_ms, s_mv, s_rs, s_on, s_og, s_x = (c.sem(n) for n in ("sq", "ms", "mv", "rs", "on", "og", "x"))
        CONSTS = 8
        block = es.enter_context(nc.Block())

        def wait(eng, sem, value):
            if type(value) is not int or value > 0:
                eng.wait_ge(sem, value)

        def slots(eng, slot):
            slot(-1, 1, False, False, True, 1)
            slot(0, 0, False, True, True, 1)
            with eng.Fori(0, NT // 2 - 1) as i:
                slot(2 * i + 1, 1, True, True, True, i + 2)
                slot(2 * i + 2, 0, True, True, True, i + 2)
            slot(NT - 1, 1, True, True, False, None)
            slot(NT, 0, True, False, False, None)

        @block.sync
        def _(sp):
            def stage(t, w):
                for k in range(2):
                    sp.dma_start(xs[w][k][:, :, :].bitcast(F32), xt[k][:, :, :].bitcast(F32).rearrange("p h (t n) -> p t h n", n=P)[:, t, :, :]
                                 ).then_inc(s_xs[w], 16)

            sp.dma_start(wst[:, :, :], io["Wret"].rearrange("(h p) n -> p h n", p=P)).then_inc(s_w, 16)
            stage(0, 0)
            stage(1, 1)
            for dst, src in ((wo[:, :, :], io["WoB"].rearrange("(c p) n -> p c n", p=P)),
                             (cos[:, :, :], io["cos"]), (sin[:, :, :], io["sin"]),
                             (dec[:, :, 0], io["dec"]), (mask[:, 0, :], io["mask"]), (bd[:, 0, :, 0], io["bd"]),
                             (gdec[:, :, :], io["gdec"]),
                             (gw[:, 0, :], io["gnw"].rearrange("(o n) -> o n", o=1).broadcast_to([P, DV]))):
                sp.dma_start(dst, src).then_inc(s_const, 16)
            with sp.Fori(0, NT // 2 - 1) as i:
                for w in range(2):
                    sp.wait_ge(s_g, 2 * i + w + 1)
                    stage(2 * i + w + 2, w)

        @block.tensor
        def _(pe):
            def project(t, i, w):
                pe.wait_ge(s_xs[w], 32 * i)
                for out, col, width, sem, freed in ((p_qk, 0, QK, s_qk, s_rope), (p_v, QK, DVT, s_v, s_vc),
                                                    (p_g, QK + DVT, DVT, s_g, s_sg)):
                    wait(pe, freed, t)
                    for h in range(DH):
                        mm = products(pe, out[:, :], [a[:, h, :] for a in xs[w]],
                                      [a[:, h, col:col + width] for a in (whi, wlo)], h == 0, h == DH - 1)
                    mm.then_inc(sem, 1)

            def slot(t, w, prev, cur, nxt, staged):
                if cur:
                    pe.wait_ge(s_dk, t + 1)
                    wait(pe, s_sm, t)
                    for g in range(2 * G):
                        mm = pe.transpose(p_t[:, g * P:(g + 1) * P], qk[:, w, g * P:(g + 1) * P], ident[:, :])
                    mm.then_inc(s_tr, 1)
                if nxt:
                    project(t + 1, staged, 1 - w)
                if prev:
                    pe.wait_ge(s_og, t)
                    wait(pe, s_x, t)
                    for g in range(DVT // P):
                        mm = pe.transpose(p_y[:, g * P:(g + 1) * P], og[:, g * P:(g + 1) * P], ident[:, :])
                    mm.then_inc(s_ot, 1)
                if cur:
                    pe.wait_ge(s_tc, t + 1)
                    pe.wait_ge(s_bd, t + 1)
                    for g in range(G):
                        wait(pe, s_sc[g], t)
                        pe.matmul(p_s[g][:, :], qkT[:, G + g, :], qbd[:, g, :, :], start=True, stop=True).then_inc(s_s[g], 1)
                if prev:
                    pe.wait_ge(s_otc, t)
                    for g in range(DVT // P):
                        mm = pe.matmul(p_y[:, 0:D], oT[:, g, :], wo[:, g, :], start=(g == 0), stop=(g == DVT // P - 1))
                    mm.then_inc(s_y, 1)
                if cur:
                    pe.wait_ge(s_vc, t + 1)
                    for g in range(G):
                        mm = pe.matmul(p_t[:, g * H4 * DV:(g + 1) * H4 * DV], qk[:, w, (G + g) * P:(G + g + 1) * P],
                                       v[:, w, g * H4 * DV:(g + 1) * H4 * DV], start=True, stop=True)
                    mm.then_inc(s_st, 1)
                    pe.wait_ge(s_state, t + 1)
                    pe.wait_ge(s_on, t + 1)
                    for g in range(G):
                        pe.matmul(p_o[:, g * H4 * DV:(g + 1) * H4 * DV], qkT[:, g, :], st[:, g, :, :],
                                  start=(g == 0), stop=False, skip_group_check=True)
                    for g in range(G):
                        pe.wait_ge(s_sc[g], t + 1)
                        for h in range(H4):
                            n = g * H4 + h
                            mm = pe.matmul(p_o[:, n * DV:(n + 1) * DV], sc[:, g, h, :], v[:, w, n * DV:(n + 1) * DV],
                                           start=False, stop=(n == HB - 1), skip_group_check=True)
                    mm.then_inc(s_o, 1)

            pe.wait_ge(s_whi, 1)
            pe.wait_ge(s_wlo, 1)
            pe.sem_inc(s_ot, 1)
            slots(pe, slot)

        @block.scalar
        def _(act):
            def slot(t, w, prev, cur, nxt, staged):
                if prev:
                    act.wait_ge(s_o, t)
                    wait(act, s_ms, t)
                    act.activation(sq[:, :, :], p_o[:, :].rearrange("p (h v) -> p h v", v=DV), ACT.Square).then_inc(s_sq, 1)
                if cur:
                    act.wait_ge(s_tr, t + 1)
                    act.activation(qkT[:, :, :], p_t[:, :].rearrange("p (g n) -> p g n", n=P), ACT.Copy).then_inc(s_tc, 1)
                    for h in range(H4):
                        rows = slice(h * DK, (h + 1) * DK)
                        ins = act.activation(qbd[rows, :, h, :], p_t[rows, 0:G * P].rearrange("p (g n) -> p g n", n=P), ACT.Copy)
                    ins.then_inc(s_bd, 1)
                if nxt:
                    act.wait_ge(s_v, t + 2)
                    act.activation(v[:, 1 - w, :], p_v[:, :], ACT.Copy).then_inc(s_vc, 1)
                    act.wait_ge(s_g, t + 2)
                    wait(act, s_gate, t + 1)
                    act.activation(sg[:, :, :], p_g[:, :].rearrange("p (h v) -> p h v", v=DV), ACT.Silu).then_inc(s_sg, 1)
                if prev:
                    act.wait_ge(s_ot, t + 1)
                    act.activation(oT[:, :, :], p_y[:, :].rearrange("p (g n) -> p g n", n=P), ACT.Copy).then_inc(s_otc, 1)

            act.wait_ge(s_w, 16)
            act.activation(whi[:, :, :], wst[:, :, :], ACT.Copy).then_inc(s_whi, 1)
            act.wait_ge(s_zero, 1)
            slots(act, slot)

        @block.gpsimd
        def _(pool):
            def slot(t, w, prev, cur, nxt, staged):
                if prev:
                    pool.wait_ge(s_mv, t)
                    wait(pool, s_on, t)
                    pool.tensor_tensor(rs[:, :, :], mv[:, :, :], nhalf[:, :, :], ALU.pow).then_inc(s_rs, 1)
                if nxt:
                    pool.wait_ge(s_rope, t + 2)
                    pool.tensor_tensor(rr[:, :, :], ra[:, :, :], rb[:, :, :], ALU.add).then_inc(s_sum, 1)
                    pool.wait_ge(s_sum, t + 2)
                    wait(pool, s_st, t)
                    pool.tensor_tensor(qk[:, 1 - w, :].rearrange("p (h n) -> p h n", n=DK), rr[:, :, :],
                                       dec[:, :, :].broadcast_to([P, 2 * HB, DK]), ALU.mult).then_inc(s_dk, 1)
                    pool.wait_ge(s_sg, t + 2)
                    wait(pool, s_og, t)
                    pool.tensor_tensor(gate[:, 1 - w, :, :], sg[:, :, :], gw[:, :, :].broadcast_to([P, HB, DV]),
                                       ALU.mult).then_inc(s_gate, 1)

            pool.wait_ge(s_const, 16 * CONSTS)
            pool.memset(nhalf[:, :, :], -0.5).then_inc(s_half, 1)
            pool.wait_ge(s_half, 1)
            pool.sem_inc(s_rs, 1)
            slots(pool, slot)

        @block.vector
        def _(dve):
            def slot(t, w, prev, cur, nxt, staged):
                if prev:
                    dve.wait_ge(s_sq, t)
                    dve.tensor_reduce(ms[:, :, :], sq[:, :, :], AX_X, ALU.add).then_inc(s_ms, 1)
                    dve.wait_ge(s_ms, t + 1)
                    wait(dve, s_rs, t)
                    dve.tensor_scalar(mv[:, :, :], ms[:, :, :], 1.0 / DV, EPS, ALU.mult, ALU.add).then_inc(s_mv, 1)
                    dve.wait_ge(s_rs, t + 1)
                    dve.tensor_tensor(on[:, :, :], p_o[:, :].rearrange("p (h v) -> p h v", v=DV),
                                      rs[:, :, :].broadcast_to([P, HB, DV]), ALU.mult).then_inc(s_on, 1)
                    dve.wait_ge(s_on, t + 1)
                    dve.wait_ge(s_gate, t)
                    wait(dve, s_ot, t)
                    dve.tensor_tensor(og[:, :].rearrange("p (h v) -> p h v", v=DV), on[:, :, :], gate[:, 1 - w, :, :],
                                      ALU.mult).then_inc(s_og, 1)
                if nxt:
                    q = p_qk[:, :].rearrange("p (h n) -> p h n", n=DK)
                    dve.wait_ge(s_qk, t + 2)
                    wait(dve, s_sum, t + 1)
                    dve.tensor_tensor(ra[:, :, :], q, cos[:, bass.ds(t + 1, 1), :].broadcast_to([P, 2 * HB, DK]), ALU.mult)
                    for a in range(2):
                        lo, hi = a * DK // 2, (a + 1) * DK // 2
                        ins = dve.tensor_tensor(rb[:, :, lo:hi], q[:, :, DK // 2 - lo:DK - lo],
                                                sin[:, bass.ds(t + 1, 1), lo:hi].broadcast_to([P, 2 * HB, DK // 2]), ALU.mult)
                    ins.then_inc(s_rope, 1)
                if cur:
                    wait(dve, s_o, t)
                    for g in range(G):
                        dve.wait_ge(s_s[g], t + 1)
                        dve.tensor_tensor(sc[:, g, :, :], p_s[g][:, :].rearrange("p (h n) -> p h n", n=P),
                                          mask[:, :, :].broadcast_to([P, H4, P]), ALU.mult).then_inc(s_sc[g], 1)
                if prev:
                    dve.wait_ge(s_y, t)
                    xv = x[:, t - 1, :]
                    dve.tensor_tensor(xv, p_y[:, 0:D], xv, ALU.add).then_inc(s_x, 1)
                if cur:
                    dve.wait_ge(s_st, t + 1)
                    dve.tensor_tensor(sm[:, :, :, :], p_t[:, :].rearrange("p (g h v) -> p g h v", g=G, h=H4),
                                      bd[:, :, :, :].broadcast_to([P, G, H4, DV]), ALU.mult).then_inc(s_sm, 1)
                    dve.wait_ge(s_sm, t + 1)
                    dve.wait_ge(s_state, t + 1)
                    dve.tensor_tensor(sa[:, :, :, :], st[:, :, :, :], sm[:, :, :, :], ALU.add).then_inc(s_sa, 1)
                    dve.wait_ge(s_sa, t + 1)
                    dve.wait_ge(s_o, t + 1)
                    for g in range(G):
                        ins = dve.tensor_scalar(st[:, g, :, :], sa[:, g, :, :], gdec[:, g, bass.ds(t, 1)], None, ALU.mult)
                    ins.then_inc(s_state, 1)

            dve.memset(qbd[:, :, :, :], 0.0).then_inc(s_zero, 1)
            dve.memset(st[:, :, :, :], 0.0).then_inc(s_state, 1)
            dve.wait_ge(s_whi, 1)
            dve.tensor_tensor(wlo[:, :, :], wst[:, :, :], whi[:, :, :].bitcast(F32), ALU.subtract).then_inc(s_wlo, 1)
            dve.wait_ge(s_const, 16 * CONSTS)
            for sem in (s_x, s_ms, s_on):
                dve.sem_inc(sem, 1)
            slots(dve, slot)


def build(nc, io, out, stages=4):
    with ExitStack() as es:
        c = Ctx(nc, es, "g")
        x = c.sb("x", [P, NT, D])
        xt = [c.sb(n, [P, DH, N], F32R) for n in ("xt_hi", "xt_lo")]
        ident = c.sb("ident", [P, P])
        identb = c.sb("identb", [P, P], BF16)
        rbias = c.sb("rbias", [P, NE])
        iota = c.sb("iota", [P, NE])
        comb = c.sb("comb", [P, NU, NT])
        s_in, s_id, s_out = c.sem("inputs"), c.sem("ident"), c.sem("stored")

        def bcast(ap, n):
            return ap.rearrange("(o n) -> o n", o=1).broadcast_to([P, n])

        with nc.Block() as block:
            @block.sync
            def _(sp):
                xv = io["x"].rearrange("b (t p) d -> p (b t) d", p=P)
                for b in range(NB):
                    sp.dma_start(x[:, b * TPB:(b + 1) * TPB, :], xv[:, b * TPB:(b + 1) * TPB, :]).then_inc(s_in, 16)
                sp.dma_start(ident[:, :], io["ident"]).then_inc(s_in, 16)
                sp.dma_start(rbias[:, :], bcast(io["rbias"], NE)).then_inc(s_in, 16)
                sp.dma_start(iota[:, :], bcast(io["iota"], NE)).then_inc(s_in, 16)
                sp.wait_ge(s_in, 16 * (NB + 3))

            @block.vector
            def _(dve):
                dve.wait_ge(s_in, 16 * (NB + 3))
                dve.tensor_copy(identb[:, :], ident[:, :]).then_inc(s_id, 1)

        normalise(nc, "n1", x, ident, xt)
        with ExitStack() as es2:
            a = Ctx(nc, es2, "a")
            wo = a.sb("wo", [P, DH, D])
            oall = a.sb("oall", [P, B * DH, 2, 2, BLK])
            vb, bo = a.sb("vb", [P, D]), a.sb("bo", [P, D])
            vaug = a.sb("vaug", [P, B, DH, KT, HA // DH, 2 * HDA])
            scratch = nc.dram_tensor("qk_parts", [2, 3, B * DH, 2, HPG, HDA, L], BF16, kind="Internal").ap()
            s_b, s_one = a.sem("biases"), a.sem("ones")
            with nc.Block() as block:
                @block.sync
                def _(sp):
                    sp.dma_start(vb[:, :], bcast(io["bias"][2], D)).then_inc(s_b, 16)
                    sp.dma_start(bo[:, :], bcast(io["bias"][3], D)).then_inc(s_b, 16)
                    sp.wait_ge(s_b, 32)

                @block.gpsimd
                def _(pool):
                    pool.memset(vaug[:, :, :, :, :, HDA:2 * HDA].rearrange("p b a k h r -> p (b a k h) r"), 1.0).then_inc(s_one, 1)
            project_qkv(nc, io, x, xt, scratch, vaug, vb, bo, wo)
            attend(nc, scratch, vaug, oall, identb)
            project_out(nc, x, oall, wo, ident)
        if stages >= 2:
            normalise(nc, "n2", x, ident, xt)
            route(nc, io, "r2", xt, comb, rbias, iota)
            experts(nc, io, "e2", x, xt, comb)
        if stages >= 3:
            normalise(nc, "n3", x, ident, xt)
            retain(nc, io, x, xt, ident)
        if stages >= 4:
            normalise(nc, "n4", x, ident, xt)
            route(nc, io, "r4", xt, comb, rbias, iota)
            experts(nc, io, "e4", x, xt, comb)
        with nc.Block() as block:
            @block.sync
            def _(sp):
                ov = out.rearrange("b (t p) d -> p (b t) d", p=P)
                for b in range(NB):
                    sp.dma_start(ov[:, b * TPB:(b + 1) * TPB, :], x[:, b * TPB:(b + 1) * TPB, :]).then_inc(s_out, 16)
                sp.wait_ge(s_out, 16 * NB)


def constants():
    gamma = 1.0 - np.exp2(-5.0 - np.arange(HB, dtype=np.float64))
    inv = 1.0 / 10000.0 ** (np.arange(0, DK, 2, dtype=np.float64) / DK)
    f = np.arange(L, dtype=np.float64)[:, None] * inv[None, :]
    i = np.arange(P, dtype=np.float64)[:, None]
    f4 = np.float32

    def tiles(a):
        return np.tile(a.reshape(KT, P, -1).transpose(1, 0, 2), (1, B, 1))

    gdec = np.zeros((P, 2, NT))
    for g in range(2):
        gdec[:, g, :] = (gamma[g * 4 + np.arange(P) // 32] ** P)[:, None]
    gdec[:, :, KT - 1::KT] = 0.0
    return {
        "cos": tiles(np.concatenate([np.cos(f), np.cos(f)], 1)).astype(f4),
        "sin": tiles(np.concatenate([-np.sin(f), np.sin(f)], 1)).astype(f4),
        "dec": np.concatenate([gamma ** i * DK ** -0.5, gamma ** -i], 1).astype(f4),
        "mask": (np.arange(P)[None, :] >= np.arange(P)[:, None]).astype(f4),
        "bd": (np.arange(P)[:, None] // 32 == np.arange(4)[None, :]).astype(f4),
        "gdec": gdec.astype(f4),
        "ident": np.eye(P, dtype=f4),
        "iota": np.arange(NE, dtype=f4),
    }


def lay_out(i):
    g = {k.replace("L0_", ""): np.asarray(v) for k, v in i.items()}
    a = lambda n: [g[f"attn_a_{n}{m}"] for m in "qkvo"]
    sh = [g["ffn_Su"][0], g["ffn_Sg"][0], g["ffn_Sd"][0]]
    up = np.concatenate([np.stack([g["ffn_Wu"], g["ffn_Wg"]], 2).reshape(NE, D, 2 * ED),
                         np.stack([np.concatenate([sh[0][:, k * ED:(k + 1) * ED], sh[1][:, k * ED:(k + 1) * ED]], 1)
                                   for k in range(2)])], 0)
    dn = np.concatenate([g["ffn_Wd"], sh[2].reshape(2, ED, D)], 0)
    return {
        "x": g["attn_a_x"],
        "WT": np.stack([w.T for w in a("W")]), "bias": np.stack(a("b")),
        "biasT": np.stack(a("b")[:3]).reshape(3, DH, P).transpose(2, 0, 1),
        "Bm": np.stack(a("B")), "AmT": np.stack([m.T for m in a("A")]),
        "RwT": np.ascontiguousarray(g["ffn_router_w"].T), "rbias": g["ffn_router_bias"],
        "Wup": up.reshape(NU // 2, 2, D, 2 * ED), "Wdn": dn.reshape(NU // 2, 2, ED, D),
        "Wret": np.concatenate([g[f"attn_b_W{m}"] for m in "qkvg"], 1), "WoB": g["attn_b_Wo"],
        "gnw": g["attn_b_g_norm_weight"],
    } | constants()


def kernel(**inputs):
    import concourse.bacc as bacc
    from concourse.bass_utils import run_bass_kernel_spmd

    nc = bacc.Bacc("TRN2", target_bir_lowering=False, num_devices=1)
    arrays = {f"in_{k}": np.ascontiguousarray(v) for k, v in lay_out(inputs).items()}
    io = {k[3:]: nc.dram_tensor(k, v.shape, mybir.dt.from_np(v.dtype), kind="ExternalInput").ap()
          for k, v in arrays.items()}
    out = nc.dram_tensor("out_x", [B, L, D], F32, kind="ExternalOutput").ap()
    build(nc, io, out)
    r = run_bass_kernel_spmd(nc, [arrays], core_ids=[0])
    return r.results[0]["out_x"]
```

```python
from contextlib import ExitStack

import numpy as np
import concourse.bass as bass
from concourse import mybir

F32 = mybir.dt.float32
F32R = mybir.dt.float32r
BF16 = mybir.dt.bfloat16
U32 = mybir.dt.uint32
I32 = mybir.dt.int32
ALU = mybir.AluOpType
ACT = mybir.ActivationFunctionType
AX_X = mybir.AxisListType.X

P = 128
B, L, D = 2, 1024, 256
N = B * L
NT = N // P
BLK = 512
NB = N // BLK
TPB = BLK // P
DH = D // P
EPS = 1e-5

HA, HDA, RANK = 16, 16, 16
SCALING = 8.0 / RANK
SCALE_A = HDA ** -0.5
HPG = 4
KT = L // P
TERMS = [(0, 0), (0, 1), (1, 0), (1, 1), (0, 2), (2, 0)]
KROWS = len(TERMS) * HDA
KEXP = KROWS + 3
JOBS = HPG * (BLK // P) * 2
RING = 3
RPS = JOBS + 1
SKEW = 3
TJ = 4

NE, ED = 16, 128
NU = NE + 2
TILES = 2 * N // P + NE
WORDS = TILES // 4
WC = DH * 2 * ED
WN = WC + D

HB, DK, DV = 8, 32, 64
QK = 2 * HB * DK
DVT = HB * DV


class Ctx:

    semaphores = []

    def __init__(self, nc, es, tag):
        self.nc, self.es, self.tag = nc, es, tag

    def sb(self, name, shape, dt=F32):
        return self.es.enter_context(self.nc.sbuf_tensor(f"{self.tag}_{name}", shape, dt))

    def ps(self, name, shape, dt=F32):
        return self.es.enter_context(self.nc.psum_tensor(f"{self.tag}_{name}", shape, dt))

    def sem(self, name):
        s_ = self.nc.alloc_semaphore(f"{self.tag}_{name}")
        Ctx.semaphores.append(s_)
        return s_


def clear_semaphores(nc):
    nc.clear_and_free_semaphores(Ctx.semaphores)
    nc.all_engine_barrier()
    Ctx.semaphores = []


def products(eng, out, lhs, rhs, first, last):
    pairs = [(0, 0), (0, 1), (1, 0)]
    for n, (a, b) in enumerate(pairs):
        mm = eng.matmul(out, lhs[a], rhs[b], start=first and n == 0, stop=last and n == 2)
    return mm


def normalise(nc, tag, x, ident, xt, keep=None):
    with ExitStack() as es:
        c = Ctx(nc, es, tag)
        stats = c.sb("stats", [P, NT, 6])
        mv = c.sb("mv", [P, NT, 2])
        ve, nhalf, rstd = (c.sb(n, [P, NT, 1]) for n in ("ve", "nhalf", "rstd"))
        xn = keep if keep is not None else c.sb("xn", [P, 2 * TPB, D])
        TX = NT if keep is not None else 2 * TPB
        pt = [c.ps(f"pt{n}", [P, BLK]) for n in range(4)]
        s_stats, s_mv, s_var, s_rstd = c.sem("stats"), c.sem("mv"), c.sem("var"), c.sem("rstd")
        s_half = c.sem("half")
        s_xn, s_t, s_hi, s_lo = c.sem("xn"), c.sem("transposed"), c.sem("hi"), c.sem("lo")
        block = es.enter_context(nc.Block())

        @block.vector
        def _(dve):
            for t in range(NT):
                dve.bn_stats(stats[:, t, :], x[:, t, :]).then_inc(s_stats, 1)
            for t in range(NT):
                dve.wait_ge(s_stats, t + 1)
                dve.bn_aggr(mv[:, t, :], stats[:, t, :]).then_inc(s_mv, 1)
            dve.wait_ge(s_mv, NT)
            dve.tensor_scalar(ve[:, :, :], mv[:, :, 1:2], EPS, None, ALU.add).then_inc(s_var, 1)
            dve.wait_ge(s_rstd, 1)

            def scale(b):
                if b >= 2 and keep is None:
                    dve.wait_ge(s_t, 2 * (b - 1))
                for j in range(TPB):
                    t = b * TPB + j
                    dve.tensor_scalar(xn[:, t % TX, :], x[:, t, :], mv[:, t, 0:1], rstd[:, t, :],
                                      ALU.subtract, ALU.mult).then_inc(s_xn, 1)

            scale(0)
            for b in range(NB):
                if b + 1 < NB:
                    scale(b + 1)
                for h in range(DH):
                    n = DH * b + h
                    dve.wait_ge(s_hi, n + 1)
                    dve.tensor_tensor(xt[1][:, h, b * BLK:(b + 1) * BLK], pt[n % 4][:, :],
                                      xt[0][:, h, b * BLK:(b + 1) * BLK].bitcast(F32),
                                      ALU.subtract).then_inc(s_lo, 1)

        @block.gpsimd
        def _(pool):
            pool.memset(nhalf[:, :, :], -0.5).then_inc(s_half, 1)
            pool.wait_ge(s_half, 1)
            pool.wait_ge(s_var, 1)
            pool.tensor_tensor(rstd[:, :, :], ve[:, :, :], nhalf[:, :, :], ALU.pow).then_inc(s_rstd, 1)

        @block.tensor
        def _(pe):
            for b in range(NB):
                pe.wait_ge(s_xn, TPB * (b + 1))
                for h in range(DH):
                    n = DH * b + h
                    if n >= 4:
                        pe.wait_ge(s_lo, n - 3)
                    for j in range(TPB):
                        mm = pe.transpose(pt[n % 4][:, j * P:(j + 1) * P],
                                          xn[:, (b * TPB + j) % TX, h * P:(h + 1) * P], ident[:, :])
                    mm.then_inc(s_t, 1)

        @block.scalar
        def _(act):
            for n in range(DH * NB):
                b, h = n // DH, n % DH
                act.wait_ge(s_t, n + 1)
                act.activation(xt[0][:, h, b * BLK:(b + 1) * BLK], pt[n % 4][:, :], ACT.Copy).then_inc(s_hi, 1)


def project_qkv(nc, io, x, xt, scratch, vaug, vb, bo, wo):
    with ExitStack() as es:
        c = Ctx(nc, es, "pj")
        wt = c.sb("wt", [P, 4, DH, D])
        bm = c.sb("bm", [RANK, 4, D])
        am = c.sb("am", [RANK, 4, D])
        bias = c.sb("bias", [P, 3, DH])
        biass = c.sb("biass", [P, 3, DH])
        weff = c.sb("weff", [P, 3, DH, D])
        whi = c.sb("whi", [P, 3, DH, D], F32R)
        wlo = c.sb("wlo", [P, 3, DH, D], F32R)
        xf = c.sb("xf", [P, 2, BLK])
        rf = c.sb("rf", [P, 2, BLK])
        parts = c.sb("parts", [P, 2, 3, BLK], BF16)
        pw = [c.ps(f"pw{n}", [P, BLK]) for n in range(2)]
        pp = [c.ps(f"pp{n}", [P, BLK]) for n in range(3)]
        pv = [c.ps(f"pv{n}", [P, BLK]) for n in range(2)]
        s_w, s_lora, s_weff, s_hi, s_lo, s_bias = (c.sem(n) for n in ("w", "lora", "weff", "whi", "wlo", "bias"))
        s_mm, s_xf, s_h, s_r, s_m, s_l = (c.sem(n) for n in ("mm", "xf", "h", "r", "m", "l"))
        s_st = [c.sem(f"stored{n}") for n in range(2)]
        s_vm, s_va, s_xb = c.sem("vmm"), c.sem("vadd"), c.sem("x_bias")
        JQ = 2 * DH * NB
        block = es.enter_context(nc.Block())

        @block.sync
        def _(sp):
            for n in range(4):
                sp.dma_start(wt[:, n, :, :], io["WT"][n].rearrange("(h p) o -> p h o", p=P)).then_inc(s_w, 16)
            sp.dma_start(bm[:, :, :], io["Bm"].rearrange("n r d -> r n d")).then_inc(s_w, 16)
            sp.dma_start(am[:, :, :], io["AmT"].rearrange("n r o -> r n o")).then_inc(s_w, 16)
            sp.dma_start(bias[:, :, :], io["biasT"]).then_inc(s_w, 16)
            for n in range(JQ):
                side, half, tb = n // (DH * NB), n // NB % DH, n % NB
                bb, off = tb * BLK // L, tb * BLK % L
                sp.wait_ge(s_l, n + 1)
                for k in range(3):
                    sp.dma_start(scratch[side, k, bb * DH + half].rearrange("u h r t -> (u h r) t")[:, off:off + BLK],
                                 parts[:, n % 2, k, :]).then_inc(s_st[n % 2], 16)
            for s_ in s_st:
                sp.wait_ge(s_, 16 * 3 * JQ // 2)

        @block.tensor
        def _(pe):
            pe.wait_ge(s_w, 16 * 7)
            for n in range(4):
                if n >= 2:
                    pe.wait_ge(s_weff, n - 1)
                for h in range(DH):
                    mm = pe.matmul(pw[n % 2][:, h * D:(h + 1) * D], bm[:, n, h * P:(h + 1) * P], am[:, n, :],
                                   start=True, stop=True)
                mm.then_inc(s_lora, 1)
            pe.wait_ge(s_hi, 3)
            pe.wait_ge(s_lo, 3)
            w = (whi, wlo)
            for n in range(JQ):
                side, half, tb = n // (DH * NB), n // NB % DH, n % NB
                if n >= 3:
                    pe.wait_ge(s_xf, n - 2)
                for h in range(DH):
                    mm = products(pe, pp[n % 3][:, :], [a[:, side, h, half * P:(half + 1) * P] for a in w],
                                  [a[:, h, tb * BLK:(tb + 1) * BLK] for a in xt], h == 0, h == DH - 1)
                mm.then_inc(s_mm, 1)
                t = n
                if t >= 2:
                    pe.wait_ge(s_va, t - 1)
                for h in range(DH):
                    mm = products(pe, pv[t % 2][:, 0:D], [a[:, h, t * P:(t + 1) * P] for a in xt],
                                  [a[:, 2, h, :] for a in w], h == 0, h == DH - 1)
                mm.then_inc(s_vm, 1)

        @block.gpsimd
        def _(pool):
            for t in range(NT):
                pool.tensor_tensor(x[:, t, :], x[:, t, :], bo[:, :], ALU.add).then_inc(s_xb, 1)

        @block.scalar
        def _(act):
            act.wait_ge(s_w, 16 * 7)
            act.mul(biass[:, :, :], bias[:, :, :], SCALE_A).then_inc(s_bias, 1)
            for n in range(3):
                act.wait_ge(s_weff, n + 1)
                act.activation(whi[:, n, :, :], weff[:, n, :, :], ACT.Copy).then_inc(s_hi, 1)
            act.wait_ge(s_bias, 1)
            for n in range(JQ):
                side, half = n // (DH * NB), n // NB % DH
                act.wait_ge(s_mm, n + 1)
                if n >= 2:
                    act.wait_ge(s_r, n - 1)
                    act.wait_ge(s_st[n % 2], 16 * 3 * (n // 2))
                b = biass if side == 0 else bias
                act.activation(xf[:, n % 2, :], pp[n % 3][:, :], ACT.Identity, bias=b[:, side, half:half + 1],
                               scale=SCALE_A if side == 0 else 1.0).then_inc(s_xf, 1)
                act.wait_ge(s_xf, n + 1)
                act.activation(parts[:, n % 2, 0, :], xf[:, n % 2, :], ACT.Copy).then_inc(s_h, 1)
                act.wait_ge(s_r, n + 1)
                act.activation(parts[:, n % 2, 1, :], rf[:, n % 2, :], ACT.Copy).then_inc(s_m, 1)

        @block.vector
        def _(dve):
            dve.wait_ge(s_w, 16 * 7)
            for n in range(4):
                dve.wait_ge(s_lora, n + 1)
                dve.scalar_tensor_tensor(out=weff[:, n, :, :] if n < 3 else wo[:, :, :], in0=pw[n % 2][:, :].rearrange("p (h o) -> p h o", h=DH),
                                         scalar=SCALING, in1=wt[:, n, :, :], op0=ALU.mult,
                                         op1=ALU.add).then_inc(s_weff, 1)
            for n in range(3):
                dve.wait_ge(s_hi, n + 1)
                dve.tensor_tensor(wlo[:, n, :, :], weff[:, n, :, :], whi[:, n, :, :].bitcast(F32),
                                  ALU.subtract).then_inc(s_lo, 1)
            for n in range(JQ):
                dve.wait_ge(s_h, n + 1)
                dve.tensor_tensor(rf[:, n % 2, :], xf[:, n % 2, :], parts[:, n % 2, 0, :], ALU.subtract).then_inc(s_r, 1)
                t = n
                dve.wait_ge(s_vm, t + 1)
                dve.tensor_tensor(vaug[:, t // KT, :, t % KT, :, 0:HDA],
                                  pv[t % 2][:, 0:D].rearrange("p (a h r) -> p a h r", a=DH, r=HDA),
                                  vb[:, :].rearrange("p (a h r) -> p a h r", a=DH, r=HDA), ALU.add).then_inc(s_va, 1)
                dve.wait_ge(s_m, n + 1)
                dve.tensor_tensor(parts[:, n % 2, 2, :], rf[:, n % 2, :], parts[:, n % 2, 1, :],
                                  ALU.subtract).then_inc(s_l, 1)


def attend(nc, scratch, vaug, oall, identb):
    STEPS = B * DH
    SUBS = 4
    with ExitStack() as es:
        c = Ctx(nc, es, "at")
        kst = [c.sb(f"kst{u}", [KEXP, HPG, L], BF16) for u in range(2)]
        qst = [c.sb(f"qst{u}", [KEXP, 2, HPG, BLK], BF16) for u in range(2)]
        vst = [c.sb(f"vst{u}", [P, KT, HPG, 32]) for u in range(2)]
        prob = [c.sb(f"prob{n}", [P, HPG, BLK]) for n in range(4)]
        mx = c.sb("mx", [P, JOBS])
        mrow = c.sb("mrow", [P, 2, JOBS // 2])
        mneg = c.sb("mneg", [P, JOBS // 2])
        mres = c.sb("mres", [P, JOBS // 2])
        zero = c.sb("zero", [P, JOBS // 2])
        msplit = c.sb("msplit", [P, P], BF16)
        mT = [c.sb(f"mT{n}", [P, P], BF16) for n in range(2)]
        ps_s = [c.ps(f"score{n}", [P, 2, BLK]) for n in range(2)]
        ps_m = [c.ps(f"max{n}", [P, BLK]) for n in range(RING)]
        ps_o = c.ps("out", [P, BLK])
        s_stack = [c.sem(f"stack_loaded{u}") for u in range(2)]
        s_rows, s_ones = c.sem("max_rows_loaded"), c.sem("ones")
        s_vst = c.sem("v_staged")
        s_score = [c.sem(f"scores_ready{n}") for n in range(2)]
        s_exp = [c.sem(f"exp_done{n}") for n in range(2)]
        s_pv, s_oev = c.sem("sub_values_done"), c.sem("out_evacuated")
        s_mm, s_free, s_chain, s_split = (c.sem(n) for n in ("max_ready", "max_bank_free", "max_chain", "max_split"))
        s_comb, s_zero = c.sem("max_combined"), c.sem("zero")
        SLOTS = SUBS * KT
        JPS = JOBS // KT
        UNIT_DMAS = 3 * len(TERMS)
        CH = 4
        block = es.enter_context(nc.Block())

        def sub(i, s):
            return SUBS * i + s

        def job_slot(n, j):
            if type(n) is int and n == 0:
                return j, j % RING
            k = j if j < TJ else j + 1
            return RPS * n + k - 1, (k - 1) % RING

        def turn_slot(n):
            k = TJ if type(n) is not int or n < SUBS * STEPS - 1 else 0
            return RPS * (n + 1) + k - 1, (k - 1) % RING

        @block.sync
        def _(sp):
            def load_unit(i, u):
                for n, (ck, cq) in enumerate(TERMS):
                    rows = slice(n * HDA, (n + 1) * HDA)
                    sp.dma_start(kst[u][rows, :, :], scratch[1, ck, i, u].rearrange("h r t -> r h t")).then_inc(s_stack[u], 16)
                    for qh in range(2):
                        sp.dma_start(qst[u][rows, qh, :, :],
                                     scratch[0, cq, i, u].rearrange("h r t -> r h t")[:, :, qh * BLK:(qh + 1) * BLK]
                                     ).then_inc(s_stack[u], 16)

            def load_rows(n, s):
                sp.wait_ge(s_free, turn_slot(n)[0] + 1)
                for k in range(3):
                    sp.dma_start(qst[s // 2][KROWS + k:KROWS + k + 1, s % 2, :, :].rearrange("o h (t j) -> o (h t) j", j=P),
                                 mT[s % 2][k * (JOBS // 2):(k + 1) * (JOBS // 2), :]).then_inc(s_rows, 16)

            load_unit(0, 0)
            load_unit(0, 1)
            load_rows(0, 0)

            def step(i, last):
                for s in range(SUBS):
                    if not (last and s == SUBS - 1):
                        load_rows(sub(i, s) + 1, (s + 1) % SUBS)
                    if s % 2 and not last:
                        sp.wait_ge(s_score[1], KT * (sub(i, s) + 1))
                        load_unit(i + 1, s // 2)

            with sp.Fori(0, STEPS - 1) as i:
                step(i, False)
            step(STEPS - 1, True)

        @block.gpsimd
        def _(pool):
            def stage(i, u):
                pool.tensor_copy(vst[u][:, :, :, :],
                                 vaug[:, :, :, :, :, :].rearrange("p b a k h r -> p (b a) k h r")
                                 [:, i, :, u * HPG:(u + 1) * HPG, :]).then_inc(s_vst, 1)

            def split(n, s):
                h, m, l = (msplit[:, k * JOBS // 2:(k + 1) * JOBS // 2] for k in range(3))
                pool.wait_ge(s_comb, n + 1)
                if type(n) is not int or n > 0:
                    pool.wait_ge(s_mm, turn_slot(n - 1)[0] + 1)
                pool.tensor_tensor(mneg[:, :], zero[:, :], mrow[:, s % 2, :], ALU.subtract).then_inc(s_chain, 1)
                pool.wait_ge(s_chain, CH * n + 1)
                pool.tensor_tensor(h, mneg[:, :], zero[:, :], ALU.add).then_inc(s_chain, 1)
                pool.wait_ge(s_chain, CH * n + 2)
                pool.tensor_tensor(mres[:, :], mneg[:, :], h, ALU.subtract).then_inc(s_chain, 1)
                pool.wait_ge(s_chain, CH * n + 3)
                pool.tensor_tensor(m, mres[:, :], zero[:, :], ALU.add).then_inc(s_chain, 1)
                pool.wait_ge(s_chain, CH * n + 4)
                pool.tensor_tensor(l, mres[:, :], m, ALU.subtract).then_inc(s_split, 1)

            pool.memset(zero[:, :], 0.0).then_inc(s_zero, 1)
            pool.wait_ge(s_zero, 1)
            split(0, 0)
            stage(0, 0)
            stage(0, 1)
            with pool.Fori(0, STEPS - 1) as i:
                for s in range(SUBS):
                    split(sub(i, s) + 1, s + 1)
                    if s % 2:
                        pool.wait_ge(s_pv, sub(i, s) + 1)
                        stage(i + 1, s // 2)
            for s in range(SUBS - 1):
                split(sub(STEPS - 1, s) + 1, s + 1)

        @block.tensor
        def _(pe):
            def max_job(i, s, j):
                i, s = i + s // SUBS, s % SUBS
                n = sub(i, s)
                slot, bank = job_slot(n, j)
                if type(n) is not int or slot >= RING:
                    pe.wait_ge(s_free, slot - RING + 1)
                if j == 0 and s % 2 == 0:
                    pe.wait_ge(s_stack[s // 2], UNIT_DMAS * 16 * (i + 1))
                h, qt, kh = j // 8, j // 2 % 4, j % 2
                pe.matmul(ps_m[bank][:, :], qst[s // 2][0:KROWS, s % 2, h, qt * P:(qt + 1) * P],
                          kst[s // 2][0:KROWS, h, kh * BLK:(kh + 1) * BLK], start=True, stop=True).then_inc(s_mm, 1)

            def max_turn(n, s):
                slot, bank = turn_slot(n)
                pe.wait_ge(s_split, n + 1)
                pe.wait_ge(s_free, slot - RING + 1)
                pe.transpose(ps_m[bank][:, 0:P // 2].bitcast(BF16), msplit[:, :], identb[:, :]).then_inc(s_mm, 1)

            def scores(n, s, kt, pair):
                if kt == 0 and pair == 0:
                    pe.wait_ge(s_rows, 16 * 3 * (n + 1))
                pe.wait_ge(s_exp[pair], KT * n + kt + 1)
                for k in range(2):
                    h = 2 * pair + k
                    mm = pe.matmul(ps_s[pair][:, k, :], kst[s // 2][:, h, kt * P:(kt + 1) * P],
                                   qst[s // 2][:, s % 2, h, :], start=True, stop=True)
                mm.then_inc(s_score[pair], 1)

            def values(i, s, kt):
                n = sub(i, s)
                for pair in range(2):
                    pe.wait_ge(s_exp[pair], KT * n + kt + 2)
                if kt == 0:
                    pe.wait_ge(s_oev, n + 1)
                    if s % 2 == 0:
                        pe.wait_ge(s_vst, 2 * i + s // 2 + 1)
                for h in range(HPG):
                    mm = pe.matmul(ps_o[32 * h:32 * h + 32, :], vst[s // 2][:, kt, h, :], prob[kt % 4][:, h, :],
                                   start=(kt == 0), stop=(kt == KT - 1))
                if kt == KT - 1:
                    mm.then_inc(s_pv, 1)

            def slot(i, r, last):
                i, r = i + r // SLOTS, r % SLOTS
                s, kt = r // KT, r % KT

                def job(q):
                    j = JPS * (kt + SKEW) + q
                    ahead = s + 1 + j // JOBS
                    if j % JOBS == TJ and j >= JOBS and not (last and s + 1 >= SUBS):
                        max_turn(sub(i, s) + 1, (s + 1) % SUBS)
                    if not (last and ahead >= SUBS):
                        max_job(i, ahead, j % JOBS)

                scores(sub(i, s), s, kt, 0)
                job(0)
                scores(sub(i, s), s, kt, 1)
                job(1)
                job(2)
                if type(i) is not int or i > 0 or r > 0:
                    p = r - 1
                    values(i if p >= 0 else i - 1, p % SLOTS // KT, p % KT)
                job(3)

            pe.wait_ge(s_ones, 3)
            for j in range(JOBS):
                max_job(0, 0, j)
            for j in range(TJ):
                max_job(0, 1, j)
            max_turn(0, 0)
            for j in range(TJ, JPS * SKEW):
                max_job(0, 1, j)
            slot(0, 0, False)
            with pe.Fori(0, STEPS - 1) as i:
                for r in range(1, SLOTS + 1):
                    slot(i, r, False)
            for r in range(1, SLOTS):
                slot(STEPS - 1, r, True)
            values(STEPS - 1, SUBS - 1, KT - 1)

        @block.scalar
        def _(act):
            def evacuate(i, s):
                n = sub(i, s)
                act.wait_ge(s_pv, n + 1)
                act.activation(oall[:, i, s // 2, s % 2, :], ps_o[:, :], ACT.Copy).then_inc(s_oev, 1)

            def slot(i, r):
                i, r = i + r // SLOTS, r % SLOTS
                s, kt = r // KT, r % KT
                for pair in range(2):
                    act.wait_ge(s_score[pair], KT * sub(i, s) + kt + 1)
                    act.activation(prob[kt % 4][:, 2 * pair:2 * pair + 2, :], ps_s[pair][:, :, :],
                                   ACT.Exp).then_inc(s_exp[pair], 1)

            for sem in (*s_exp, s_oev):
                act.sem_inc(sem, 1)
            slot(0, 0)
            with act.Fori(0, STEPS - 1) as i:
                for r in range(1, SLOTS + 1):
                    slot(i, r)
                    if r % KT == 0:
                        evacuate(i, r // KT - 1)
            for r in range(1, SLOTS):
                slot(STEPS - 1, r)
                if r % KT == 0:
                    evacuate(STEPS - 1, r // KT - 1)
            evacuate(STEPS - 1, SUBS - 1)

        @block.vector
        def _(dve):
            def reduce(n, j):
                slot, bank = job_slot(n, j)
                dve.wait_ge(s_mm, slot + 1)
                dve.tensor_reduce(mx[:, j:j + 1], ps_m[bank][:, :], AX_X, ALU.max).then_inc(s_free, 1)

            def combine(n, s):
                dve.wait_ge(s_free, job_slot(n, JOBS - 1)[0] + 1)
                if type(n) is not int or n > 1:
                    dve.wait_ge(s_split, n - 1)
                dve.tensor_reduce(mrow[:, s % 2, :], mx[:, :].rearrange("p (n k) -> p n k", k=2), AX_X,
                                  ALU.max).then_inc(s_comb, 1)
                dve.wait_ge(s_comb, n + 1)

            def turned(n, s):
                slot, bank = turn_slot(n)
                dve.wait_ge(s_mm, slot + 1)
                dve.tensor_copy(mT[s % 2][:, :], ps_m[bank][:, 0:P // 2].bitcast(BF16)).then_inc(s_free, 1)

            def step(i, last):
                for s in range(SUBS):
                    n = sub(i, s)
                    if last and s + 1 >= SUBS:
                        continue
                    for j in range(JPS * SKEW, JOBS):
                        reduce(n + 1, j)
                    combine(n + 1, s + 1)
                    for j in range(JPS * SKEW):
                        if j == TJ:
                            turned(n + 1, (s + 1) % SUBS)
                        if not (last and s + 2 >= SUBS):
                            reduce(n + 2, j)

            dve.memset(msplit[:, :], 0.0).then_inc(s_ones, 1)
            for u in range(2):
                dve.memset(kst[u][KROWS:KEXP, :, :], 1.0).then_inc(s_ones, 1)
            for j in range(JOBS):
                reduce(0, j)
            combine(0, 0)
            for j in range(JPS * SKEW):
                if j == TJ:
                    turned(0, 0)
                reduce(1, j)
            with dve.Fori(0, STEPS - 1) as i:
                step(i, False)
            step(STEPS - 1, True)


def project_out(nc, x, oall, wo, ident):
    with ExitStack() as es:
        c = Ctx(nc, es, "po")
        rec = c.sb("rec", [P, 2, HA, 1])
        at = c.sb("at", [P, 2, D])
        atT = c.sb("atT", [P, 2, D])
        p_h = [c.ps(f"heads{n}", [P, BLK]) for n in range(2)]
        p_t = [c.ps(f"turned{n}", [P, BLK]) for n in range(2)]
        p_y = [c.ps(f"y{n}", [P, BLK]) for n in range(2)]
        s_h, s_rec, s_at, s_t, s_tc, s_y, s_x = (c.sem(n) for n in ("heads", "rec", "at", "t", "tc", "y", "x"))
        block = es.enter_context(nc.Block())

        @block.tensor
        def _(pe):
            def heads(t):
                b, qh, j = t // KT, t % KT // TPB, t % TPB
                if t >= 2:
                    pe.wait_ge(s_at, t - 1)
                for g in range(4):
                    mm = pe.transpose(p_h[t % 2][:, g * P:(g + 1) * P],
                                      oall[:, DH * b + g // 2, g % 2, qh, j * P:(j + 1) * P], ident[:, :])
                mm.then_inc(s_h, 1)

            def project(t):
                pe.wait_ge(s_tc, t + 1)
                if t >= 2:
                    pe.wait_ge(s_x, t - 1)
                for h in range(DH):
                    mm = pe.matmul(p_y[t % 2][:, 0:D], atT[:, t % 2, h * P:(h + 1) * P], wo[:, h, :],
                                   start=(h == 0), stop=(h == DH - 1))
                mm.then_inc(s_y, 1)

            heads(0)
            for t in range(NT):
                if t + 1 < NT:
                    heads(t + 1)
                pe.wait_ge(s_at, t + 1)
                if t >= 2:
                    pe.wait_ge(s_tc, t - 1)
                for h in range(DH):
                    mm = pe.transpose(p_t[t % 2][:, h * P:(h + 1) * P], at[:, t % 2, h * P:(h + 1) * P], ident[:, :])
                mm.then_inc(s_t, 1)
                if t >= 1:
                    project(t - 1)
            project(NT - 1)

        @block.scalar
        def _(act):
            for t in range(NT):
                act.wait_ge(s_t, t + 1)
                if t >= 2:
                    act.wait_ge(s_y, t - 1)
                act.activation(atT[:, t % 2, :], p_t[t % 2][:, 0:D], ACT.Copy).then_inc(s_tc, 1)

        @block.vector
        def _(dve):
            def add(t):
                dve.wait_ge(s_y, t + 1)
                dve.tensor_tensor(x[:, t, :], p_y[t % 2][:, 0:D], x[:, t, :], ALU.add).then_inc(s_x, 1)

            for t in range(NT):
                heads = p_h[t % 2][:, :].rearrange("p (h r) -> p h r", r=2 * HDA)
                dve.wait_ge(s_h, t + 1)
                dve.reciprocal(rec[:, t % 2, :, :], heads[:, :, HDA:HDA + 1]).then_inc(s_rec, 1)
                dve.wait_ge(s_rec, t + 1)
                if t >= 2:
                    dve.wait_ge(s_t, t - 1)
                dve.tensor_tensor(at[:, t % 2, :].rearrange("p (h r) -> p h r", r=HDA), heads[:, :, 0:HDA],
                                  rec[:, t % 2, :, :].broadcast_to([P, HA, HDA]), ALU.mult).then_inc(s_at, 1)
                if t >= 2:
                    add(t - 2)
            add(NT - 2)
            add(NT - 1)


def route(nc, io, tag, xt, c2):
    with ExitStack() as es:
        c = Ctx(nc, es, tag)
        rw = c.sb("rw", [P, DH, NE])
        rhi, rlo = c.sb("rhi", [P, DH, NE], F32R), c.sb("rlo", [P, DH, NE], F32R)
        lg, lb, sh, ex, pos = (c.sb(n, [P, NT, NE]) for n in ("lg", "lb", "sh", "ex", "pos"))
        m8 = c.sb("m8", [P, NT, 8])
        i8 = c.sb("i8", [P, NT, 8], U32)
        idx = c.sb("idx", [P, NT, 2])
        oh, ow, op = (c.sb(n, [P, 2, NT, NE]) for n in ("oh", "ow", "op"))
        sel = c.sb("sel", [P, NT, NE], BF16)
        mraw, tot, rt = (c.sb(n, [P, NT, 1]) for n in ("mraw", "tot", "rt"))
        wraw, slotf = c.sb("wraw", [P, 2, NT]), c.sb("slotf", [P, 2, NT])
        cnt, tiles, first, base, end = (c.sb(n, [P, NE, 1]) for n in ("cnt", "tiles", "first", "base", "end"))
        more, before = c.sb("more", [P, NE, NE]), c.sb("before", [P, NE, NE])
        half, upper = c.sb("half", [1, WORDS, 1]), c.sb("upper", [1, WORDS - 1], I32)
        past, eidf = c.sb("past", [1, TILES, NE]), c.sb("eidf", [1, TILES, 1])
        pl, pr, pc = (c.ps(n, [P, BLK]) for n in ("logits", "ranks", "counts"))
        s_w, s_hi, s_lo, s_l, s_lg, s_e, s_c, s_sel, s_rank = (
            c.sem(n) for n in ("w", "hi", "lo", "logits", "lg", "exp", "chain", "sel", "rank"))
        block = es.enter_context(nc.Block())
        shape = [P, NT, NE]

        @block.sync
        def _(sp):
            sp.dma_start(rw[:, :, :], io["RwT"].rearrange("(h p) e -> p h e", p=P)).then_inc(s_w, 16)

        @block.tensor
        def _(pe):
            pe.wait_ge(s_lo, 1)
            for t in range(NT):
                for h in range(DH):
                    mm = products(pe, pl[:, t * NE:(t + 1) * NE], [a[:, h, t * P:(t + 1) * P] for a in xt],
                                  [rhi[:, h, :], rlo[:, h, :]], h == 0, h == DH - 1)
            mm.then_inc(s_l, 1)
            pe.wait_ge(s_sel, 1)
            pe.matmul(pc[:, 0:NT * NE], c2.onesb[:, :], sel[:, :, :], start=True, stop=True)
            pe.matmul(pr[:, 0:NT * NE], c2.trib[:, :], sel[:, :, :], start=True, stop=False, skip_group_check=True)
            for t in range(NT - 1):
                mm = pe.matmul(pr[:, (t + 1) * NE:NT * NE], c2.onesb[:, :],
                               sel[:, t:t + 1, :].broadcast_to([P, NT - 1 - t, NE]), start=False, stop=(t == NT - 2),
                               skip_group_check=True)
            mm.then_inc(s_rank, 1)

        @block.scalar
        def _(act):
            act.wait_ge(s_w, 16)
            act.activation(rhi[:, :, :], rw[:, :, :], ACT.Copy).then_inc(s_hi, 1)
            act.wait_ge(s_l, 1)
            act.activation(lg[:, :, :], pl[:, 0:NT * NE].rearrange("p (t e) -> p t e", e=NE), ACT.Copy).then_inc(s_lg, 1)
            act.wait_ge(s_c, 2)
            act.activation(ex[:, :, :], sh[:, :, :], ACT.Exp).then_inc(s_e, 1)

        @block.vector
        def _(dve):
            done = [0]

            def link(ins):
                done[0] += 1
                ins.then_inc(s_c, 1)
                dve.wait_ge(s_c, done[0])

            dve.wait_ge(s_hi, 1)
            dve.tensor_tensor(rlo[:, :, :], rw[:, :, :], rhi[:, :, :].bitcast(F32), ALU.subtract).then_inc(s_lo, 1)
            dve.wait_ge(s_lg, 1)
            link(dve.tensor_reduce(mraw[:, :, :], lg[:, :, :], AX_X, ALU.max))
            link(dve.tensor_tensor(sh[:, :, :], lg[:, :, :], mraw[:, :, :].broadcast_to(shape), ALU.subtract))
            link(dve.tensor_tensor(lb[:, :, :], lg[:, :, :], c2.rbias[:, :, :].broadcast_to(shape), ALU.add))
            for t in range(NT):
                dve.max(m8[:, t, :], lb[:, t, :]).then_inc(s_c, 1)
                done[0] += 1
            dve.wait_ge(s_c, done[0])
            for t in range(NT):
                dve.max_index(i8[:, t, :], m8[:, t, :], lb[:, t, :]).then_inc(s_c, 1)
                done[0] += 1
            dve.wait_ge(s_c, done[0])
            link(dve.tensor_copy(idx[:, :, :], i8[:, :, 0:2]))
            for k in range(2):
                link(dve.tensor_tensor(oh[:, k, :, :], c2.iota[:, :, 0:NE].broadcast_to(shape),
                                       idx[:, :, k:k + 1].broadcast_to(shape), ALU.is_equal))
            dve.tensor_tensor(sel[:, :, :], oh[:, 0, :, :], oh[:, 1, :, :], ALU.add).then_inc(s_sel, 1)
            dve.wait_ge(s_e, 1)
            for k in range(2):
                link(dve.tensor_tensor(ow[:, k, :, :], oh[:, k, :, :], ex[:, :, :], ALU.mult))
            link(dve.tensor_reduce(wraw[:, :, :], ow[:, :, :, :], AX_X, ALU.add))
            link(dve.tensor_tensor(tot[:, :, 0], wraw[:, 0, :], wraw[:, 1, :], ALU.add))
            link(dve.reciprocal(rt[:, :, 0], tot[:, :, 0]))
            link(dve.tensor_tensor(c2.weight[:, :, :], wraw[:, :, :],
                                   rt[:, :, 0:1].rearrange("p t o -> p o t").broadcast_to([P, 2, NT]), ALU.mult))
            dve.wait_ge(s_rank, 1)
            link(dve.tensor_reduce(cnt[:, :, 0], pc[:, 0:NT * NE].rearrange("p (t e) -> p e t", e=NE), AX_X, ALU.add))
            link(dve.tensor_tensor(more[:, :, :], cnt[:, :, :].broadcast_to([P, NE, NE]),
                                   c2.steps[:, :, :].broadcast_to([P, NE, NE]), ALU.is_gt))
            link(dve.tensor_reduce(tiles[:, :, 0], more[:, :, :], AX_X, ALU.add))
            link(dve.tensor_tensor(before[:, :, :], c2.lower[:, :, :],
                                   tiles[:, :, :].rearrange("p e o -> p o e").broadcast_to([P, NE, NE]), ALU.mult))
            link(dve.tensor_reduce(first[:, :, 0], before[:, :, :], AX_X, ALU.add))
            link(dve.tensor_scalar(base[:, :, 0], first[:, :, 0], float(P), None, ALU.mult))
            link(dve.tensor_tensor(pos[:, :, :], pr[:, 0:NT * NE].rearrange("p (t e) -> p t e", e=NE),
                                   base[:, :, :].rearrange("p e o -> p o e").broadcast_to(shape), ALU.add))
            for k in range(2):
                link(dve.tensor_tensor(op[:, k, :, :], oh[:, k, :, :], pos[:, :, :], ALU.mult))
            link(dve.tensor_reduce(slotf[:, :, :], op[:, :, :, :], AX_X, ALU.add))
            link(dve.tensor_copy(c2.slot[:, :, :], slotf[:, :, :]))
            link(dve.tensor_tensor(end[:, :, 0], first[:, :, 0], tiles[:, :, 0], ALU.add))
            link(dve.tensor_tensor(past[:, :, :], end[0:1, :, :].rearrange("p e o -> p o e").broadcast_to([1, TILES, NE]),
                                   c2.iota[0:1, :, :].rearrange("p o j -> p j o").broadcast_to([1, TILES, NE]), ALU.is_le))
            link(dve.tensor_reduce(eidf[:, :, 0], past[:, :, :], AX_X, ALU.add))
            link(dve.tensor_scalar(eidf[:, :, 0], eidf[:, :, 0], float(NE - 1), None, ALU.min))
            link(dve.tensor_tensor(eidf[:, :, 0].rearrange("p (m k) -> p m k", k=4), eidf[:, :, 0].rearrange("p (m k) -> p m k", k=4),
                                   c2.sixteens[:, :, :].broadcast_to([1, WORDS, 4]), ALU.mult))
            link(dve.tensor_reduce(half[:, :, 0], eidf[:, :, 0].rearrange("p (m k) -> p m k", k=4), AX_X, ALU.add))
            link(dve.tensor_copy(c2.experts[:, :], half[:, :, 0]))
            link(dve.tensor_scalar(upper[:, :], c2.experts[:, 1:WORDS], 16, None, ALU.logical_shift_left))
            link(dve.tensor_tensor(c2.experts[:, 0:WORDS - 1], c2.experts[:, 0:WORDS - 1], upper[:, :], ALU.bitwise_or))


def shared_expert(nc, io, tag, x, xt, c2, whi, wlo):
    with ExitStack() as es:
        c = Ctx(nc, es, tag)
        RAW = 3
        shi = [c.sb(f"shi{u}", [P, WN], F32R) for u in range(2)]
        slo = [c.sb(f"slo{u}", [P, WN], F32R) for u in range(2)]
        raw = [c.sb(f"raw{n}", [P, WN]) for n in range(RAW)]
        su, hf = c.sb("su", [P, 2, BLK]), c.sb("hf", [P, 2, BLK])
        hhi, hlo = c.sb("hhi", [P, 3, BLK], F32R), c.sb("hlo", [P, 3, BLK], F32R)
        pu = [c.ps(f"up{n}", [P, BLK]) for n in range(2)]
        pg = [c.ps(f"gate{n}", [P, BLK]) for n in range(2)]
        pd = [c.ps(f"down{n}", [P, TPB, D]) for n in range(2)]
        s_raw = [c.sem(f"raw{n}") for n in range(RAW)]
        s_whi, s_wlo = c.sem("weights_hi"), c.sem("weights_lo")
        s_ug, s_su, s_hf, s_hh, s_hl = (c.sem(n) for n in ("up_gate", "silu", "hidden", "hidden_hi", "hidden_lo"))
        s_d, s_x, s_sc = c.sem("down"), c.sem("x_added"), c.sem("scattered")
        SLOTS = 2 * NB
        EPS_ = NE // SLOTS
        LAG = 2
        block = es.enter_context(nc.Block())

        def load(sp, dst, up, down, sem):
            sp.dma_start(dst[:, 0:WC].rearrange("p (h n) -> p h n", h=DH), up.rearrange("(h p) n -> p h n", p=P)).then_inc(sem, 16)
            sp.dma_start(dst[:, WC:WN], down).then_inc(sem, 16)

        @block.sync
        def _(sp):
            for n in range(NU):
                if n >= RAW:
                    sp.wait_ge(s_wlo, n - RAW + 1)
                load(sp, raw[n % RAW], io["Wup"][(n - 2) % NU], io["Wdn"][(n - 2) % NU], s_raw[n % RAW])

        @block.gpsimd
        def _(pool):
            for t in range(NT):
                for k in range(2):
                    pool.indirect_dma_start(c2.rows_in, bass.IndirectOffsetOnAxis(ap=c2.slot[:, k, t:t + 1], axis=0),
                                            c2.xn[:, t, :], None).then_inc(s_sc, 16)
            pool.wait_ge(s_sc, 16 * 2 * NT)

        @block.tensor
        def _(pe):
            def up(k):
                u, tb = k // NB, k % NB
                if tb == 0:
                    pe.wait_ge(s_whi, u + 1)
                    pe.wait_ge(s_wlo, u + 1)
                if k >= 2:
                    pe.wait_ge(s_hf, k - 1)
                for p_, off in ((pu, 0), (pg, ED)):
                    for h in range(DH):
                        mm = products(pe, p_[k % 2][:, :], [a[:, h * 2 * ED + off:h * 2 * ED + off + ED] for a in (shi[u], slo[u])],
                                      [a[:, h, tb * BLK:(tb + 1) * BLK] for a in xt], h == 0, h == DH - 1)
                mm.then_inc(s_ug, 1)

            def down(k):
                pe.wait_ge(s_hh, k + 1)
                pe.wait_ge(s_hl, k + 1)
                if k >= 2:
                    pe.wait_ge(s_x, k - 1)
                for j in range(TPB):
                    mm = products(pe, pd[k % 2][:, j, :], [a[:, k % 3, j * P:(j + 1) * P] for a in (hhi, hlo)],
                                  [a[:, WC:WN] for a in (shi[k // NB], slo[k // NB])], True, True)
                mm.then_inc(s_d, 1)

            for k in range(SLOTS + LAG):
                if k < SLOTS:
                    up(k)
                if k >= LAG:
                    down(k - LAG)

        @block.scalar
        def _(act):
            def split(n, dst):
                act.wait_ge(s_raw[n % RAW], 32 * (n // RAW + 1))
                act.activation(dst, raw[n % RAW][:, :], ACT.Copy).then_inc(s_whi, 1)

            for u in range(2):
                split(u, shi[u][:, :])
            for k in range(SLOTS):
                act.wait_ge(s_ug, k + 1)
                act.activation(su[:, k % 2, :], pu[k % 2][:, :], ACT.Silu).then_inc(s_su, 1)
                for e in range(EPS_ * k, EPS_ * (k + 1)):
                    split(e + 2, whi[:, e, :])
                    if e == EPS_ * k:
                        act.wait_ge(s_hf, k + 1)
                        act.activation(hhi[:, k % 3, :], hf[:, k % 2, :], ACT.Copy).then_inc(s_hh, 1)

        @block.vector
        def _(dve):
            def add(k):
                tb = k % NB
                dve.wait_ge(s_d, k + 1)
                xb = x[:, tb * TPB:(tb + 1) * TPB, :]
                dve.tensor_tensor(xb, pd[k % 2][:, :, :], xb, ALU.add).then_inc(s_x, 1)

            def split(n, dst, hi):
                dve.wait_ge(s_whi, n + 1)
                dve.tensor_tensor(dst, raw[n % RAW][:, :], hi.bitcast(F32), ALU.subtract).then_inc(s_wlo, 1)

            for u in range(2):
                split(u, slo[u][:, :], shi[u][:, :])
            for k in range(SLOTS):
                dve.wait_ge(s_su, k + 1)
                dve.tensor_tensor(hf[:, k % 2, :], su[:, k % 2, :], pg[k % 2][:, :], ALU.mult).then_inc(s_hf, 1)
                dve.wait_ge(s_hh, k + 1)
                dve.tensor_tensor(hlo[:, k % 3, :], hf[:, k % 2, :], hhi[:, k % 3, :].bitcast(F32), ALU.subtract).then_inc(s_hl, 1)
                for e in range(EPS_ * k, EPS_ * (k + 1)):
                    split(e + 2, wlo[:, e, :], whi[:, e, :])
                if k >= LAG:
                    add(k - LAG)
            for k in range(SLOTS - LAG, SLOTS):
                add(k)


def routed_experts(nc, tag, x, c2, ident, whi, wlo):
    RING = 4
    PAIRS = TILES // 2
    LOOPS = (PAIRS - 4) // RING
    AHEAD = 3
    with ExitStack() as es:
        c = Ctx(nc, es, tag)
        xg = [c.sb(f"xg{n}", [P, 2, D]) for n in range(RING)]
        xhi, xlo = c.sb("xhi", [P, 2, 2 * DH, P], F32R), c.sb("xlo", [P, 2, 2 * DH, P], F32R)
        su, hf = c.sb("su", [P, 2, 2, ED]), c.sb("hf", [P, 2, 2, ED])
        hhi, hlo = c.sb("hhi", [P, 2, 2, P], F32R), c.sb("hlo", [P, 2, 2, P], F32R)
        ys = [c.sb(f"ys{n}", [P, 2, D]) for n in range(RING)]
        yg = [c.sb(f"yg{n}", [P, 2, D]) for n in range(RING)]
        pa, pb, pd = ([c.ps(f"{m}{n}", [P, 2, 2 * ED]) for n in range(2)] for m in ("rowsT", "upgate", "down"))
        pc = [c.ps(f"hiddenT{n}", [P, 2 * P]) for n in range(2)]
        s_xg = [c.sem(f"rows_loaded{n}") for n in range(RING)]
        s_st = [c.sem(f"rows_stored{n}") for n in range(RING)]
        s_yg = [c.sem(f"rows_gathered{n}") for n in range(RING)]
        s_a, s_b, s_c, s_d = (c.sem(n) for n in ("rows_transposed", "up_gate", "hidden_transposed", "down"))
        s_xh, s_xl, s_su, s_h, s_hh, s_hl, s_ev = (
            c.sem(n) for n in ("rows_hi", "rows_lo", "silu", "hidden", "hidden_hi", "hidden_lo", "down_copied"))
        s_x = c.sem("x_added")
        rows_in, rows_out = (r.rearrange("(n t p) d -> n p t d", t=2, p=P) for r in (c2.rows_in, c2.rows_out))
        block = es.enter_context(nc.Block())

        def slots(eng, slot):
            for j in range(-2, 1):
                slot(j, j % RING)
            with eng.Fori(0, LOOPS) as i:
                for r in range(1, RING + 1):
                    slot(RING * i + r, r % RING, i)
            for j in range(RING * LOOPS + 1, PAIRS + 1):
                slot(j, j % RING)

        def there(j):
            return type(j) is not int or 0 <= j < PAIRS

        @block.sync
        def _(sp):
            def slot(j, r):
                if there(j + 5):
                    sp.wait_ge(s_a, j + 2)
                    sp.dma_start(xg[(r + 1) % RING][:, :, :], rows_in[j + 5]).then_inc(s_xg[(r + 1) % RING], 16)
                if there(j - 1):
                    sp.wait_ge(s_ev, j + AHEAD)
                    sp.dma_start(rows_out[j - 1], ys[(r - 1) % RING][:, :, :]).then_inc(s_st[(r - 1) % RING], 16)

            for j in range(RING):
                sp.dma_start(xg[j][:, :, :], rows_in[j]).then_inc(s_xg[j], 16)
            slot(-1, 3)
            slot(0, 0)
            with sp.Fori(0, LOOPS - 1) as i:
                for r in range(1, RING + 1):
                    slot(RING * i + r, r % RING)
            for j in range(RING * (LOOPS - 1) + 1, PAIRS + 1):
                slot(j, j % RING)

        @block.tensor
        def _(pe):
            word = [None]

            def expert_of(k):
                return (word[0] >> (4 * k)) & (NE - 1)

            def slot(j, r, i=None):
                if j == -1 if i is None and j < 1 else r % 2:
                    m = max(j - 1, 0) // 2 if i is None else 2 * i + (r - 1) // 2
                    word[0] = pe.value_load(c2.experts[0:1, bass.ds(m, 1)])
                back = 1 - r % 2 if i is not None or j > 0 else j - 1
                if there(j + 2):
                    n, w = (r + 2) % RING, r % 2
                    pe.wait_ge(s_xg[n], 16 * ((j + 2) // RING + 1) if i is None else 16 * (i + ((r or RING) + 2) // RING + 1))
                    pe.wait_ge(s_xl, j + 1 + AHEAD)
                    for q in range(2):
                        for h in range(DH):
                            mm = pe.transpose(pa[w][:, q, h * P:(h + 1) * P], xg[n][:, q, h * P:(h + 1) * P], ident[:, :])
                    mm.then_inc(s_a, 1)
                if there(j + 1):
                    w = (r + 1) % 2
                    e = [expert_of(2 * (back + 2) + q) for q in range(2)]
                    pe.wait_ge(s_xh, j + 2)
                    pe.wait_ge(s_xl, j + 2 + AHEAD)
                    pe.wait_ge(s_h, j + AHEAD)
                    for q in range(2):
                        for h in range(DH):
                            mm = products(pe, pb[w][:, q, :], [a[:, w, q * DH + h, :] for a in (xhi, xlo)],
                                          [a[:, bass.ds(e[q], 1), h * 2 * ED:(h + 1) * 2 * ED] for a in (whi, wlo)],
                                          h == 0, h == DH - 1)
                    mm.then_inc(s_b, 1)
                if there(j):
                    w = r % 2
                    pe.wait_ge(s_h, j + 1 + AHEAD)
                    pe.wait_ge(s_hl, j - 1 + AHEAD)
                    for q in range(2):
                        mm = pe.transpose(pc[w][:, q * P:(q + 1) * P], hf[:, w, q, :], ident[:, :])
                    mm.then_inc(s_c, 1)
                if there(j - 1):
                    w = (r - 1) % 2
                    e = [expert_of(2 * back + q) for q in range(2)]
                    pe.wait_ge(s_hh, j)
                    pe.wait_ge(s_hl, j + AHEAD)
                    pe.wait_ge(s_ev, j - 2 + AHEAD)
                    for q in range(2):
                        mm = products(pe, pd[w][:, q, :], [a[:, w, q, :] for a in (hhi, hlo)],
                                      [a[:, bass.ds(e[q], 1), WC:WN] for a in (whi, wlo)], True, True)
                    mm.then_inc(s_d, 1)

            slots(pe, slot)

        @block.scalar
        def _(act):
            def slot(j, r, i=None):
                if there(j + 2):
                    w = r % 2
                    act.wait_ge(s_a, j + 3)
                    act.activation(xhi[:, w, :, :], pa[w][:, :, :].rearrange("p q (h n) -> p (q h) n", n=P), ACT.Copy).then_inc(s_xh, 1)
                if there(j + 1):
                    w = (r + 1) % 2
                    act.wait_ge(s_b, j + 2)
                    act.activation(su[:, w, :, :], pb[w][:, :, 0:ED], ACT.Silu).then_inc(s_su, 1)
                if there(j):
                    w = r % 2
                    act.wait_ge(s_c, j + 1)
                    act.activation(hhi[:, w, :, :], pc[w][:, :].rearrange("p (q n) -> p q n", q=2), ACT.Copy).then_inc(s_hh, 1)
                if there(j - 1):
                    w, n = (r - 1) % 2, (r - 1) % RING
                    act.wait_ge(s_d, j)
                    act.wait_ge(s_st[n], 16 * ((j - 1) // RING + 1) if i is None else 16 * (i + 1))
                    act.activation(ys[n][:, :, :], pd[w][:, :, :], ACT.Copy).then_inc(s_ev, 1)

            act.sem_inc(s_ev, AHEAD)
            for s_ in s_st:
                act.sem_inc(s_, 16)
            slots(act, slot)

        @block.vector
        def _(dve):
            def slot(j, r, i=None):
                if there(j + 2):
                    w = r % 2
                    dve.wait_ge(s_xh, j + 3)
                    dve.tensor_tensor(xlo[:, w, :, :], pa[w][:, :, :].rearrange("p q (h n) -> p (q h) n", n=P),
                                      xhi[:, w, :, :].bitcast(F32), ALU.subtract).then_inc(s_xl, 1)
                if there(j + 1):
                    w = (r + 1) % 2
                    dve.wait_ge(s_su, j + 2)
                    dve.tensor_tensor(hf[:, w, :, :], su[:, w, :, :], pb[w][:, :, ED:2 * ED], ALU.mult).then_inc(s_h, 1)
                if there(j):
                    w = r % 2
                    dve.wait_ge(s_hh, j + 1)
                    dve.tensor_tensor(hlo[:, w, :, :], pc[w][:, :].rearrange("p (q n) -> p q n", q=2),
                                      hhi[:, w, :, :].bitcast(F32), ALU.subtract).then_inc(s_hl, 1)

            for s_ in (s_xl, s_h, s_hl):
                dve.sem_inc(s_, AHEAD)
            slots(dve, slot)
            for t in range(NT):
                dve.wait_ge(s_yg[t % RING], 32 * (t // RING + 1))
                for k in range(2):
                    dve.scalar_tensor_tensor(out=x[:, t, :], in0=yg[t % RING][:, k, :], scalar=c2.weight[:, k, t:t + 1],
                                             in1=x[:, t, :], op0=ALU.mult, op1=ALU.add).then_inc(s_x, 1)
                    dve.wait_ge(s_x, 2 * t + k + 1)

        @block.gpsimd
        def _(pool):
            for n in range(RING):
                pool.wait_ge(s_st[n], 16 * (PAIRS // RING + 1))
            for t in range(NT):
                if t >= RING:
                    pool.wait_ge(s_x, 2 * (t - RING + 1))
                for k in range(2):
                    pool.indirect_dma_start(yg[t % RING][:, k, :], None, c2.rows_out,
                                            bass.IndirectOffsetOnAxis(ap=c2.slot[:, k, t:t + 1], axis=0)).then_inc(s_yg[t % RING], 16)


class Routing:
    pass


def mixture(nc, io, tag, x, xt, ident, c2):
    with ExitStack() as es:
        c = Ctx(nc, es, tag)
        c2.xn = c.sb("xn", [P, NT, D])
        c2.slot = c.sb("slot", [P, 2, NT], U32)
        c2.weight = c.sb("weight", [P, 2, NT])
        c2.experts = c.sb("experts", [1, WORDS], I32)
        whi, wlo = c.sb("whi", [P, NE, WN], F32R), c.sb("wlo", [P, NE, WN], F32R)
        normalise(nc, tag + "n", x, ident, xt, c2.xn)
        route(nc, io, tag + "r", xt, c2)
        shared_expert(nc, io, tag + "s", x, xt, c2, whi, wlo)
        routed_experts(nc, tag + "e", x, c2, ident, whi, wlo)


def retain(nc, io, x, xt, ident):
    G = 2
    H4 = HB // G
    W3 = QK + 2 * DVT
    with ExitStack() as es:
        c = Ctx(nc, es, "rt")
        wst = c.sb("wst", [P, DH, W3])
        whi = c.sb("whi", [P, DH, W3], F32R)
        wlo = c.sb("wlo", [P, DH, W3], F32R)
        wo = c.sb("wo", [P, DVT // P, D])
        xs = [[c.sb(f"xs{w}{k}", [P, DH, P], F32R) for k in range(2)] for w in range(2)]
        cos = c.sb("cos", [P, NT, DK])
        sin = c.sb("sin", [P, NT, DK])
        dec = c.sb("dec", [P, 2 * HB, 1])
        mask = c.sb("mask", [P, 1, P])
        bd = c.sb("bd", [P, 1, H4, 1])
        gdec = c.sb("gdec", [P, G, NT])
        gw = c.sb("gw", [P, 1, DV])
        nhalf = c.sb("nhalf", [P, HB, 1])
        ra, rb, rr = (c.sb(n, [P, 2 * HB, DK]) for n in ("ra", "rb", "rr"))
        qk = c.sb("qk", [P, 2, QK])
        v = c.sb("v", [P, 2, DVT])
        sg = c.sb("sg", [P, HB, DV])
        gate = c.sb("gate", [P, 2, HB, DV])
        qkT = c.sb("qkT", [P, 2 * G, P])
        qbd = c.sb("qbd", [P, G, H4, P])
        sc = c.sb("sc", [P, G, H4, P])
        st, sm, sa = (c.sb(n, [P, G, H4, DV]) for n in ("st", "sm", "sa"))
        sq, on = (c.sb(n, [P, HB, DV]) for n in ("sq", "on"))
        ms, mv, rs = (c.sb(n, [P, HB, 1]) for n in ("ms", "mv", "rs"))
        og = c.sb("og", [P, DVT])
        oT = c.sb("oT", [P, DVT // P, P])
        p_qk, p_v, p_g, p_t, p_o, p_y = (c.ps("p_" + n, [P, BLK]) for n in ("qk", "v", "g", "t", "o", "y"))
        p_s = [c.ps(f"p_s{g}", [P, BLK]) for g in range(G)]
        s_w, s_whi, s_wlo, s_const, s_zero, s_half = (c.sem(n) for n in ("w", "whi", "wlo", "const", "zero", "half"))
        s_xs = [c.sem(f"x_staged{w}") for w in range(2)]
        s_qk, s_v, s_g, s_o, s_st, s_y = (c.sem("mm_" + n) for n in ("qk", "v", "g", "o", "state", "y"))
        s_s = [c.sem(f"mm_scores{g}") for g in range(G)]
        s_tr, s_ot = c.sem("qk_transposed"), c.sem("o_transposed")
        s_rope, s_sum, s_dk, s_gate = (c.sem(n) for n in ("rope_products", "rope_sum", "qk_decayed", "gate"))
        s_vc, s_sg, s_tc, s_bd, s_otc = (c.sem(n) for n in ("v_copied", "silu", "qkT_copied", "q_block_diag", "oT_copied"))
        s_sc = [c.sem(f"scores_masked{g}") for g in range(G)]
        s_sm, s_sa, s_state = c.sem("update_masked"), c.sem("state_sum"), c.sem("state_ready")
        s_sq, s_ms, s_mv, s_rs, s_on, s_og, s_x = (c.sem(n) for n in ("sq", "ms", "mv", "rs", "on", "og", "x"))
        CONSTS = 8
        block = es.enter_context(nc.Block())

        def wait(eng, sem, value):
            if type(value) is not int or value > 0:
                eng.wait_ge(sem, value)

        def slots(eng, slot):
            slot(-1, 1, False, False, True, 1)
            slot(0, 0, False, True, True, 1)
            with eng.Fori(0, NT // 2 - 1) as i:
                slot(2 * i + 1, 1, True, True, True, i + 2)
                slot(2 * i + 2, 0, True, True, True, i + 2)
            slot(NT - 1, 1, True, True, False, None)
            slot(NT, 0, True, False, False, None)

        @block.sync
        def _(sp):
            def stage(t, w):
                for k in range(2):
                    sp.dma_start(xs[w][k][:, :, :].bitcast(F32), xt[k][:, :, :].bitcast(F32).rearrange("p h (t n) -> p t h n", n=P)[:, t, :, :]
                                 ).then_inc(s_xs[w], 16)

            sp.dma_start(wst[:, :, :], io["Wret"].rearrange("(h p) n -> p h n", p=P)).then_inc(s_w, 16)
            stage(0, 0)
            stage(1, 1)
            for dst, src in ((wo[:, :, :], io["WoB"].rearrange("(c p) n -> p c n", p=P)),
                             (cos[:, :, :], io["cos"]), (sin[:, :, :], io["sin"]),
                             (dec[:, :, 0], io["dec"]), (mask[:, 0, :], io["mask"]), (bd[:, 0, :, 0], io["bd"]),
                             (gdec[:, :, :], io["gdec"]),
                             (gw[:, 0, :], io["gnw"].rearrange("(o n) -> o n", o=1).broadcast_to([P, DV]))):
                sp.dma_start(dst, src).then_inc(s_const, 16)
            with sp.Fori(0, NT // 2 - 1) as i:
                for w in range(2):
                    sp.wait_ge(s_g, 2 * i + w + 1)
                    stage(2 * i + w + 2, w)

        @block.tensor
        def _(pe):
            def project(t, i, w):
                pe.wait_ge(s_xs[w], 32 * i)
                for out, col, width, sem, freed in ((p_qk, 0, QK, s_qk, s_rope), (p_v, QK, DVT, s_v, s_vc),
                                                    (p_g, QK + DVT, DVT, s_g, s_sg)):
                    wait(pe, freed, t)
                    for h in range(DH):
                        mm = products(pe, out[:, :], [a[:, h, :] for a in xs[w]],
                                      [a[:, h, col:col + width] for a in (whi, wlo)], h == 0, h == DH - 1)
                    mm.then_inc(sem, 1)

            def slot(t, w, prev, cur, nxt, staged):
                if cur:
                    pe.wait_ge(s_dk, t + 1)
                    wait(pe, s_sm, t)
                    for g in range(2 * G):
                        mm = pe.transpose(p_t[:, g * P:(g + 1) * P], qk[:, w, g * P:(g + 1) * P], ident[:, :])
                    mm.then_inc(s_tr, 1)
                if nxt:
                    project(t + 1, staged, 1 - w)
                if prev:
                    pe.wait_ge(s_og, t)
                    wait(pe, s_x, t)
                    for g in range(DVT // P):
                        mm = pe.transpose(p_y[:, g * P:(g + 1) * P], og[:, g * P:(g + 1) * P], ident[:, :])
                    mm.then_inc(s_ot, 1)
                if cur:
                    pe.wait_ge(s_tc, t + 1)
                    pe.wait_ge(s_bd, t + 1)
                    for g in range(G):
                        wait(pe, s_sc[g], t)
                        pe.matmul(p_s[g][:, :], qkT[:, G + g, :], qbd[:, g, :, :], start=True, stop=True).then_inc(s_s[g], 1)
                if prev:
                    pe.wait_ge(s_otc, t)
                    for g in range(DVT // P):
                        mm = pe.matmul(p_y[:, 0:D], oT[:, g, :], wo[:, g, :], start=(g == 0), stop=(g == DVT // P - 1))
                    mm.then_inc(s_y, 1)
                if cur:
                    pe.wait_ge(s_vc, t + 1)
                    for g in range(G):
                        mm = pe.matmul(p_t[:, g * H4 * DV:(g + 1) * H4 * DV], qk[:, w, (G + g) * P:(G + g + 1) * P],
                                       v[:, w, g * H4 * DV:(g + 1) * H4 * DV], start=True, stop=True)
                    mm.then_inc(s_st, 1)
                    pe.wait_ge(s_state, t + 1)
                    pe.wait_ge(s_on, t + 1)
                    for g in range(G):
                        pe.matmul(p_o[:, g * H4 * DV:(g + 1) * H4 * DV], qkT[:, g, :], st[:, g, :, :],
                                  start=(g == 0), stop=False, skip_group_check=True)
                    for g in range(G):
                        pe.wait_ge(s_sc[g], t + 1)
                        for h in range(H4):
                            n = g * H4 + h
                            mm = pe.matmul(p_o[:, n * DV:(n + 1) * DV], sc[:, g, h, :], v[:, w, n * DV:(n + 1) * DV],
                                           start=False, stop=(n == HB - 1), skip_group_check=True)
                    mm.then_inc(s_o, 1)

            pe.wait_ge(s_whi, 1)
            pe.wait_ge(s_wlo, 1)
            pe.sem_inc(s_ot, 1)
            slots(pe, slot)

        @block.scalar
        def _(act):
            def slot(t, w, prev, cur, nxt, staged):
                if prev:
                    act.wait_ge(s_o, t)
                    wait(act, s_ms, t)
                    act.activation(sq[:, :, :], p_o[:, :].rearrange("p (h v) -> p h v", v=DV), ACT.Square).then_inc(s_sq, 1)
                if cur:
                    act.wait_ge(s_tr, t + 1)
                    act.activation(qkT[:, :, :], p_t[:, :].rearrange("p (g n) -> p g n", n=P), ACT.Copy).then_inc(s_tc, 1)
                    for h in range(H4):
                        rows = slice(h * DK, (h + 1) * DK)
                        ins = act.activation(qbd[rows, :, h, :], p_t[rows, 0:G * P].rearrange("p (g n) -> p g n", n=P), ACT.Copy)
                    ins.then_inc(s_bd, 1)
                if nxt:
                    act.wait_ge(s_v, t + 2)
                    act.activation(v[:, 1 - w, :], p_v[:, :], ACT.Copy).then_inc(s_vc, 1)
                    act.wait_ge(s_g, t + 2)
                    wait(act, s_gate, t + 1)
                    act.activation(sg[:, :, :], p_g[:, :].rearrange("p (h v) -> p h v", v=DV), ACT.Silu).then_inc(s_sg, 1)
                if prev:
                    act.wait_ge(s_ot, t + 1)
                    act.activation(oT[:, :, :], p_y[:, :].rearrange("p (g n) -> p g n", n=P), ACT.Copy).then_inc(s_otc, 1)

            act.wait_ge(s_w, 16)
            act.activation(whi[:, :, :], wst[:, :, :], ACT.Copy).then_inc(s_whi, 1)
            act.wait_ge(s_zero, 1)
            slots(act, slot)

        @block.gpsimd
        def _(pool):
            def slot(t, w, prev, cur, nxt, staged):
                if prev:
                    pool.wait_ge(s_mv, t)
                    wait(pool, s_on, t)
                    pool.tensor_tensor(rs[:, :, :], mv[:, :, :], nhalf[:, :, :], ALU.pow).then_inc(s_rs, 1)
                if nxt:
                    pool.wait_ge(s_rope, t + 2)
                    pool.tensor_tensor(rr[:, :, :], ra[:, :, :], rb[:, :, :], ALU.add).then_inc(s_sum, 1)
                    pool.wait_ge(s_sum, t + 2)
                    wait(pool, s_st, t)
                    pool.tensor_tensor(qk[:, 1 - w, :].rearrange("p (h n) -> p h n", n=DK), rr[:, :, :],
                                       dec[:, :, :].broadcast_to([P, 2 * HB, DK]), ALU.mult).then_inc(s_dk, 1)
                    pool.wait_ge(s_sg, t + 2)
                    wait(pool, s_og, t)
                    pool.tensor_tensor(gate[:, 1 - w, :, :], sg[:, :, :], gw[:, :, :].broadcast_to([P, HB, DV]),
                                       ALU.mult).then_inc(s_gate, 1)

            pool.wait_ge(s_const, 16 * CONSTS)
            pool.memset(nhalf[:, :, :], -0.5).then_inc(s_half, 1)
            pool.wait_ge(s_half, 1)
            pool.sem_inc(s_rs, 1)
            slots(pool, slot)

        @block.vector
        def _(dve):
            def slot(t, w, prev, cur, nxt, staged):
                if prev:
                    dve.wait_ge(s_sq, t)
                    dve.tensor_reduce(ms[:, :, :], sq[:, :, :], AX_X, ALU.add).then_inc(s_ms, 1)
                    dve.wait_ge(s_ms, t + 1)
                    wait(dve, s_rs, t)
                    dve.tensor_scalar(mv[:, :, :], ms[:, :, :], 1.0 / DV, EPS, ALU.mult, ALU.add).then_inc(s_mv, 1)
                    dve.wait_ge(s_rs, t + 1)
                    dve.tensor_tensor(on[:, :, :], p_o[:, :].rearrange("p (h v) -> p h v", v=DV),
                                      rs[:, :, :].broadcast_to([P, HB, DV]), ALU.mult).then_inc(s_on, 1)
                    dve.wait_ge(s_on, t + 1)
                    dve.wait_ge(s_gate, t)
                    wait(dve, s_ot, t)
                    dve.tensor_tensor(og[:, :].rearrange("p (h v) -> p h v", v=DV), on[:, :, :], gate[:, 1 - w, :, :],
                                      ALU.mult).then_inc(s_og, 1)
                if nxt:
                    q = p_qk[:, :].rearrange("p (h n) -> p h n", n=DK)
                    dve.wait_ge(s_qk, t + 2)
                    wait(dve, s_sum, t + 1)
                    dve.tensor_tensor(ra[:, :, :], q, cos[:, bass.ds(t + 1, 1), :].broadcast_to([P, 2 * HB, DK]), ALU.mult)
                    for a in range(2):
                        lo, hi = a * DK // 2, (a + 1) * DK // 2
                        ins = dve.tensor_tensor(rb[:, :, lo:hi], q[:, :, DK // 2 - lo:DK - lo],
                                                sin[:, bass.ds(t + 1, 1), lo:hi].broadcast_to([P, 2 * HB, DK // 2]), ALU.mult)
                    ins.then_inc(s_rope, 1)
                if cur:
                    wait(dve, s_o, t)
                    for g in range(G):
                        dve.wait_ge(s_s[g], t + 1)
                        dve.tensor_tensor(sc[:, g, :, :], p_s[g][:, :].rearrange("p (h n) -> p h n", n=P),
                                          mask[:, :, :].broadcast_to([P, H4, P]), ALU.mult).then_inc(s_sc[g], 1)
                if prev:
                    dve.wait_ge(s_y, t)
                    xv = x[:, t - 1, :]
                    dve.tensor_tensor(xv, p_y[:, 0:D], xv, ALU.add).then_inc(s_x, 1)
                if cur:
                    dve.wait_ge(s_st, t + 1)
                    dve.tensor_tensor(sm[:, :, :, :], p_t[:, :].rearrange("p (g h v) -> p g h v", g=G, h=H4),
                                      bd[:, :, :, :].broadcast_to([P, G, H4, DV]), ALU.mult).then_inc(s_sm, 1)
                    dve.wait_ge(s_sm, t + 1)
                    dve.wait_ge(s_state, t + 1)
                    dve.tensor_tensor(sa[:, :, :, :], st[:, :, :, :], sm[:, :, :, :], ALU.add).then_inc(s_sa, 1)
                    dve.wait_ge(s_sa, t + 1)
                    dve.wait_ge(s_o, t + 1)
                    for g in range(G):
                        ins = dve.tensor_scalar(st[:, g, :, :], sa[:, g, :, :], gdec[:, g, bass.ds(t, 1)], None, ALU.mult)
                    ins.then_inc(s_state, 1)

            dve.memset(qbd[:, :, :, :], 0.0).then_inc(s_zero, 1)
            dve.memset(st[:, :, :, :], 0.0).then_inc(s_state, 1)
            dve.wait_ge(s_whi, 1)
            dve.tensor_tensor(wlo[:, :, :], wst[:, :, :], whi[:, :, :].bitcast(F32), ALU.subtract).then_inc(s_wlo, 1)
            dve.wait_ge(s_const, 16 * CONSTS)
            for sem in (s_x, s_ms, s_on):
                dve.sem_inc(sem, 1)
            slots(dve, slot)


def build(nc, io, out, stages=4):
    Ctx.semaphores = []
    with ExitStack() as es:
        c = Ctx(nc, es, "g")
        x = c.sb("x", [P, NT, D])
        xt = [c.sb(n, [P, DH, N], F32R) for n in ("xt_hi", "xt_lo")]
        ident = c.sb("ident", [P, P])
        identb = c.sb("identb", [P, P], BF16)
        c2 = Routing()
        c2.rbias = c.sb("rbias", [P, 1, NE])
        c2.iota = c.sb("iota", [P, 1, TILES])
        c2.sixteens = c.sb("sixteens", [1, 1, 4])
        c2.steps = c.sb("steps", [P, 1, NE])
        c2.lower = c.sb("lower", [P, NE, NE])
        tri = c.sb("tri", [P, P])
        c2.trib = c.sb("trib", [P, P], BF16)
        c2.onesb = c.sb("onesb", [P, P], BF16)
        rows = [nc.dram_tensor(f"rows_{n}", [TILES * P, D], F32, kind="Internal").ap() for n in ("in", "out")]
        c2.rows_in, c2.rows_out = rows
        s_in, s_id = c.sem("inputs"), c.sem("ident")
        INPUTS = NB + 7

        def bcast(ap, n):
            return ap.rearrange("(o n) -> o n", o=1).broadcast_to([P, n])

        with nc.Block() as block:
            @block.sync
            def _(sp):
                xv = io["x"].rearrange("b (t p) d -> p (b t) d", p=P)
                for b in range(NB):
                    sp.dma_start(x[:, b * TPB:(b + 1) * TPB, :], xv[:, b * TPB:(b + 1) * TPB, :]).then_inc(s_in, 16)
                sp.dma_start(ident[:, :], io["ident"]).then_inc(s_in, 16)
                for dst, src, n in ((c2.rbias[:, 0, :], io["rbias"], NE), (c2.iota[:, 0, :], io["iota"], TILES),
                                    (c2.steps[:, 0, :], io["steps"], NE),
                                    (c2.lower[:, :, :].rearrange("p a b -> p (a b)"), io["lower"], NE * NE)):
                    sp.dma_start(dst, bcast(src, n)).then_inc(s_in, 16)
                sp.dma_start(tri[:, :], io["tri"]).then_inc(s_in, 16)
                sp.dma_start(c2.sixteens[:, 0, :], io["sixteens"].rearrange("(o n) -> o n", o=1)).then_inc(s_in, 16)
                sp.wait_ge(s_in, 16 * INPUTS)

            @block.vector
            def _(dve):
                dve.memset(c2.onesb[:, :], 1.0).then_inc(s_id, 1)
                dve.wait_ge(s_in, 16 * INPUTS)
                dve.tensor_copy(c2.trib[:, :], tri[:, :]).then_inc(s_id, 1)
                dve.tensor_copy(identb[:, :], ident[:, :]).then_inc(s_id, 1)

        normalise(nc, "n1", x, ident, xt)
        with ExitStack() as es2:
            a = Ctx(nc, es2, "a")
            wo = a.sb("wo", [P, DH, D])
            oall = a.sb("oall", [P, B * DH, 2, 2, BLK])
            vb, bo = a.sb("vb", [P, D]), a.sb("bo", [P, D])
            vaug = a.sb("vaug", [P, B, DH, KT, HA // DH, 2 * HDA])
            scratch = nc.dram_tensor("qk_parts", [2, 3, B * DH, 2, HPG, HDA, L], BF16, kind="Internal").ap()
            zeros = a.sb("zeros", [P, 2 * D])
            s_b, s_one, s_zero, s_rows = a.sem("biases"), a.sem("ones"), a.sem("zeros"), a.sem("rows_zeroed")
            with nc.Block() as block:
                @block.sync
                def _(sp):
                    sp.dma_start(vb[:, :], bcast(io["bias"][2], D)).then_inc(s_b, 16)
                    sp.dma_start(bo[:, :], bcast(io["bias"][3], D)).then_inc(s_b, 16)
                    sp.wait_ge(s_b, 32)
                    sp.wait_ge(s_zero, 1)
                    for n in range(TILES // 2):
                        sp.dma_start(c2.rows_in.rearrange("(n p a) d -> n p (a d)", p=P, a=2)[n], zeros[:, :]).then_inc(s_rows, 16)

                @block.vector
                def _(dve):
                    dve.memset(zeros[:, :], 0.0).then_inc(s_zero, 1)

                @block.gpsimd
                def _(pool):
                    pool.memset(vaug[:, :, :, :, :, HDA:2 * HDA].rearrange("p b a k h r -> p (b a k h) r"), 1.0).then_inc(s_one, 1)
            project_qkv(nc, io, x, xt, scratch, vaug, vb, bo, wo)
            attend(nc, scratch, vaug, oall, identb)
            project_out(nc, x, oall, wo, ident)
            with nc.Block() as block:
                @block.gpsimd
                def _(pool):
                    pool.wait_ge(s_rows, 16 * (TILES // 2))
        if stages >= 2:
            mixture(nc, io, "m2", x, xt, ident, c2)
        clear_semaphores(nc)
        if stages >= 3:
            normalise(nc, "n3", x, ident, xt)
            retain(nc, io, x, xt, ident)
        if stages >= 4:
            mixture(nc, io, "m4", x, xt, ident, c2)
        s_out = c.sem("stored")
        with nc.Block() as block:
            @block.sync
            def _(sp):
                ov = out.rearrange("b (t p) d -> p (b t) d", p=P)
                for b in range(NB):
                    sp.dma_start(ov[:, b * TPB:(b + 1) * TPB, :], x[:, b * TPB:(b + 1) * TPB, :]).then_inc(s_out, 16)
                sp.wait_ge(s_out, 16 * NB)


def constants():
    gamma = 1.0 - np.exp2(-5.0 - np.arange(HB, dtype=np.float64))
    inv = 1.0 / 10000.0 ** (np.arange(0, DK, 2, dtype=np.float64) / DK)
    f = np.arange(L, dtype=np.float64)[:, None] * inv[None, :]
    i = np.arange(P, dtype=np.float64)[:, None]
    f4 = np.float32

    def tiles(a):
        return np.tile(a.reshape(KT, P, -1).transpose(1, 0, 2), (1, B, 1))

    gdec = np.zeros((P, 2, NT))
    for g in range(2):
        gdec[:, g, :] = (gamma[g * 4 + np.arange(P) // 32] ** P)[:, None]
    gdec[:, :, KT - 1::KT] = 0.0
    return {
        "cos": tiles(np.concatenate([np.cos(f), np.cos(f)], 1)).astype(f4),
        "sin": tiles(np.concatenate([-np.sin(f), np.sin(f)], 1)).astype(f4),
        "dec": np.concatenate([gamma ** i * DK ** -0.5, gamma ** -i], 1).astype(f4),
        "mask": (np.arange(P)[None, :] >= np.arange(P)[:, None]).astype(f4),
        "bd": (np.arange(P)[:, None] // 32 == np.arange(4)[None, :]).astype(f4),
        "gdec": gdec.astype(f4),
        "ident": np.eye(P, dtype=f4),
        "iota": np.arange(TILES, dtype=f4),
        "sixteens": (16.0 ** np.arange(4)).astype(f4),
        "steps": (P * np.arange(NE)).astype(f4),
        "lower": (np.arange(NE)[None, :] < np.arange(NE)[:, None]).astype(f4).reshape(-1),
        "tri": (np.arange(P)[:, None] < np.arange(P)[None, :]).astype(f4),
    }


def lay_out(i):
    g = {k.replace("L0_", ""): np.asarray(v) for k, v in i.items()}
    a = lambda n: [g[f"attn_a_{n}{m}"] for m in "qkvo"]
    sh = [g["ffn_Su"][0], g["ffn_Sg"][0], g["ffn_Sd"][0]]
    up = np.concatenate([np.stack([g["ffn_Wu"], g["ffn_Wg"]], 2).reshape(NE, D, 2 * ED),
                         np.stack([np.concatenate([sh[0][:, k * ED:(k + 1) * ED], sh[1][:, k * ED:(k + 1) * ED]], 1)
                                   for k in range(2)])], 0)
    dn = np.concatenate([g["ffn_Wd"], sh[2].reshape(2, ED, D)], 0)
    return {
        "x": g["attn_a_x"],
        "WT": np.stack([w.T for w in a("W")]), "bias": np.stack(a("b")),
        "biasT": np.stack(a("b")[:3]).reshape(3, DH, P).transpose(2, 0, 1),
        "Bm": np.stack(a("B")), "AmT": np.stack([m.T for m in a("A")]),
        "RwT": np.ascontiguousarray(g["ffn_router_w"].T), "rbias": g["ffn_router_bias"],
        "Wup": up, "Wdn": dn,
        "Wret": np.concatenate([g[f"attn_b_W{m}"] for m in "qkvg"], 1), "WoB": g["attn_b_Wo"],
        "gnw": g["attn_b_g_norm_weight"],
    } | constants()


def kernel(**inputs):
    import concourse.bacc as bacc
    from concourse.bass_utils import run_bass_kernel_spmd

    nc = bacc.Bacc("TRN2", target_bir_lowering=False, num_devices=1)
    arrays = {f"in_{k}": np.ascontiguousarray(v) for k, v in lay_out(inputs).items()}
    io = {k[3:]: nc.dram_tensor(k, v.shape, mybir.dt.from_np(v.dtype), kind="ExternalInput").ap()
          for k, v in arrays.items()}
    out = nc.dram_tensor("out_x", [B, L, D], F32, kind="ExternalOutput").ap()
    build(nc, io, out)
    r = run_bass_kernel_spmd(nc, [arrays], core_ids=[0])
    return r.results[0]["out_x"]
```

```python
from contextlib import ExitStack

import numpy as np
import concourse.bass as bass
from concourse import mybir

F32 = mybir.dt.float32
F32R = mybir.dt.float32r
BF16 = mybir.dt.bfloat16
U32 = mybir.dt.uint32
I32 = mybir.dt.int32
ALU = mybir.AluOpType
ACT = mybir.ActivationFunctionType
AX_X = mybir.AxisListType.X

P = 128
B, L, D = 2, 1024, 256
N = B * L
NT = N // P
BLK = 512
NB = N // BLK
TPB = BLK // P
DH = D // P
EPS = 1e-5

HA, HDA, RANK = 16, 16, 16
SCALING = 8.0 / RANK
SCALE_A = HDA ** -0.5
HPG = 4
KT = L // P
TERMS = [(0, 0), (0, 1), (1, 0), (1, 1), (0, 2), (2, 0)]
KROWS = len(TERMS) * HDA
KEXP = KROWS + 3
JOBS = HPG * (BLK // P) * 2
RING = 3
RPS = JOBS + 1
SKEW = 3
TJ = 4

NE, ED = 16, 128
NU = NE + 2
TILES = 2 * N // P + NE
WORDS = TILES // 4
WC = DH * 2 * ED
WN = WC + D

HB, DK, DV = 8, 32, 64
QK = 2 * HB * DK
DVT = HB * DV


class Ctx:

    semaphores = []

    def __init__(self, nc, es, tag):
        self.nc, self.es, self.tag = nc, es, tag

    def sb(self, name, shape, dt=F32):
        return self.es.enter_context(self.nc.sbuf_tensor(f"{self.tag}_{name}", shape, dt))

    def ps(self, name, shape, dt=F32):
        return self.es.enter_context(self.nc.psum_tensor(f"{self.tag}_{name}", shape, dt))

    def sem(self, name):
        s_ = self.nc.alloc_semaphore(f"{self.tag}_{name}")
        Ctx.semaphores.append(s_)
        return s_


def clear_semaphores(nc):
    nc.clear_and_free_semaphores(Ctx.semaphores)
    nc.all_engine_barrier()
    Ctx.semaphores = []


def products(eng, out, lhs, rhs, first, last, **options):
    pairs = [(0, 0), (0, 1), (1, 0)]
    for n, (a, b) in enumerate(pairs):
        mm = eng.matmul(out, lhs[a], rhs[b], start=first and n == 0, stop=last and n == 2, **options)
    return mm


def normalise(nc, tag, x, ident, xt, keep=None, router=None, fetch=None, beside=None):
    with ExitStack() as es:
        c = Ctx(nc, es, tag)
        stats = c.sb("stats", [P, NT, 6])
        mv = c.sb("mv", [P, NT, 2])
        ve, nhalf, rstd, shift = (c.sb(n, [P, NT, 1]) for n in ("ve", "nhalf", "rstd", "shift"))
        xn = keep if keep is not None else c.sb("xn", [P, 2 * TPB, D])
        TX = NT if keep is not None else 2 * TPB
        pt = [c.ps(f"pt{n}", [P, BLK]) for n in range(4)]
        s_stats, s_mv, s_var, s_rstd, s_shift = (c.sem(n) for n in ("stats", "mv", "var", "rstd", "shift"))
        s_half = c.sem("half")
        s_xn, s_xa, s_t, s_hi, s_lo = (c.sem(n) for n in ("xn_vector", "xn_scalar", "transposed", "hi", "lo"))
        if router:
            rw = c.sb("rw", [P, DH, NE])
            rhi, rlo = c.sb("rhi", [P, DH, NE], F32R), c.sb("rlo", [P, DH, NE], F32R)
            pl = [c.ps(f"logits{n}", [NE, BLK]) for n in range(2)]
            s_rw, s_rhi, s_rlo, s_l, s_lg = (c.sem(n) for n in ("rw", "rw_hi", "rw_lo", "logits", "logits_copied"))
        SELF = TPB // 2
        block = es.enter_context(nc.Block())

        @block.sync
        def _(sp):
            if beside:
                beside.sync(sp)
            if fetch:
                fetch(sp)
            if router:
                sp.dma_start(rw[:, :, :], router[0].rearrange("(h p) e -> p h e", p=P)).then_inc(s_rw, 16)

        @block.vector
        def _(dve):
            def moments(b):
                ts = range(b * TPB, (b + 1) * TPB)
                if beside:
                    beside.there(dve, b)
                for t in ts:
                    dve.bn_stats(stats[:, t, :], x[:, t, :]).then_inc(s_stats, 1)
                for t in ts:
                    dve.wait_ge(s_stats, t + 1)
                    dve.bn_aggr(mv[:, t, :], stats[:, t, :]).then_inc(s_mv, 1)
                dve.wait_ge(s_mv, TPB * (b + 1))
                dve.tensor_scalar(ve[:, ts[0]:ts[-1] + 1, :], mv[:, ts[0]:ts[-1] + 1, 1:2], EPS, None, ALU.add).then_inc(s_var, 1)

            def scale(b):
                o = slice(b * TPB, (b + 1) * TPB)
                dve.wait_ge(s_rstd, b + 1)
                dve.scalar_tensor_tensor(out=shift[:, o, :], in0=mv[:, o, 0:1], scalar=-1.0, in1=rstd[:, o, :],
                                         op0=ALU.mult, op1=ALU.mult).then_inc(s_shift, 1)
                if b >= 2 and keep is None:
                    dve.wait_ge(s_t, 2 * (b - 1))
                for j in range(SELF):
                    t = b * TPB + j
                    dve.tensor_scalar(xn[:, t % TX, :], x[:, t, :], mv[:, t, 0:1], rstd[:, t, :],
                                      ALU.subtract, ALU.mult).then_inc(s_xn, 1)

            if beside:
                beside.fills(dve)
            moments(0)
            moments(1)
            if beside:
                beside.fold(dve)
            scale(0)
            if router:
                dve.wait_ge(s_rhi, 1)
                dve.tensor_tensor(rlo[:, :, :], rw[:, :, :], rhi[:, :, :].bitcast(F32), ALU.subtract).then_inc(s_rlo, 1)
            for b in range(NB):
                if b + 1 < NB:
                    scale(b + 1)
                if b + 2 < NB:
                    moments(b + 2)
                for h in range(DH):
                    n = DH * b + h
                    dve.wait_ge(s_hi, n + 1)
                    dve.tensor_tensor(xt[1][:, h, b * BLK:(b + 1) * BLK], pt[n % 4][:, :],
                                      xt[0][:, h, b * BLK:(b + 1) * BLK].bitcast(F32),
                                      ALU.subtract).then_inc(s_lo, 1)
                if beside and b == 0:
                    beside.low(dve)
            if beside:
                beside.set_constants(dve)

        @block.gpsimd
        def _(pool):
            pool.memset(nhalf[:, :, :], -0.5).then_inc(s_half, 1)
            pool.wait_ge(s_half, 1)
            if beside:
                beside.gpsimd(pool)
            for b in range(NB):
                o = slice(b * TPB, (b + 1) * TPB)
                pool.wait_ge(s_var, b + 1)
                pool.tensor_tensor(rstd[:, o, :], ve[:, o, :], nhalf[:, o, :], ALU.pow).then_inc(s_rstd, 1)

        @block.tensor
        def _(pe):
            def logits(b):
                pe.wait_ge(s_lo, DH * (b + 1))
                if b >= 2:
                    pe.wait_ge(s_lg, b - 1)
                for h in range(DH):
                    mm = products(pe, pl[b % 2][:, :], [a[:, h, :] for a in (rhi, rlo)],
                                  [a[:, h, b * BLK:(b + 1) * BLK] for a in xt], h == 0, h == DH - 1)
                mm.then_inc(s_l, 1)

            if beside:
                beside.tensor(pe)
                beside.constants_there(pe)
            if router:
                pe.wait_ge(s_rhi, 1)
                pe.wait_ge(s_rlo, 1)
            for b in range(NB):
                pe.wait_ge(s_xn, SELF * (b + 1))
                pe.wait_ge(s_xa, (TPB - SELF) * (b + 1))
                for h in range(DH):
                    n = DH * b + h
                    if n >= 4:
                        pe.wait_ge(s_lo, n - 3)
                    for j in range(TPB):
                        mm = pe.transpose(pt[n % 4][:, j * P:(j + 1) * P],
                                          xn[:, (b * TPB + j) % TX, h * P:(h + 1) * P], ident[:, :])
                    mm.then_inc(s_t, 1)
                if router and b >= 1:
                    logits(b - 1)
            if router:
                logits(NB - 1)

        @block.scalar
        def _(act):
            def scale(b):
                act.wait_ge(s_shift, b + 1)
                if b >= 2 and keep is None:
                    act.wait_ge(s_t, 2 * (b - 1))
                for j in range(SELF, TPB):
                    t = b * TPB + j
                    act.activation(xn[:, t % TX, :], x[:, t, :], ACT.Identity, bias=shift[:, t, :],
                                   scale=rstd[:, t, :]).then_inc(s_xa, 1)

            def copy_logits(b):
                act.wait_ge(s_l, b + 1)
                act.activation(router[1][:, b * BLK:(b + 1) * BLK], pl[b % 2][:, :], ACT.Copy).then_inc(s_lg, 1)

            if beside:
                beside.high(act)
            scale(0)
            if router:
                act.wait_ge(s_rw, 16)
                act.activation(rhi[:, :, :], rw[:, :, :], ACT.Copy).then_inc(s_rhi, 1)
            for b in range(NB):
                if b + 1 < NB:
                    scale(b + 1)
                for h in range(DH):
                    n = DH * b + h
                    act.wait_ge(s_t, n + 1)
                    act.activation(xt[0][:, h, b * BLK:(b + 1) * BLK], pt[n % 4][:, :], ACT.Copy).then_inc(s_hi, 1)
                if router and b >= 2:
                    copy_logits(b - 2)
            if beside:
                beside.scale_bias(act)
            if router:
                for b in range(NB - 2, NB):
                    copy_logits(b)


class Stacks:

    DMAS = 3 * len(TERMS)

    def __init__(self, nc, es, scratch):
        c = Ctx(nc, es, "stk")
        self.scratch = scratch
        self.k = [c.sb(f"k{u}", [KEXP, HPG, L], BF16) for u in range(2)]
        self.q = [c.sb(f"q{u}", [KEXP, 2, HPG, BLK], BF16) for u in range(2)]
        self.loaded = [c.sem(f"loaded{u}") for u in range(2)]

    def pieces(self, i, u):
        for n, (ck, cq) in enumerate(TERMS):
            rows = slice(n * HDA, (n + 1) * HDA)
            yield self.k[u][rows, :, :], self.scratch[1, ck, i, u].rearrange("h r t -> r h t")
            for qh in range(2):
                yield (self.q[u][rows, qh, :, :],
                       self.scratch[0, cq, i, u].rearrange("h r t -> r h t")[:, :, qh * BLK:(qh + 1) * BLK])

    def load(self, sp, i, u):
        for to, source in self.pieces(i, u):
            sp.dma_start(to, source).then_inc(self.loaded[u], 16)


class Lora:

    def __init__(self, nc, es):
        c = Ctx(nc, es, "lo")
        self.whi, self.wlo = c.sb("whi", [P, 3, DH, D], F32R), c.sb("wlo", [P, 3, DH, D], F32R)
        self.wo = c.sb("wo", [P, DH, D])
        self.bias, self.biass = c.sb("bias", [P, 3, DH]), c.sb("biass", [P, 3, DH])
        self.vb, self.bo = c.sb("vb", [P, D]), c.sb("bo", [P, D])


class Begin:

    def __init__(self, nc, es, io, x, ident, identb, c2, lora, vaug, stacks, zeros):
        c = Ctx(nc, es, "bg")
        self.x, self.io, self.lora, self.vaug, self.stacks = x, io, lora, vaug, stacks
        self.ident, self.identb, self.c2, self.zeros = ident, identb, c2, zeros
        self.wt = c.sb("wt", [P, 4, DH, D])
        self.bm = c.sb("bm", [RANK, 4, D])
        self.am = c.sb("am", [RANK, 4, D])
        self.weff = c.sb("weff", [P, 3, DH, D])
        self.tri = c.sb("tri", [P, P])
        self.pw = [c.ps(f"pw{n}", [P, BLK]) for n in range(4)]
        self.s_x = [c.sem(f"x{b}") for b in range(NB)]
        self.s_w, self.s_const, self.s_lora, self.s_weff, self.s_hi, self.s_lo, self.s_bias, self.s_set, self.s_ones = (
            c.sem(n) for n in ("weights", "constants", "products", "folded", "whi", "wlo", "bias", "set", "ones"))

        def row(ap, n):
            return ap.rearrange("(o n) -> o n", o=1).broadcast_to([P, n])

        self.weights = [(self.bm[:, :, :], io["Bm"].rearrange("n r d -> r n d")),
                        (self.am[:, :, :], io["AmT"].rearrange("n r o -> r n o"))]
        self.weights += [(self.wt[:, n, :, :], io["WT"][n].rearrange("(h p) o -> p h o", p=P)) for n in range(4)]
        self.constants = [(ident[:, :], io["ident"]), (self.tri[:, :], io["tri"]), (lora.bias[:, :, :], io["biasT"]),
                          (lora.vb[:, :], row(io["bias"][2], D)), (lora.bo[:, :], row(io["bias"][3], D)),
                          (c2.rbias[:, 0, :], row(io["rbias"], NE)), (c2.iota[:, 0, :], row(io["iota"], TILES)),
                          (c2.steps[:, 0, :], row(io["steps"], NE)),
                          (c2.lower[:, :, :].rearrange("p a b -> p (a b)"), row(io["lower"], NE * NE)),
                          (c2.sixteens[:, 0, :], io["sixteens"].rearrange("(o n) -> o n", o=1)), (c2.token[:, :], io["token"])]

    def there(self, eng, b):
        eng.wait_ge(self.s_x[b], 16)

    def constants_there(self, eng):
        eng.wait_ge(self.s_const, 16 * len(self.constants))

    def sync(self, sp):
        def load_x(b):
            tiles = slice(b * TPB, (b + 1) * TPB)
            sp.dma_start(self.x[:, tiles, :], self.io["x"].rearrange("b (t p) d -> p (b t) d", p=P)[:, tiles, :]).then_inc(self.s_x[b], 16)

        for b in range(2):
            load_x(b)
        for dst, src in self.weights:
            sp.dma_start(dst, src).then_inc(self.s_w, 16)
        for b in range(2, NB):
            load_x(b)
        for dst, src in self.constants:
            sp.dma_start(dst, src).then_inc(self.s_const, 16)

    def tensor(self, pe):
        pe.wait_ge(self.s_w, 16 * len(self.weights))
        for n in range(4):
            for h in range(DH):
                mm = pe.matmul(self.pw[n][:, h * D:(h + 1) * D], self.bm[:, n, h * P:(h + 1) * P], self.am[:, n, :],
                               start=True, stop=True)
            mm.then_inc(self.s_lora, 1)

    def fills(self, dve):
        dve.memset(self.c2.onesb[:, :], 1.0).then_inc(self.s_set, 1)
        dve.memset(self.zeros[:, :], 0.0).then_inc(self.s_set, 1)

    def fold(self, dve):
        lora, weff = self.lora, self.weff
        dve.wait_ge(self.s_w, 16 * len(self.weights))
        for n in range(4):
            dve.wait_ge(self.s_lora, n + 1)
            dve.scalar_tensor_tensor(out=weff[:, n, :, :] if n < 3 else lora.wo[:, :, :],
                                     in0=self.pw[n][:, :].rearrange("p (h o) -> p h o", h=DH),
                                     scalar=SCALING, in1=self.wt[:, n, :, :], op0=ALU.mult, op1=ALU.add).then_inc(self.s_weff, 1)

    def high(self, act):
        for n in range(3):
            act.wait_ge(self.s_weff, n + 1)
            act.activation(self.lora.whi[:, n, :, :], self.weff[:, n, :, :], ACT.Copy).then_inc(self.s_hi, 1)

    def low(self, dve):
        for n in range(3):
            dve.wait_ge(self.s_hi, n + 1)
            dve.tensor_tensor(self.lora.wlo[:, n, :, :], self.weff[:, n, :, :], self.lora.whi[:, n, :, :].bitcast(F32),
                              ALU.subtract).then_inc(self.s_lo, 1)

    def set_constants(self, dve):
        self.constants_there(dve)
        dve.tensor_copy(self.c2.trib[:, :], self.tri[:, :]).then_inc(self.s_set, 1)
        dve.tensor_copy(self.identb[:, :], self.ident[:, :]).then_inc(self.s_set, 1)

    def scale_bias(self, act):
        self.constants_there(act)
        act.mul(self.lora.biass[:, :, :], self.lora.bias[:, :, :], SCALE_A).then_inc(self.s_bias, 1)

    def gpsimd(self, pool):
        pool.memset(self.vaug[:, :, :, :, :, HDA:2 * HDA].rearrange("p b a k h r -> p (b a k h) r"), 1.0).then_inc(self.s_ones, 1)
        for u in range(2):
            pool.wait_ge(self.s_ones, u + 1)
            pool.memset(self.stacks.k[u][KROWS:KEXP, :, :].rearrange("p h t -> p (h t)"), 1.0).then_inc(self.s_ones, 1)
        pool.wait_ge(self.s_ones, 3)


def project_qkv(nc, x, xt, scratch, vaug, lora, stacks):
    with ExitStack() as es:
        c = Ctx(nc, es, "pj")
        R = 4
        xf = c.sb("xf", [P, R, BLK])
        rf = c.sb("rf", [P, R, BLK])
        parts = c.sb("parts", [P, R, 3, BLK], BF16)
        pp = [c.ps(f"pp{n}", [P, BLK]) for n in range(4)]
        pv = [c.ps(f"pv{n}", [P, BLK]) for n in range(2)]
        s_mm, s_xf, s_h, s_r, s_m, s_l = (c.sem(n) for n in ("mm", "xf", "h", "r", "m", "l"))
        s_st = [c.sem(f"stored{n}") for n in range(R)]
        s_vm, s_va, s_xb = c.sem("vmm"), c.sem("vadd"), c.sem("x_bias")
        JQ = 2 * DH * NB
        block = es.enter_context(nc.Block())

        def job(n):
            return n % 2, n // 4 % DH, n // 8 * 2 + n // 2 % 2

        @block.sync
        def _(sp):
            first = list(stacks.pieces(0, 0))
            PER_JOB = -(-len(first) // (JQ - 7))
            for n in range(JQ):
                side, half, tb = job(n)
                bb, off = tb * BLK // L, tb * BLK % L
                sp.wait_ge(s_l, n + 1)
                for k in range(3):
                    sp.dma_start(scratch[side, k, bb * DH + half].rearrange("u h r t -> (u h r) t")[:, off:off + BLK],
                                 parts[:, n % R, k, :]).then_inc(s_st[n % R], 16)
                if n == 7:
                    for s_ in s_st:
                        sp.wait_ge(s_, 16 * 3)
                if n >= 7:
                    for to, source in first[(n - 7) * PER_JOB:(n - 6) * PER_JOB]:
                        sp.dma_start(to, source).then_inc(stacks.loaded[0], 16)
            for s_ in s_st:
                sp.wait_ge(s_, 16 * 3 * JQ // R)

        @block.tensor
        def _(pe):
            w = (lora.whi, lora.wlo)
            for n in range(JQ):
                side, half, tb = job(n)
                if n >= 4:
                    pe.wait_ge(s_xf, n - 3)
                for h in range(DH):
                    mm = products(pe, pp[n % 4][:, :], [a[:, side, h, half * P:(half + 1) * P] for a in w],
                                  [a[:, h, tb * BLK:(tb + 1) * BLK] for a in xt], h == 0, h == DH - 1)
                mm.then_inc(s_mm, 1)
                t = n
                if t >= 2:
                    pe.wait_ge(s_va, t - 1)
                for h in range(DH):
                    mm = products(pe, pv[t % 2][:, 0:D], [a[:, h, t * P:(t + 1) * P] for a in xt],
                                  [a[:, 2, h, :] for a in w], h == 0, h == DH - 1)
                mm.then_inc(s_vm, 1)

        @block.gpsimd
        def _(pool):
            for t in range(NT):
                pool.tensor_tensor(x[:, t, :], x[:, t, :], lora.bo[:, :], ALU.add).then_inc(s_xb, 1)

        @block.scalar
        def _(act):
            def middle(n):
                act.wait_ge(s_r, n + 1)
                act.activation(parts[:, n % R, 1, :], rf[:, n % R, :], ACT.Copy).then_inc(s_m, 1)

            for n in range(JQ):
                side, half, tb = job(n)
                act.wait_ge(s_mm, n + 1)
                if n >= R:
                    act.wait_ge(s_r, n - R + 1)
                    act.wait_ge(s_st[n % R], 16 * 3 * (n // R))
                b = lora.biass if side == 0 else lora.bias
                act.activation(xf[:, n % R, :], pp[n % 4][:, :], ACT.Identity, bias=b[:, side, half:half + 1],
                               scale=SCALE_A if side == 0 else 1.0).then_inc(s_xf, 1)
                act.wait_ge(s_xf, n + 1)
                act.activation(parts[:, n % R, 0, :], xf[:, n % R, :], ACT.Copy).then_inc(s_h, 1)
                if n >= 1:
                    middle(n - 1)
            middle(JQ - 1)

        @block.vector
        def _(dve):
            def last(n):
                dve.wait_ge(s_m, n + 1)
                dve.tensor_tensor(parts[:, n % R, 2, :], rf[:, n % R, :], parts[:, n % R, 1, :],
                                  ALU.subtract).then_inc(s_l, 1)

            for n in range(JQ):
                dve.wait_ge(s_h, n + 1)
                if n >= R:
                    dve.wait_ge(s_m, n - R + 1)
                dve.tensor_tensor(rf[:, n % R, :], xf[:, n % R, :], parts[:, n % R, 0, :], ALU.subtract).then_inc(s_r, 1)
                t = n
                dve.wait_ge(s_vm, t + 1)
                dve.tensor_tensor(vaug[:, t // KT, :, t % KT, :, 0:HDA],
                                  pv[t % 2][:, 0:D].rearrange("p (a h r) -> p a h r", a=DH, r=HDA),
                                  lora.vb[:, :].rearrange("p (a h r) -> p a h r", a=DH, r=HDA), ALU.add).then_inc(s_va, 1)
                if n >= 1:
                    last(n - 1)
            last(JQ - 1)


def attend(nc, vaug, stacks, oall, identb, zero_rows):
    STEPS = B * DH
    SUBS = 4
    with ExitStack() as es:
        c = Ctx(nc, es, "at")
        kst, qst, s_stack = stacks.k, stacks.q, stacks.loaded
        vst = [c.sb(f"vst{u}", [P, KT, HPG, 32]) for u in range(2)]
        prob = [c.sb(f"prob{n}", [P, HPG, BLK]) for n in range(4)]
        mx = c.sb("mx", [P, JOBS])
        mrow = c.sb("mrow", [P, 2, JOBS // 2])
        mneg = c.sb("mneg", [P, JOBS // 2])
        mres = c.sb("mres", [P, JOBS // 2])
        zero = c.sb("zero", [P, JOBS // 2])
        msplit = c.sb("msplit", [P, P], BF16)
        mT = [c.sb(f"mT{n}", [P, P], BF16) for n in range(2)]
        ps_s = [c.ps(f"score{n}", [P, 2, BLK]) for n in range(2)]
        ps_m = [c.ps(f"max{n}", [P, BLK]) for n in range(RING)]
        ps_o = c.ps("out", [P, BLK])
        s_rows, s_ones = c.sem("max_rows_loaded"), c.sem("ones")
        s_vst = c.sem("v_staged")
        s_score = [c.sem(f"scores_ready{n}") for n in range(2)]
        s_exp = [c.sem(f"exp_done{n}") for n in range(2)]
        s_pv, s_oev = c.sem("sub_values_done"), c.sem("out_evacuated")
        s_mm, s_free, s_chain, s_split = (c.sem(n) for n in ("max_ready", "max_bank_free", "max_chain", "max_split"))
        s_comb, s_zero = c.sem("max_combined"), c.sem("zero")
        SLOTS = SUBS * KT
        JPS = JOBS // KT
        UNIT_DMAS = stacks.DMAS
        CH = 4
        block = es.enter_context(nc.Block())

        def sub(i, s):
            return SUBS * i + s

        def job_slot(n, j):
            if type(n) is int and n == 0:
                return j, j % RING
            k = j if j < TJ else j + 1
            return RPS * n + k - 1, (k - 1) % RING

        def turn_slot(n):
            k = TJ if type(n) is not int or n < SUBS * STEPS - 1 else 0
            return RPS * (n + 1) + k - 1, (k - 1) % RING

        @block.sync
        def _(sp):
            def load_rows(n, s):
                sp.wait_ge(s_free, turn_slot(n)[0] + 1)
                for k in range(3):
                    sp.dma_start(qst[s // 2][KROWS + k:KROWS + k + 1, s % 2, :, :].rearrange("o h (t j) -> o (h t) j", j=P),
                                 mT[s % 2][k * (JOBS // 2):(k + 1) * (JOBS // 2), :]).then_inc(s_rows, 16)

            stacks.load(sp, 0, 1)
            load_rows(0, 0)
            zero_rows(sp)

            def step(i, last):
                for s in range(SUBS):
                    if not (last and s == SUBS - 1):
                        load_rows(sub(i, s) + 1, (s + 1) % SUBS)
                    if s % 2 and not last:
                        sp.wait_ge(s_score[1], KT * (sub(i, s) + 1))
                        stacks.load(sp, i + 1, s // 2)

            with sp.Fori(0, STEPS - 1) as i:
                step(i, False)
            step(STEPS - 1, True)

        @block.gpsimd
        def _(pool):
            def stage(i, u):
                pool.tensor_copy(vst[u][:, :, :, :],
                                 vaug[:, :, :, :, :, :].rearrange("p b a k h r -> p (b a) k h r")
                                 [:, i, :, u * HPG:(u + 1) * HPG, :]).then_inc(s_vst, 1)

            def split(n, s):
                h, m, l = (msplit[:, k * JOBS // 2:(k + 1) * JOBS // 2] for k in range(3))
                pool.wait_ge(s_comb, n + 1)
                if type(n) is not int or n > 0:
                    pool.wait_ge(s_mm, turn_slot(n - 1)[0] + 1)
                pool.tensor_tensor(mneg[:, :], zero[:, :], mrow[:, s % 2, :], ALU.subtract).then_inc(s_chain, 1)
                pool.wait_ge(s_chain, CH * n + 1)
                pool.tensor_tensor(h, mneg[:, :], zero[:, :], ALU.add).then_inc(s_chain, 1)
                pool.wait_ge(s_chain, CH * n + 2)
                pool.tensor_tensor(mres[:, :], mneg[:, :], h, ALU.subtract).then_inc(s_chain, 1)
                pool.wait_ge(s_chain, CH * n + 3)
                pool.tensor_tensor(m, mres[:, :], zero[:, :], ALU.add).then_inc(s_chain, 1)
                pool.wait_ge(s_chain, CH * n + 4)
                pool.tensor_tensor(l, mres[:, :], m, ALU.subtract).then_inc(s_split, 1)

            pool.memset(zero[:, :], 0.0).then_inc(s_zero, 1)
            pool.wait_ge(s_zero, 1)
            split(0, 0)
            stage(0, 0)
            stage(0, 1)
            with pool.Fori(0, STEPS - 1) as i:
                for s in range(SUBS):
                    split(sub(i, s) + 1, s + 1)
                    if s % 2:
                        pool.wait_ge(s_pv, sub(i, s) + 1)
                        stage(i + 1, s // 2)
            for s in range(SUBS - 1):
                split(sub(STEPS - 1, s) + 1, s + 1)

        @block.tensor
        def _(pe):
            def max_job(i, s, j):
                i, s = i + s // SUBS, s % SUBS
                n = sub(i, s)
                slot, bank = job_slot(n, j)
                if type(n) is not int or slot >= RING:
                    pe.wait_ge(s_free, slot - RING + 1)
                if j == 0 and s % 2 == 0:
                    pe.wait_ge(s_stack[s // 2], UNIT_DMAS * 16 * (i + 1))
                h, qt, kh = j // 8, j // 2 % 4, j % 2
                pe.matmul(ps_m[bank][:, :], qst[s // 2][0:KROWS, s % 2, h, qt * P:(qt + 1) * P],
                          kst[s // 2][0:KROWS, h, kh * BLK:(kh + 1) * BLK], start=True, stop=True).then_inc(s_mm, 1)

            def max_turn(n, s):
                slot, bank = turn_slot(n)
                pe.wait_ge(s_split, n + 1)
                pe.wait_ge(s_free, slot - RING + 1)
                pe.transpose(ps_m[bank][:, 0:P // 2].bitcast(BF16), msplit[:, :], identb[:, :]).then_inc(s_mm, 1)

            def scores(n, s, kt, pair):
                if kt == 0 and pair == 0:
                    pe.wait_ge(s_rows, 16 * 3 * (n + 1))
                pe.wait_ge(s_exp[pair], KT * n + kt + 1)
                for k in range(2):
                    h = 2 * pair + k
                    mm = pe.matmul(ps_s[pair][:, k, :], kst[s // 2][:, h, kt * P:(kt + 1) * P],
                                   qst[s // 2][:, s % 2, h, :], start=True, stop=True)
                mm.then_inc(s_score[pair], 1)

            def values(i, s, kt):
                n = sub(i, s)
                for pair in range(2):
                    pe.wait_ge(s_exp[pair], KT * n + kt + 2)
                if kt == 0:
                    pe.wait_ge(s_oev, n + 1)
                    if s % 2 == 0:
                        pe.wait_ge(s_vst, 2 * i + s // 2 + 1)
                for h in range(HPG):
                    mm = pe.matmul(ps_o[32 * h:32 * h + 32, :], vst[s // 2][:, kt, h, :], prob[kt % 4][:, h, :],
                                   start=(kt == 0), stop=(kt == KT - 1))
                if kt == KT - 1:
                    mm.then_inc(s_pv, 1)

            def slot(i, r, last):
                i, r = i + r // SLOTS, r % SLOTS
                s, kt = r // KT, r % KT

                def job(q):
                    j = JPS * (kt + SKEW) + q
                    ahead = s + 1 + j // JOBS
                    if j % JOBS == TJ and j >= JOBS and not (last and s + 1 >= SUBS):
                        max_turn(sub(i, s) + 1, (s + 1) % SUBS)
                    if not (last and ahead >= SUBS):
                        max_job(i, ahead, j % JOBS)

                scores(sub(i, s), s, kt, 0)
                job(0)
                scores(sub(i, s), s, kt, 1)
                job(1)
                job(2)
                if type(i) is not int or i > 0 or r > 0:
                    p = r - 1
                    values(i if p >= 0 else i - 1, p % SLOTS // KT, p % KT)
                job(3)

            pe.wait_ge(s_ones, 1)
            for j in range(JOBS):
                max_job(0, 0, j)
            for j in range(TJ):
                max_job(0, 1, j)
            max_turn(0, 0)
            for j in range(TJ, JPS * SKEW):
                max_job(0, 1, j)
            slot(0, 0, False)
            with pe.Fori(0, STEPS - 1) as i:
                for r in range(1, SLOTS + 1):
                    slot(i, r, False)
            for r in range(1, SLOTS):
                slot(STEPS - 1, r, True)
            values(STEPS - 1, SUBS - 1, KT - 1)

        @block.scalar
        def _(act):
            def evacuate(i, s):
                n = sub(i, s)
                act.wait_ge(s_pv, n + 1)
                act.activation(oall[:, i, s // 2, s % 2, :], ps_o[:, :], ACT.Copy).then_inc(s_oev, 1)

            def slot(i, r):
                i, r = i + r // SLOTS, r % SLOTS
                s, kt = r // KT, r % KT
                for pair in range(2):
                    act.wait_ge(s_score[pair], KT * sub(i, s) + kt + 1)
                    act.activation(prob[kt % 4][:, 2 * pair:2 * pair + 2, :], ps_s[pair][:, :, :],
                                   ACT.Exp).then_inc(s_exp[pair], 1)

            for sem in (*s_exp, s_oev):
                act.sem_inc(sem, 1)
            slot(0, 0)
            with act.Fori(0, STEPS - 1) as i:
                for r in range(1, SLOTS + 1):
                    slot(i, r)
                    if r % KT == 0:
                        evacuate(i, r // KT - 1)
            for r in range(1, SLOTS):
                slot(STEPS - 1, r)
                if r % KT == 0:
                    evacuate(STEPS - 1, r // KT - 1)
            evacuate(STEPS - 1, SUBS - 1)

        @block.vector
        def _(dve):
            def reduce(n, j):
                slot, bank = job_slot(n, j)
                dve.wait_ge(s_mm, slot + 1)
                dve.tensor_reduce(mx[:, j:j + 1], ps_m[bank][:, :], AX_X, ALU.max).then_inc(s_free, 1)

            def combine(n, s):
                dve.wait_ge(s_free, job_slot(n, JOBS - 1)[0] + 1)
                if type(n) is not int or n > 1:
                    dve.wait_ge(s_split, n - 1)
                dve.tensor_reduce(mrow[:, s % 2, :], mx[:, :].rearrange("p (n k) -> p n k", k=2), AX_X,
                                  ALU.max).then_inc(s_comb, 1)
                dve.wait_ge(s_comb, n + 1)

            def turned(n, s):
                slot, bank = turn_slot(n)
                dve.wait_ge(s_mm, slot + 1)
                dve.tensor_copy(mT[s % 2][:, :], ps_m[bank][:, 0:P // 2].bitcast(BF16)).then_inc(s_free, 1)

            def step(i, last):
                for s in range(SUBS):
                    n = sub(i, s)
                    if last and s + 1 >= SUBS:
                        continue
                    for j in range(JPS * SKEW, JOBS):
                        reduce(n + 1, j)
                    combine(n + 1, s + 1)
                    for j in range(JPS * SKEW):
                        if j == TJ:
                            turned(n + 1, (s + 1) % SUBS)
                        if not (last and s + 2 >= SUBS):
                            reduce(n + 2, j)

            dve.memset(msplit[:, :], 0.0).then_inc(s_ones, 1)
            for j in range(JOBS):
                reduce(0, j)
            combine(0, 0)
            for j in range(JPS * SKEW):
                if j == TJ:
                    turned(0, 0)
                reduce(1, j)
            with dve.Fori(0, STEPS - 1) as i:
                step(i, False)
            step(STEPS - 1, True)


def project_out(nc, x, oall, wo, ident):
    with ExitStack() as es:
        c = Ctx(nc, es, "po")
        rec = c.sb("rec", [P, 2, HA, 1])
        at = c.sb("at", [P, 2, D])
        atT = c.sb("atT", [P, 2, D])
        p_h = [c.ps(f"heads{n}", [P, BLK]) for n in range(2)]
        p_t = [c.ps(f"turned{n}", [P, BLK]) for n in range(2)]
        p_y = [c.ps(f"y{n}", [P, BLK]) for n in range(2)]
        s_h, s_rec, s_at, s_t, s_tc, s_y, s_x = (c.sem(n) for n in ("heads", "rec", "at", "t", "tc", "y", "x"))
        block = es.enter_context(nc.Block())

        @block.tensor
        def _(pe):
            def heads(t):
                b, qh, j = t // KT, t % KT // TPB, t % TPB
                if t >= 2:
                    pe.wait_ge(s_at, t - 1)
                for g in range(4):
                    mm = pe.transpose(p_h[t % 2][:, g * P:(g + 1) * P],
                                      oall[:, DH * b + g // 2, g % 2, qh, j * P:(j + 1) * P], ident[:, :])
                mm.then_inc(s_h, 1)

            def project(t):
                pe.wait_ge(s_tc, t + 1)
                if t >= 2:
                    pe.wait_ge(s_x, t - 1)
                for h in range(DH):
                    mm = pe.matmul(p_y[t % 2][:, 0:D], atT[:, t % 2, h * P:(h + 1) * P], wo[:, h, :],
                                   start=(h == 0), stop=(h == DH - 1))
                mm.then_inc(s_y, 1)

            heads(0)
            for t in range(NT):
                if t + 1 < NT:
                    heads(t + 1)
                pe.wait_ge(s_at, t + 1)
                if t >= 2:
                    pe.wait_ge(s_tc, t - 1)
                for h in range(DH):
                    mm = pe.transpose(p_t[t % 2][:, h * P:(h + 1) * P], at[:, t % 2, h * P:(h + 1) * P], ident[:, :])
                mm.then_inc(s_t, 1)
                if t >= 1:
                    project(t - 1)
            project(NT - 1)

        @block.scalar
        def _(act):
            for t in range(NT):
                act.wait_ge(s_t, t + 1)
                if t >= 2:
                    act.wait_ge(s_y, t - 1)
                act.activation(atT[:, t % 2, :], p_t[t % 2][:, 0:D], ACT.Copy).then_inc(s_tc, 1)

        @block.vector
        def _(dve):
            def add(t):
                dve.wait_ge(s_y, t + 1)
                dve.tensor_tensor(x[:, t, :], p_y[t % 2][:, 0:D], x[:, t, :], ALU.add).then_inc(s_x, 1)

            for t in range(NT):
                heads = p_h[t % 2][:, :].rearrange("p (h r) -> p h r", r=2 * HDA)
                dve.wait_ge(s_h, t + 1)
                dve.reciprocal(rec[:, t % 2, :, :], heads[:, :, HDA:HDA + 1]).then_inc(s_rec, 1)
                dve.wait_ge(s_rec, t + 1)
                if t >= 2:
                    dve.wait_ge(s_t, t - 1)
                dve.tensor_tensor(at[:, t % 2, :].rearrange("p (h r) -> p h r", r=HDA), heads[:, :, 0:HDA],
                                  rec[:, t % 2, :, :].broadcast_to([P, HA, HDA]), ALU.mult).then_inc(s_at, 1)
                if t >= 2:
                    add(t - 2)
            add(NT - 2)
            add(NT - 1)


def route_and_share(nc, io, tag, x, xt, c2, ident, whi, wlo):
    with ExitStack() as es:
        c = Ctx(nc, es, tag)
        lb, sh = c.sb("lb", [P, NT, NE]), c.sb("sh", [P, NT, NE])
        m8 = c.sb("m8", [P, NT, 8])
        idx = c.sb("idx", [P, NT, 2])
        oh, op = c.sb("oh", [P, 2, NT, NE], BF16), c.sb("op", [P, 2, NT, NE])
        sel = c.sb("sel", [P, NT, NE], BF16)
        mraw, tot, rt = (c.sb(n, [P, NT, 1]) for n in ("mraw", "tot", "rt"))
        wraw, slotf = c.sb("wraw", [P, 2, NT]), c.sb("slotf", [P, 2, NT])
        cnt, tiles, first, base, end = (c.sb(n, [P, NE, 1]) for n in ("cnt", "tiles", "first", "base", "end"))
        more = c.sb("more", [P, NE, NE])
        i8 = more[:, 0:NE // 2, :].bitcast(U32).rearrange("p a (b k) -> p (a b) k", k=8)
        half, upper = c.sb("half", [1, WORDS, 1]), c.sb("upper", [1, WORDS - 1], I32)
        past, eidf = c.sb("past", [1, TILES, NE], BF16), c.sb("eidf", [1, TILES, 1])
        pr = c.ps("router", [P, 2, NT * NE])
        s_l, s_e, s_c, s_sel, s_rank, s_lb, s_slot = (
            c.sem(n) for n in ("logits", "exp", "chain", "selected", "ranks", "logits_used", "slots"))
        RAW = 3
        shi = [c.sb(f"shi{u}", [P, WN], F32R) for u in range(2)]
        slo = [c.sb(f"slo{u}", [P, WN], F32R) for u in range(2)]
        raw = [c.sb(f"raw{n}", [P, WN]) for n in range(RAW)]
        su, hf = c.sb("su", [P, BLK]), c.sb("hf", [P, 2, BLK])
        hhi, hlo = c.sb("hhi", [P, 2, BLK], F32R), c.sb("hlo", [P, 2, BLK], F32R)
        pu = [c.ps(f"up{n}", [P, BLK]) for n in range(2)]
        pg = [c.ps(f"gate{n}", [P, BLK]) for n in range(2)]
        DQ = 3
        pd = [c.ps(f"down{n}", [P, 2, D]) for n in range(DQ)]
        s_raw = [c.sem(f"raw{n}") for n in range(RAW)]
        s_whi, s_wlo = c.sem("weights_hi"), c.sem("weights_lo")
        s_ug, s_su, s_hf, s_hh, s_hl = (c.sem(n) for n in ("up_gate", "silu", "hidden", "hidden_hi", "hidden_lo"))
        s_d, s_x, s_place = c.sem("down"), c.sem("x_added"), c.sem("places")
        s_sc = [c.sem(f"scattered{n}") for n in range(4)]
        SLOTS = 2 * NB
        SPLITS = NE // SLOTS
        shape = [P, NT, NE]
        block = es.enter_context(nc.Block())

        @block.sync
        def _(sp):
            for n in range(NU):
                u, dst, sem = (n - 2) % NU, raw[n % RAW], s_raw[n % RAW]
                if n >= RAW:
                    sp.wait_ge(s_wlo, n - RAW + 1)
                sp.dma_start(dst[:, 0:WC].rearrange("p (h n) -> p h n", h=DH),
                             io["Wup"][u].rearrange("(h p) n -> p h n", p=P)).then_inc(sem, 16)
                sp.dma_start(dst[:, WC:WN], io["Wdn"][u]).then_inc(sem, 16)

        @block.gpsimd
        def _(pool):
            pool.wait_ge(s_slot, 1)
            for n in range(4):
                pool.wait_ge(s_place, max(n, 1))
                for t in range(n % 2 * NT // 2, (n % 2 + 1) * NT // 2):
                    pool.indirect_dma_start(c2.rows_in, bass.IndirectOffsetOnAxis(ap=c2.slot[:, n // 2, t:t + 1], axis=0),
                                            c2.xn[:, t, :], None).then_inc(s_sc[n], 16)
            for n in (2, 3):
                pool.wait_ge(s_sc[n], 16 * NT // 2)

        @block.tensor
        def _(pe):
            def up(k):
                tb, u = k // 2, k % 2
                if tb == 0:
                    pe.wait_ge(s_wlo, u + 1)
                if k >= 2:
                    pe.wait_ge(s_hf, k - 1)
                for p_, off in ((pu, 0), (pg, ED)):
                    for h in range(DH):
                        mm = products(pe, p_[k % 2][:, :], [a[:, h * 2 * ED + off:h * 2 * ED + off + ED] for a in (shi[u], slo[u])],
                                      [a[:, h, tb * BLK:(tb + 1) * BLK] for a in xt], h == 0, h == DH - 1)
                mm.then_inc(s_ug, 1)

            def down(k):
                pe.wait_ge(s_hl, k + 1)
                for q in range(2):
                    m = k // 2 * 2 + q
                    if m >= DQ and k % 2 == 0:
                        pe.wait_ge(s_x, m - DQ + 1)
                    for j in range(2):
                        o = (2 * q + j) * P
                        mm = products(pe, pd[m % DQ][:, j, :], [a[:, k % 2, o:o + P] for a in (hhi, hlo)],
                                      [a[:, WC:WN] for a in (shi[k % 2], slo[k % 2])], k % 2 == 0 and j == 0, k % 2 == 1,
                                      skip_group_check=True)
                    mm.then_inc(s_d, 1)

            for t in range(NT):
                mm = pe.transpose(pr[:, 0, t * NE:(t + 1) * NE], c2.logits[:, t * P:(t + 1) * P], ident[0:NE, 0:NE])
            mm.then_inc(s_l, 1)
            pe.wait_ge(s_sel, 1)
            pe.matmul(pr[:, 0, :], c2.onesb[:, :], sel[:, :, :], start=True, stop=True, skip_group_check=True)
            pe.matmul(pr[:, 1, :], c2.trib[:, :], sel[:, :, :], start=True, stop=False, skip_group_check=True)
            for t in range(NT - 1):
                mm = pe.matmul(pr[:, 1, (t + 1) * NE:NT * NE], c2.onesb[:, :],
                               sel[:, t:t + 1, :].broadcast_to([P, NT - 1 - t, NE]), start=False, stop=(t == NT - 2),
                               skip_group_check=True)
            mm.then_inc(s_rank, 1)
            up(0)
            up(1)
            down(0)
            for k in range(2, SLOTS):
                up(k)
                down(k - 1)
            down(SLOTS - 1)

        @block.scalar
        def _(act):
            def split(n, dst):
                act.wait_ge(s_raw[n % RAW], 32 * (n // RAW + 1))
                act.activation(dst, raw[n % RAW][:, :], ACT.Copy).then_inc(s_whi, 1)

            for u in range(2):
                split(u, shi[u][:, :])
            act.wait_ge(s_lb, 1)
            act.activation(sh[:, :, :], sh[:, :, :], ACT.Exp).then_inc(s_e, 1)
            for k in range(SLOTS):
                act.wait_ge(s_ug, k + 1)
                if k >= 1:
                    act.wait_ge(s_hf, k)
                act.activation(su[:, :], pu[k % 2][:, :], ACT.Silu).then_inc(s_su, 1)
                for e in range(SPLITS * k, SPLITS * (k + 1)):
                    split(e + 2, whi[:, e, :])
                    if e == SPLITS * k:
                        act.wait_ge(s_hf, k + 1)
                        if k >= 2:
                            act.wait_ge(s_d, 2 * (k - 1))
                        act.activation(hhi[:, k % 2, :], hf[:, k % 2, :], ACT.Copy).then_inc(s_hh, 1)

        @block.vector
        def _(dve):
            done = [0]

            def link(ins):
                done[0] += 1
                ins.then_inc(s_c, 1)
                dve.wait_ge(s_c, done[0])

            def split(n, dst, hi):
                dve.wait_ge(s_whi, n + 1)
                dve.tensor_tensor(dst, raw[n % RAW][:, :], hi.bitcast(F32), ALU.subtract).then_inc(s_wlo, 1)

            def add(m):
                t = 2 * m
                dve.wait_ge(s_d, m // 2 * 4 + 3 + m % 2)
                dve.tensor_tensor(x[:, t:t + 2, :], pd[m % DQ][:, :, :], x[:, t:t + 2, :], ALU.add).then_inc(s_x, 1)

            def hidden(k):
                dve.wait_ge(s_su, k + 1)
                dve.tensor_tensor(hf[:, k % 2, :], su[:, :], pg[k % 2][:, :], ALU.mult).then_inc(s_hf, 1)
                for e in range(SPLITS * k, SPLITS * (k + 1)):
                    split(e + 2, wlo[:, e, :], whi[:, e, :])
                    if e == SPLITS * k:
                        dve.wait_ge(s_hh, k + 1)
                        if k >= 2:
                            dve.wait_ge(s_d, 2 * (k - 1))
                        dve.tensor_tensor(hlo[:, k % 2, :], hf[:, k % 2, :], hhi[:, k % 2, :].bitcast(F32),
                                          ALU.subtract).then_inc(s_hl, 1)

            places = c2.xn[:, :, D:D + 1].rearrange("p t o -> p (t o)").bitcast(U32)
            dve.tensor_copy(places, c2.token[:, :]).then_inc(s_place, 1)
            dve.wait_ge(s_l, 1)
            lg = pr[:, 0, :].rearrange("p (t e) -> p t e", e=NE)
            link(dve.tensor_tensor(lb[:, :, :], lg, c2.rbias[:, :, :].broadcast_to(shape), ALU.add))
            for t in range(NT):
                dve.max(m8[:, t, :], lb[:, t, :]).then_inc(s_c, 1)
                done[0] += 1
            dve.wait_ge(s_c, done[0])
            for t in range(NT):
                dve.max_index(i8[:, t, :], m8[:, t, :], lb[:, t, :]).then_inc(s_c, 1)
                done[0] += 1
            dve.wait_ge(s_c, done[0])
            link(dve.tensor_copy(idx[:, :, :], i8[:, :, 0:2]))
            for k in range(2):
                dve.tensor_tensor(oh[:, k, :, :], c2.iota[:, :, 0:NE].broadcast_to(shape),
                                  idx[:, :, k:k + 1].broadcast_to(shape), ALU.is_equal).then_inc(s_c, 1)
                done[0] += 1
            dve.tensor_reduce(mraw[:, :, :], lg, AX_X, ALU.max).then_inc(s_c, 1)
            done[0] += 1
            dve.wait_ge(s_c, done[0])
            dve.tensor_tensor(sh[:, :, :], lg, mraw[:, :, :].broadcast_to(shape), ALU.subtract).then_inc(s_lb, 1)
            dve.wait_ge(s_lb, 1)
            dve.tensor_tensor(sel[:, :, :], oh[:, 0, :, :], oh[:, 1, :, :], ALU.add).then_inc(s_sel, 1)
            for u in range(2):
                split(u, slo[u][:, :], shi[u][:, :])
            dve.wait_ge(s_rank, 1)
            link(dve.tensor_reduce(cnt[:, :, 0], pr[:, 0, :].rearrange("p (t e) -> p e t", e=NE), AX_X, ALU.add))
            link(dve.tensor_tensor(more[:, :, :], cnt[:, :, :].broadcast_to([P, NE, NE]),
                                   c2.steps[:, :, :].broadcast_to([P, NE, NE]), ALU.is_gt))
            link(dve.tensor_reduce(tiles[:, :, 0], more[:, :, :], AX_X, ALU.add))
            link(dve.tensor_tensor(more[:, :, :], c2.lower[:, :, :],
                                   tiles[:, :, :].rearrange("p e o -> p o e").broadcast_to([P, NE, NE]), ALU.mult))
            link(dve.tensor_reduce(first[:, :, 0], more[:, :, :], AX_X, ALU.add))
            link(dve.tensor_scalar(base[:, :, 0], first[:, :, 0], float(P), None, ALU.mult))
            link(dve.tensor_tensor(lb[:, :, :], pr[:, 1, :].rearrange("p (t e) -> p t e", e=NE),
                                   base[:, :, :].rearrange("p e o -> p o e").broadcast_to(shape), ALU.add))
            for k in range(2):
                link(dve.tensor_tensor(op[:, k, :, :], oh[:, k, :, :], lb[:, :, :], ALU.mult))
            link(dve.tensor_reduce(slotf[:, :, :], op[:, :, :, :], AX_X, ALU.add))
            dve.tensor_copy(c2.slot[:, :, :], slotf[:, :, :]).then_inc(s_slot, 1)
            for k in range(SLOTS):
                hidden(k)
                if k >= 2 and k % 2 == 0:
                    add(k - 2)
                    add(k - 1)
                if k in (2, 4):
                    tiles_ = slice((k - 2) // 2 * NT // 2, k // 2 * NT // 2)
                    dve.wait_ge(s_sc[(k - 2) // 2], 16 * NT // 2)
                    dve.tensor_scalar(places[:, tiles_], c2.token[:, tiles_], float(N), None, ALU.add).then_inc(s_place, 1)
            dve.wait_ge(s_e, 1)
            for k in range(2):
                link(dve.tensor_tensor(op[:, k, :, :], oh[:, k, :, :], sh[:, :, :], ALU.mult))
            link(dve.tensor_reduce(wraw[:, :, :], op[:, :, :, :], AX_X, ALU.add))
            link(dve.tensor_tensor(tot[:, :, 0], wraw[:, 0, :], wraw[:, 1, :], ALU.add))
            link(dve.reciprocal(rt[:, :, 0], tot[:, :, 0]))
            link(dve.tensor_tensor(c2.weight[:, :, :], wraw[:, :, :],
                                   rt[:, :, 0:1].rearrange("p t o -> p o t").broadcast_to([P, 2, NT]), ALU.mult))
            link(dve.tensor_tensor(end[:, :, 0], first[:, :, 0], tiles[:, :, 0], ALU.add))
            link(dve.tensor_tensor(past[:, :, :], end[0:1, :, :].rearrange("p e o -> p o e").broadcast_to([1, TILES, NE]),
                                   c2.iota[0:1, :, :].rearrange("p o j -> p j o").broadcast_to([1, TILES, NE]), ALU.is_le))
            link(dve.tensor_reduce(eidf[:, :, 0], past[:, :, :], AX_X, ALU.add))
            link(dve.tensor_scalar(eidf[:, :, 0], eidf[:, :, 0], float(NE - 1), None, ALU.min))
            fours = eidf[:, :, 0].rearrange("p (m k) -> p m k", k=4)
            link(dve.tensor_tensor(fours, fours, c2.sixteens[:, :, :].broadcast_to([1, WORDS, 4]), ALU.mult))
            link(dve.tensor_reduce(half[:, :, 0], fours, AX_X, ALU.add))
            link(dve.tensor_copy(c2.experts[:, :], half[:, :, 0]))
            link(dve.tensor_scalar(upper[:, :], c2.experts[:, 1:WORDS], 16, None, ALU.logical_shift_left))
            link(dve.tensor_tensor(c2.experts[:, 0:WORDS - 1], c2.experts[:, 0:WORDS - 1], upper[:, :], ALU.bitwise_or))
            add(SLOTS - 2)
            add(SLOTS - 1)


def routed_experts(nc, tag, x, c2, ident, whi, wlo, out):
    RING = 4
    PAIRS = TILES // 2
    LOOPS = (PAIRS - 4) // RING
    AHEAD = 3
    with ExitStack() as es:
        c = Ctx(nc, es, tag)
        xg = [c.sb(f"xg{n}", [P, 2, D + 1]) for n in range(RING)]
        place = c.sb("place", [P, TILES], U32)
        xhi, xlo = c.sb("xhi", [P, 2, 2 * DH, P], F32R), c.sb("xlo", [P, 2, 2 * DH, P], F32R)
        su, hf = c.sb("su", [P, 2, 2, ED]), c.sb("hf", [P, 2, 2, ED])
        hhi, hlo = c.sb("hhi", [P, 2, 2, P], F32R), c.sb("hlo", [P, 2, 2, P], F32R)
        ys = [c.sb(f"ys{n}", [P, 2, D]) for n in range(RING)]
        rows = c2.xn[:, :, :].rearrange("p t d -> p (t d)")
        yb = [rows[:, n * 2 * TPB * D:(n + 1) * 2 * TPB * D].rearrange("p (k t d) -> p k t d", k=2, t=TPB) for n in range(2)]
        pa, pb, pd = ([c.ps(f"{m}{n}", [P, 2, 2 * ED]) for n in range(2)] for m in ("rowsT", "upgate", "down"))
        pc = [c.ps(f"hiddenT{n}", [P, 2 * P]) for n in range(2)]
        s_xg = [c.sem(f"rows_loaded{n}") for n in range(RING)]
        s_st = [c.sem(f"rows_stored{n}") for n in range(RING)]
        s_yb = [c.sem(f"results_loaded{n}") for n in range(2)]
        s_a, s_b, s_c, s_d = (c.sem(n) for n in ("rows_transposed", "up_gate", "hidden_transposed", "down"))
        s_xh, s_xl, s_su, s_h, s_hh, s_hl, s_ev = (
            c.sem(n) for n in ("rows_hi", "rows_lo", "silu", "hidden", "hidden_hi", "hidden_lo", "down_copied"))
        s_x, s_xp, s_yw = c.sem("x_added"), c.sem("x_added_by_gpsimd"), c.sem("results_weighted")
        s_place, s_out = c.sem("places_copied"), c.sem("stored")
        rows_in = c2.rows_in.rearrange("(n t p) d -> n p t d", t=2, p=P)
        results = c2.rows_out[0:2 * N, :].rearrange("(k t p) d -> p k t d", k=2, p=P)
        block = es.enter_context(nc.Block())

        def slots(eng, slot, peeled=0):
            for j in range(-2, RING * peeled + 1):
                slot(j, j % RING)
            with eng.Fori(peeled, LOOPS) as i:
                for r in range(1, RING + 1):
                    slot(RING * i + r, r % RING, i)
            for j in range(RING * LOOPS + 1, PAIRS + 1):
                slot(j, j % RING)

        def there(j):
            return type(j) is not int or 0 <= j < PAIRS

        def whole(eng, b):
            eng.wait_ge(s_x, 2 * (TPB - 1) * (b + 1))
            eng.wait_ge(s_xp, 2 * (b + 1))

        @block.sync
        def _(sp):
            def slot(j, r):
                if there(j + 5):
                    sp.wait_ge(s_a, j + 2)
                    sp.wait_ge(s_place, j + 2)
                    sp.dma_start(xg[(r + 1) % RING][:, :, :], rows_in[j + 5]).then_inc(s_xg[(r + 1) % RING], 16)

            for j in range(RING):
                sp.dma_start(xg[j][:, :, :], rows_in[j]).then_inc(s_xg[j], 16)
            slot(-1, 3)
            slot(0, 0)
            with sp.Fori(0, LOOPS - 1) as i:
                for r in range(1, RING + 1):
                    slot(RING * i + r, r % RING)
            for j in range(RING * (LOOPS - 1) + 1, PAIRS + 1):
                slot(j, j % RING)
            for n in range(RING):
                sp.wait_ge(s_st[n], 32 * (PAIRS // RING))
            for b in range(NB):
                if b >= 2:
                    whole(sp, b - 2)
                for k in range(2):
                    sp.dma_start(yb[b % 2][:, k, :, :], results[:, k, b * TPB:(b + 1) * TPB, :]).then_inc(s_yb[b % 2], 16)
            if out is not None:
                for b in range(NB):
                    whole(sp, b)
                    tiles = slice(b * TPB, (b + 1) * TPB)
                    sp.dma_start(out.rearrange("b (t p) d -> p (b t) d", p=P)[:, tiles, :], x[:, tiles, :]).then_inc(s_out, 16)
                sp.wait_ge(s_out, 16 * NB)

        @block.tensor
        def _(pe):
            word = [None]

            def expert_of(k):
                return (word[0] >> (4 * k)) & (NE - 1)

            def slot(j, r, i=None):
                if j == -1 if i is None and j < 1 else r % 2:
                    m = max(j - 1, 0) // 2 if i is None else 2 * i + (r - 1) // 2
                    word[0] = pe.value_load(c2.experts[0:1, bass.ds(m, 1)])
                back = 1 - r % 2 if i is not None or j > 0 else j - 1
                if there(j + 2):
                    n, w = (r + 2) % RING, r % 2
                    pe.wait_ge(s_xg[n], 16 * ((j + 2) // RING + 1) if i is None else 16 * (i + ((r or RING) + 2) // RING + 1))
                    pe.wait_ge(s_xl, j + 1 + AHEAD)
                    for q in range(2):
                        for h in range(DH):
                            mm = pe.transpose(pa[w][:, q, h * P:(h + 1) * P], xg[n][:, q, h * P:(h + 1) * P], ident[:, :])
                    mm.then_inc(s_a, 1)
                if there(j + 1):
                    w = (r + 1) % 2
                    e = [expert_of(2 * (back + 2) + q) for q in range(2)]
                    pe.wait_ge(s_xh, j + 2)
                    pe.wait_ge(s_xl, j + 2 + AHEAD)
                    pe.wait_ge(s_h, j + AHEAD)
                    for q in range(2):
                        for h in range(DH):
                            mm = products(pe, pb[w][:, q, :], [a[:, w, q * DH + h, :] for a in (xhi, xlo)],
                                          [a[:, bass.ds(e[q], 1), h * 2 * ED:(h + 1) * 2 * ED] for a in (whi, wlo)],
                                          h == 0, h == DH - 1)
                    mm.then_inc(s_b, 1)
                if there(j):
                    w = r % 2
                    pe.wait_ge(s_h, j + 1 + AHEAD)
                    pe.wait_ge(s_hl, j - 1 + AHEAD)
                    for q in range(2):
                        mm = pe.transpose(pc[w][:, q * P:(q + 1) * P], hf[:, w, q, :], ident[:, :])
                    mm.then_inc(s_c, 1)
                if there(j - 1):
                    w = (r - 1) % 2
                    e = [expert_of(2 * back + q) for q in range(2)]
                    pe.wait_ge(s_hh, j)
                    pe.wait_ge(s_hl, j + AHEAD)
                    pe.wait_ge(s_ev, j - 2 + AHEAD)
                    for q in range(2):
                        mm = products(pe, pd[w][:, q, :], [a[:, w, q, :] for a in (hhi, hlo)],
                                      [a[:, bass.ds(e[q], 1), WC:WN] for a in (whi, wlo)], True, True)
                    mm.then_inc(s_d, 1)

            slots(pe, slot)

        @block.scalar
        def _(act):
            def slot(j, r, i=None):
                if there(j + 2):
                    w = r % 2
                    act.wait_ge(s_a, j + 3)
                    act.activation(xhi[:, w, :, :], pa[w][:, :, :].rearrange("p q (h n) -> p (q h) n", n=P), ACT.Copy).then_inc(s_xh, 1)
                if there(j + 1):
                    w = (r + 1) % 2
                    act.wait_ge(s_b, j + 2)
                    act.activation(su[:, w, :, :], pb[w][:, :, 0:ED], ACT.Silu).then_inc(s_su, 1)
                if there(j):
                    w = r % 2
                    act.wait_ge(s_c, j + 1)
                    act.activation(hhi[:, w, :, :], pc[w][:, :].rearrange("p (q n) -> p q n", q=2), ACT.Copy).then_inc(s_hh, 1)
                if there(j - 1):
                    w, n = (r - 1) % 2, (r - 1) % RING
                    act.wait_ge(s_d, j)
                    if i is not None or j > RING:
                        act.wait_ge(s_st[n], 32 * ((j - 1) // RING) if i is None else 32 * i)
                    act.activation(ys[n][:, :, :], pd[w][:, :, :], ACT.Copy).then_inc(s_ev, 1)

            act.sem_inc(s_ev, AHEAD)
            slots(act, slot, 1)
            for b in range(NB):
                t = (b + 1) * TPB - 1
                act.wait_ge(s_yb[b % 2], 32 * (b // 2 + 1))
                for k in range(2):
                    y = yb[b % 2][:, k, TPB - 1, :]
                    act.activation(y, y, ACT.Copy, scale=c2.weight[:, k, t:t + 1]).then_inc(s_yw, 1)

        @block.vector
        def _(dve):
            def slot(j, r, i=None):
                if there(j + 2):
                    w = r % 2
                    dve.wait_ge(s_xh, j + 3)
                    tiles = slice(2 * j + 4, 2 * j + 6) if i is None else bass.ds(2 * j + 4, 2)
                    dve.tensor_copy(place[:, tiles], xg[(r + 2) % RING][:, :, D:D + 1].rearrange("p q o -> p (q o)").bitcast(U32)
                                    ).then_inc(s_place, 1)
                    dve.tensor_tensor(xlo[:, w, :, :], pa[w][:, :, :].rearrange("p q (h n) -> p (q h) n", n=P),
                                      xhi[:, w, :, :].bitcast(F32), ALU.subtract).then_inc(s_xl, 1)
                if there(j + 1):
                    w = (r + 1) % 2
                    dve.wait_ge(s_su, j + 2)
                    dve.tensor_tensor(hf[:, w, :, :], su[:, w, :, :], pb[w][:, :, ED:2 * ED], ALU.mult).then_inc(s_h, 1)
                if there(j):
                    w = r % 2
                    dve.wait_ge(s_hh, j + 1)
                    dve.tensor_tensor(hlo[:, w, :, :], pc[w][:, :].rearrange("p (q n) -> p q n", q=2),
                                      hhi[:, w, :, :].bitcast(F32), ALU.subtract).then_inc(s_hl, 1)

            for s_ in (s_xl, s_h, s_hl):
                dve.sem_inc(s_, AHEAD)
            slots(dve, slot)
            for b in range(NB):
                dve.wait_ge(s_yb[b % 2], 32 * (b // 2 + 1))
                for k in range(2):
                    for j in range(TPB - 1):
                        t = b * TPB + j
                        dve.scalar_tensor_tensor(out=x[:, t, :], in0=yb[b % 2][:, k, j, :], scalar=c2.weight[:, k, t:t + 1],
                                                 in1=x[:, t, :], op0=ALU.mult, op1=ALU.add).then_inc(s_x, 1)
                    dve.wait_ge(s_x, (2 * b + k + 1) * (TPB - 1))

        @block.gpsimd
        def _(pool):
            for j in range(PAIRS):
                pool.wait_ge(s_place, j + 1)
                pool.wait_ge(s_ev, j + 1 + AHEAD)
                for q in range(2):
                    pool.indirect_dma_start(c2.rows_out, bass.IndirectOffsetOnAxis(ap=place[:, 2 * j + q:2 * j + q + 1], axis=0),
                                            ys[j % RING][:, q, :], None).then_inc(s_st[j % RING], 16)
            for b in range(NB):
                t = (b + 1) * TPB - 1
                for k in range(2):
                    pool.wait_ge(s_yw, 2 * b + k + 1)
                    pool.tensor_tensor(x[:, t, :], yb[b % 2][:, k, TPB - 1, :], x[:, t, :], ALU.add).then_inc(s_xp, 1)
                    pool.wait_ge(s_xp, 2 * b + k + 1)


class Routing:
    pass


def mixture(nc, io, tag, x, xt, ident, c2, fetch=None, out=None):
    with ExitStack() as es:
        c = Ctx(nc, es, tag)
        c2.xn = c.sb("xn", [P, NT, D + 1])
        c2.slot = c.sb("slot", [P, 2, NT], U32)
        c2.weight = c.sb("weight", [P, 2, NT])
        c2.experts = c.sb("experts", [1, WORDS], I32)
        whi, wlo = c.sb("whi", [P, NE, WN], F32R), c.sb("wlo", [P, NE, WN], F32R)
        c2.logits = wlo[0:NE, NE - 3:NE, :].rearrange("e n w -> e (n w)").bitcast(F32)
        normalise(nc, tag + "n", x, ident, xt, c2.xn[:, :, 0:D], (io["RwT"], c2.logits), fetch)
        route_and_share(nc, io, tag + "s", x, xt, c2, ident, whi, wlo)
        routed_experts(nc, tag + "e", x, c2, ident, whi, wlo, out)


class RetentionLoads:

    def __init__(self, nc, es, io):
        c = Ctx(nc, es, "rl")
        self.io = io
        self.wst = c.sb("wst", [P, DH, QK + 2 * DVT])
        self.wo = c.sb("wo", [P, DVT // P, D])
        self.cos, self.sin = c.sb("cos", [P, NT, DK]), c.sb("sin", [P, NT, DK])
        self.dec = c.sb("dec", [P, 2 * HB, 1])
        self.mask = c.sb("mask", [P, 1, P])
        self.bd = c.sb("bd", [P, 1, HB // 2, 1])
        self.gdec = c.sb("gdec", [P, 2, NT])
        self.gw = c.sb("gw", [P, 1, DV])
        self.loaded = c.sem("loaded")
        self.count = 0

    def fetch(self, sp):
        io = self.io
        for dst, src in ((self.wst[:, :, :], io["Wret"].rearrange("(h p) n -> p h n", p=P)),
                         (self.cos[:, :, :], io["cos"]), (self.sin[:, :, :], io["sin"]),
                         (self.dec[:, :, 0], io["dec"]), (self.mask[:, 0, :], io["mask"]), (self.bd[:, 0, :, 0], io["bd"]),
                         (self.gdec[:, :, :], io["gdec"]), (self.wo[:, :, :], io["WoB"].rearrange("(c p) n -> p c n", p=P)),
                         (self.gw[:, 0, :], io["gnw"].rearrange("(o n) -> o n", o=1).broadcast_to([P, DV]))):
            sp.dma_start(dst, src).then_inc(self.loaded, 16)
            self.count += 16


def retain(nc, x, xt, ident, loads):
    G = 2
    H4 = HB // G
    W3 = QK + 2 * DVT
    with ExitStack() as es:
        c = Ctx(nc, es, "rt")
        wst, wo, cos, sin, dec, mask, bd, gdec, gw = (
            loads.wst, loads.wo, loads.cos, loads.sin, loads.dec, loads.mask, loads.bd, loads.gdec, loads.gw)
        whi = c.sb("whi", [P, DH, W3], F32R)
        wlo = c.sb("wlo", [P, DH, W3], F32R)
        xs = [[c.sb(f"xs{w}{k}", [P, DH, P], F32R) for k in range(2)] for w in range(2)]
        nhalf = c.sb("nhalf", [P, HB, 1])
        ra, rb, rr = (c.sb(n, [P, 2 * HB, DK]) for n in ("ra", "rb", "rr"))
        qk = c.sb("qk", [P, 2, QK])
        v = c.sb("v", [P, 2, DVT])
        sg = c.sb("sg", [P, HB, DV])
        gate = c.sb("gate", [P, 2, HB, DV])
        qT = c.sb("qT", [P, G, P])
        kT = [c.sb("kT" + n, [P, G, P], F32R) for n in ("hi", "lo")]
        qbd = [c.sb("qbd" + n, [P, G, H4, P], F32R) for n in ("hi", "lo")]
        sc = c.sb("sc", [P, G, H4, P])
        st, sm, sa = (c.sb(n, [P, G, H4, DV]) for n in ("st", "sm", "sa"))
        sq, on = (c.sb(n, [P, HB, DV]) for n in ("sq", "on"))
        ms, mv, rs = (c.sb(n, [P, HB, 1]) for n in ("ms", "mv", "rs"))
        og = c.sb("og", [P, DVT])
        oT = [c.sb("oT" + n, [P, DVT // P, P], F32R) for n in ("hi", "lo")]
        wos = [c.sb("wo" + n, [P, DVT // P, D], F32R) for n in ("hi", "lo")]
        p_qk, p_v, p_g, p_t, p_o, p_y = (c.ps("p_" + n, [P, BLK]) for n in ("qk", "v", "g", "t", "o", "y"))
        p_s = [c.ps(f"p_s{g}", [P, BLK]) for g in range(G)]
        zero = c.sb("zero", [P, H4 * P])
        s_whi, s_wlo, s_zero, s_half, s_blank, s_low = (c.sem(n) for n in ("whi", "wlo", "zero", "half", "blank", "kq_lo"))
        s_xs = [c.sem(f"x_staged{w}") for w in range(2)]
        s_qk, s_v, s_g, s_o, s_st, s_y = (c.sem("mm_" + n) for n in ("qk", "v", "g", "o", "state", "y"))
        s_s = [c.sem(f"mm_scores{g}") for g in range(G)]
        s_tr, s_ot = c.sem("qk_transposed"), c.sem("o_transposed")
        s_rope, s_sum, s_dk, s_gate = (c.sem(n) for n in ("rope_products", "rope_sum", "qk_decayed", "gate"))
        s_vc, s_sg, s_tc, s_bd, s_otc, s_otl = (
            c.sem(n) for n in ("v_copied", "silu", "qkT_copied", "q_block_diag", "oT_hi", "oT_lo"))
        s_sc = [c.sem(f"scores_masked{g}") for g in range(G)]
        s_sm, s_sa, s_state = c.sem("update_masked"), c.sem("state_sum"), c.sem("state_ready")
        s_sq, s_ms, s_mv, s_rs, s_on, s_og, s_x = (c.sem(n) for n in ("sq", "ms", "mv", "rs", "on", "og", "x"))
        block = es.enter_context(nc.Block())

        def wait(eng, sem, value):
            if type(value) is not int or value > 0:
                eng.wait_ge(sem, value)

        def turned(rows, g):
            return p_t[rows, g * P:(g + G) * P].rearrange("p (g n) -> p g n", n=P)

        def slots(eng, slot):
            slot(-1, 1, False, False, True, 1)
            slot(0, 0, False, True, True, 1)
            with eng.Fori(0, NT // 2 - 1) as i:
                slot(2 * i + 1, 1, True, True, True, i + 2)
                slot(2 * i + 2, 0, True, True, True, i + 2)
            slot(NT - 1, 1, True, True, False, None)
            slot(NT, 0, True, False, False, None)

        @block.sync
        def _(sp):
            def stage(t, w):
                for k in range(2):
                    sp.dma_start(xs[w][k][:, :, :].bitcast(F32), xt[k][:, :, :].bitcast(F32).rearrange("p h (t n) -> p t h n", n=P)[:, t, :, :]
                                 ).then_inc(s_xs[w], 16)

            stage(0, 0)
            stage(1, 1)
            with sp.Fori(0, NT // 2 - 1) as i:
                for w in range(2):
                    sp.wait_ge(s_g, 2 * i + w + 1)
                    stage(2 * i + w + 2, w)

        @block.tensor
        def _(pe):
            def project(t, i, w, first):
                pe.wait_ge(s_xs[w], 32 * i)
                for out, col, width, sem, freed in ((p_qk, 0, QK, s_qk, s_rope), (p_v, QK, DVT, s_v, s_vc),
                                                    (p_g, QK + DVT, DVT, s_g, s_sg)):
                    wait(pe, freed, t)
                    if first:
                        pe.wait_ge(s_wlo, col // BLK + 1)
                    for h in range(DH):
                        mm = products(pe, out[:, :], [a[:, h, :] for a in xs[w]],
                                      [a[:, h, col:col + width] for a in (whi, wlo)], h == 0, h == DH - 1)
                    mm.then_inc(sem, 1)

            def slot(t, w, prev, cur, nxt, staged):
                if cur:
                    pe.wait_ge(s_dk, t + 1)
                    wait(pe, s_sm, t)
                    for g in range(2 * G):
                        mm = pe.transpose(p_t[:, g * P:(g + 1) * P], qk[:, w, g * P:(g + 1) * P], ident[:, :])
                    mm.then_inc(s_tr, 1)
                if nxt:
                    project(t + 1, staged, 1 - w, not (prev or cur))
                if cur:
                    pe.wait_ge(s_tc, t + 1)
                    pe.wait_ge(s_low, t + 1)
                    for g in range(G):
                        wait(pe, s_sc[g], t)
                        products(pe, p_s[g][:, :], [a[:, g, :] for a in kT], [a[:, g, :, :] for a in qbd],
                                 True, True).then_inc(s_s[g], 1)
                if prev:
                    pe.wait_ge(s_og, t)
                    wait(pe, s_x, t)
                    for g in range(DVT // P):
                        mm = pe.transpose(p_y[:, g * P:(g + 1) * P], og[:, g * P:(g + 1) * P], ident[:, :])
                    mm.then_inc(s_ot, 1)
                if cur:
                    pe.wait_ge(s_vc, t + 1)
                    for g in range(G):
                        mm = pe.matmul(p_t[:, g * H4 * DV:(g + 1) * H4 * DV], qk[:, w, (G + g) * P:(G + g + 1) * P],
                                       v[:, w, g * H4 * DV:(g + 1) * H4 * DV], start=True, stop=True)
                    mm.then_inc(s_st, 1)
                    pe.wait_ge(s_state, t + 1)
                    pe.wait_ge(s_on, t + 1)
                    for g in range(G):
                        pe.matmul(p_o[:, g * H4 * DV:(g + 1) * H4 * DV], qT[:, g, :], st[:, g, :, :],
                                  start=(g == 0), stop=False, skip_group_check=True)
                    for g in range(G):
                        pe.wait_ge(s_sc[g], t + 1)
                        for h in range(H4):
                            n = g * H4 + h
                            mm = pe.matmul(p_o[:, n * DV:(n + 1) * DV], sc[:, g, h, :], v[:, w, n * DV:(n + 1) * DV],
                                           start=False, stop=(n == HB - 1), skip_group_check=True)
                    mm.then_inc(s_o, 1)
                if prev:
                    pe.wait_ge(s_otl, t)
                    for g in range(DVT // P):
                        mm = products(pe, p_y[:, 0:D], [a[:, g, :] for a in oT], [a[:, g, :] for a in wos],
                                      g == 0, g == DVT // P - 1)
                    mm.then_inc(s_y, 1)

            pe.sem_inc(s_ot, 1)
            slots(pe, slot)

        @block.scalar
        def _(act):
            def slot(t, w, prev, cur, nxt, staged):
                if prev:
                    act.wait_ge(s_o, t)
                    wait(act, s_ms, t)
                    act.activation(sq[:, :, :], p_o[:, :].rearrange("p (h v) -> p h v", v=DV), ACT.Square).then_inc(s_sq, 1)
                if cur:
                    act.wait_ge(s_tr, t + 1)
                    act.activation(kT[0][:, :, :], turned(slice(0, P), G), ACT.Copy)
                    for h in range(H4):
                        rows = slice(h * DK, (h + 1) * DK)
                        ins = act.activation(qbd[0][rows, :, h, :], turned(rows, 0), ACT.Copy)
                    ins.then_inc(s_bd, 1)
                    act.activation(qT[:, :, :], turned(slice(0, P), 0), ACT.Copy).then_inc(s_tc, 1)
                if nxt:
                    act.wait_ge(s_v, t + 2)
                    act.activation(v[:, 1 - w, :], p_v[:, :], ACT.Copy).then_inc(s_vc, 1)
                    act.wait_ge(s_g, t + 2)
                    wait(act, s_gate, t + 1)
                    act.activation(sg[:, :, :], p_g[:, :].rearrange("p (h v) -> p h v", v=DV), ACT.Silu).then_inc(s_sg, 1)
                if prev:
                    act.wait_ge(s_ot, t + 1)
                    act.activation(oT[0][:, :, :], p_y[:, :].rearrange("p (g n) -> p g n", n=P), ACT.Copy).then_inc(s_otc, 1)

            act.wait_ge(loads.loaded, loads.count)
            for k in range(3):
                act.activation(whi[:, :, k * BLK:(k + 1) * BLK], wst[:, :, k * BLK:(k + 1) * BLK], ACT.Copy).then_inc(s_whi, 1)
            act.activation(wos[0][:, :, :], wo[:, :, :], ACT.Copy).then_inc(s_whi, 1)
            act.wait_ge(s_zero, 1)
            for part in qbd:
                for g in range(G):
                    act.activation(part[:, g, :, :].rearrange("p h n -> p (h n)"), zero[:, :], ACT.Copy).then_inc(s_blank, 1)
            act.wait_ge(s_blank, 2 * G)
            slots(act, slot)

        @block.gpsimd
        def _(pool):
            def slot(t, w, prev, cur, nxt, staged):
                if prev:
                    pool.wait_ge(s_mv, t)
                    wait(pool, s_on, t)
                    pool.tensor_tensor(rs[:, :, :], mv[:, :, :], nhalf[:, :, :], ALU.pow).then_inc(s_rs, 1)
                if nxt:
                    pool.wait_ge(s_rope, t + 2)
                    pool.tensor_tensor(rr[:, :, :], ra[:, :, :], rb[:, :, :], ALU.add).then_inc(s_sum, 1)
                    pool.wait_ge(s_sum, t + 2)
                    wait(pool, s_st, t)
                    pool.tensor_tensor(qk[:, 1 - w, :].rearrange("p (h n) -> p h n", n=DK), rr[:, :, :],
                                       dec[:, :, :].broadcast_to([P, 2 * HB, DK]), ALU.mult).then_inc(s_dk, 1)
                    pool.wait_ge(s_sg, t + 2)
                    wait(pool, s_og, t)
                    pool.tensor_tensor(gate[:, 1 - w, :, :], sg[:, :, :], gw[:, :, :].broadcast_to([P, HB, DV]),
                                       ALU.mult).then_inc(s_gate, 1)

            pool.memset(zero[:, :], 0.0).then_inc(s_zero, 1)
            pool.memset(st[:, :, :, :].rearrange("p g h v -> p (g h v)"), 0.0).then_inc(s_state, 1)
            pool.wait_ge(loads.loaded, loads.count)
            pool.memset(nhalf[:, :, :], -0.5).then_inc(s_half, 1)
            pool.wait_ge(s_half, 1)
            pool.sem_inc(s_rs, 1)
            slots(pool, slot)

        @block.vector
        def _(dve):
            def slot(t, w, prev, cur, nxt, staged):
                if prev:
                    dve.wait_ge(s_sq, t)
                    dve.tensor_reduce(ms[:, :, :], sq[:, :, :], AX_X, ALU.add).then_inc(s_ms, 1)
                    dve.wait_ge(s_ms, t + 1)
                    wait(dve, s_rs, t)
                    dve.tensor_scalar(mv[:, :, :], ms[:, :, :], 1.0 / DV, EPS, ALU.mult, ALU.add).then_inc(s_mv, 1)
                if cur:
                    dve.wait_ge(s_bd, t + 1)
                    dve.wait_ge(s_tc, t + 1)
                    dve.tensor_tensor(kT[1][:, :, :], turned(slice(0, P), G), kT[0][:, :, :].bitcast(F32), ALU.subtract)
                    for h in range(H4):
                        rows = slice(h * DK, (h + 1) * DK)
                        ins = dve.tensor_tensor(qbd[1][rows, :, h, :], turned(rows, 0), qbd[0][rows, :, h, :].bitcast(F32), ALU.subtract)
                    ins.then_inc(s_low, 1)
                if prev:
                    dve.wait_ge(s_rs, t + 1)
                    dve.tensor_tensor(on[:, :, :], p_o[:, :].rearrange("p (h v) -> p h v", v=DV),
                                      rs[:, :, :].broadcast_to([P, HB, DV]), ALU.mult).then_inc(s_on, 1)
                    dve.wait_ge(s_on, t + 1)
                    dve.wait_ge(s_gate, t)
                    wait(dve, s_ot, t)
                    dve.tensor_tensor(og[:, :].rearrange("p (h v) -> p h v", v=DV), on[:, :, :], gate[:, 1 - w, :, :],
                                      ALU.mult).then_inc(s_og, 1)
                if nxt:
                    q = p_qk[:, :].rearrange("p (h n) -> p h n", n=DK)
                    dve.wait_ge(s_qk, t + 2)
                    wait(dve, s_sum, t + 1)
                    dve.tensor_tensor(ra[:, :, :], q, cos[:, bass.ds(t + 1, 1), :].broadcast_to([P, 2 * HB, DK]), ALU.mult)
                    for a in range(2):
                        lo, hi = a * DK // 2, (a + 1) * DK // 2
                        ins = dve.tensor_tensor(rb[:, :, lo:hi], q[:, :, DK // 2 - lo:DK - lo],
                                                sin[:, bass.ds(t + 1, 1), lo:hi].broadcast_to([P, 2 * HB, DK // 2]), ALU.mult)
                    ins.then_inc(s_rope, 1)
                if cur:
                    wait(dve, s_o, t)
                    for g in range(G):
                        dve.wait_ge(s_s[g], t + 1)
                        dve.tensor_tensor(sc[:, g, :, :], p_s[g][:, :].rearrange("p (h n) -> p h n", n=P),
                                          mask[:, :, :].broadcast_to([P, H4, P]), ALU.mult).then_inc(s_sc[g], 1)
                if prev:
                    dve.wait_ge(s_otc, t)
                    dve.tensor_tensor(oT[1][:, :, :], p_y[:, :].rearrange("p (g n) -> p g n", n=P), oT[0][:, :, :].bitcast(F32),
                                      ALU.subtract).then_inc(s_otl, 1)
                if cur:
                    dve.wait_ge(s_st, t + 1)
                    dve.tensor_tensor(sm[:, :, :, :], p_t[:, :].rearrange("p (g h v) -> p g h v", g=G, h=H4),
                                      bd[:, :, :, :].broadcast_to([P, G, H4, DV]), ALU.mult).then_inc(s_sm, 1)
                    dve.wait_ge(s_sm, t + 1)
                    dve.wait_ge(s_state, t + 1)
                    dve.tensor_tensor(sa[:, :, :, :], st[:, :, :, :], sm[:, :, :, :], ALU.add).then_inc(s_sa, 1)
                    dve.wait_ge(s_sa, t + 1)
                    dve.wait_ge(s_o, t + 1)
                    for g in range(G):
                        ins = dve.tensor_scalar(st[:, g, :, :], sa[:, g, :, :], gdec[:, g, bass.ds(t, 1)], None, ALU.mult)
                    ins.then_inc(s_state, 1)
                if prev:
                    dve.wait_ge(s_y, t)
                    xv = x[:, t - 1, :]
                    dve.tensor_tensor(xv, p_y[:, 0:D], xv, ALU.add).then_inc(s_x, 1)

            dve.wait_ge(loads.loaded, loads.count)
            for k in range(3):
                cols = slice(k * BLK, (k + 1) * BLK)
                dve.wait_ge(s_whi, k + 1)
                dve.tensor_tensor(wlo[:, :, cols], wst[:, :, cols], whi[:, :, cols].bitcast(F32), ALU.subtract).then_inc(s_wlo, 1)
            dve.wait_ge(s_whi, 4)
            dve.tensor_tensor(wos[1][:, :, :], wo[:, :, :], wos[0][:, :, :].bitcast(F32), ALU.subtract).then_inc(s_wlo, 1)
            for sem in (s_x, s_ms, s_on):
                dve.sem_inc(sem, 1)
            dve.wait_ge(s_blank, 2 * G)
            slots(dve, slot)


def build(nc, io, out, stages=4):
    Ctx.semaphores = []
    with ExitStack() as es:
        c = Ctx(nc, es, "g")
        x = c.sb("x", [P, NT, D])
        xt = [c.sb(n, [P, DH, N], F32R) for n in ("xt_hi", "xt_lo")]
        ident = c.sb("ident", [P, P])
        identb = c.sb("identb", [P, P], BF16)
        c2 = Routing()
        c2.rbias = c.sb("rbias", [P, 1, NE])
        c2.iota = c.sb("iota", [P, 1, TILES])
        c2.sixteens = c.sb("sixteens", [1, 1, 4])
        c2.steps = c.sb("steps", [P, 1, NE])
        c2.lower = c.sb("lower", [P, NE, NE])
        c2.trib = c.sb("trib", [P, P], BF16)
        c2.onesb = c.sb("onesb", [P, P], BF16)
        c2.token = c.sb("token", [P, NT])
        c2.rows_in = nc.dram_tensor("rows_in", [TILES * P, D + 1], F32, kind="Internal").ap()
        c2.rows_out = nc.dram_tensor("rows_out", [2 * N + TILES * P, D], F32, kind="Internal").ap()
        def spare_places(sp, sem):
            with nc.allow_non_contiguous_dma(reason="one word of every row, beside other work"):
                sp.dma_start(c2.rows_in[:, D:D + 1], io["spare"]).then_inc(sem, 16)

        with ExitStack() as es2:
            a = Ctx(nc, es2, "a")
            lora = Lora(nc, es2)
            oall = a.sb("oall", [P, B * DH, 2, 2, BLK])
            vaug = a.sb("vaug", [P, B, DH, KT, HA // DH, 2 * HDA])
            zeros = a.sb("zeros", [P, 2 * D])
            scratch = nc.dram_tensor("qk_parts", [2, 3, B * DH, 2, HPG, HDA, L], BF16, kind="Internal").ap()
            stacks = Stacks(nc, es2, scratch)
            s_rows = a.sem("rows_zeroed")

            def zero_rows(sp):
                for n in range(TILES // 2):
                    sp.dma_start(c2.rows_in.rearrange("(n p a) d -> n p a d", p=P, a=2)[n, :, :, 0:D],
                                 zeros[:, :].rearrange("p (a d) -> p a d", a=2)).then_inc(s_rows, 16)
                spare_places(sp, s_rows)

            with ExitStack() as es3:
                beside = Begin(nc, es3, io, x, ident, identb, c2, lora, vaug, stacks, zeros)
                normalise(nc, "n1", x, ident, xt, beside=beside)
            project_qkv(nc, x, xt, scratch, vaug, lora, stacks)
            attend(nc, vaug, stacks, oall, identb, zero_rows)
            project_out(nc, x, oall, lora.wo, ident)
            with nc.Block() as block:
                @block.gpsimd
                def _(pool):
                    pool.wait_ge(s_rows, 16 * (TILES // 2 + 1))
        if stages >= 2:
            mixture(nc, io, "m2", x, xt, ident, c2)
        clear_semaphores(nc)
        if stages >= 3:
            with ExitStack() as es2:
                loads = RetentionLoads(nc, es2, io)
                s_spare = c.sem("spare_places")

                def fetch(sp):
                    loads.fetch(sp)
                    spare_places(sp, s_spare)

                normalise(nc, "n3", x, ident, xt, fetch=fetch)
                retain(nc, x, xt, ident, loads)
        if stages >= 4:
            mixture(nc, io, "m4", x, xt, ident, c2, lambda sp: sp.wait_ge(s_spare, 16), out)
        else:
            s_out = c.sem("stored")
            with nc.Block() as block:
                @block.sync
                def _(sp):
                    ov = out.rearrange("b (t p) d -> p (b t) d", p=P)
                    for b in range(NB):
                        sp.dma_start(ov[:, b * TPB:(b + 1) * TPB, :], x[:, b * TPB:(b + 1) * TPB, :]).then_inc(s_out, 16)
                    sp.wait_ge(s_out, 16 * NB)


def constants():
    gamma = 1.0 - np.exp2(-5.0 - np.arange(HB, dtype=np.float64))
    inv = 1.0 / 10000.0 ** (np.arange(0, DK, 2, dtype=np.float64) / DK)
    f = np.arange(L, dtype=np.float64)[:, None] * inv[None, :]
    i = np.arange(P, dtype=np.float64)[:, None]
    f4 = np.float32

    def tiles(a):
        return np.tile(a.reshape(KT, P, -1).transpose(1, 0, 2), (1, B, 1))

    gdec = np.zeros((P, 2, NT))
    for g in range(2):
        gdec[:, g, :] = (gamma[g * 4 + np.arange(P) // 32] ** P)[:, None]
    gdec[:, :, KT - 1::KT] = 0.0
    return {
        "cos": tiles(np.concatenate([np.cos(f), np.cos(f)], 1)).astype(f4),
        "sin": tiles(np.concatenate([-np.sin(f), np.sin(f)], 1)).astype(f4),
        "dec": np.concatenate([gamma ** i * DK ** -0.5, gamma ** -i], 1).astype(f4),
        "mask": (np.arange(P)[None, :] >= np.arange(P)[:, None]).astype(f4),
        "bd": (np.arange(P)[:, None] // 32 == np.arange(4)[None, :]).astype(f4),
        "gdec": gdec.astype(f4),
        "ident": np.eye(P, dtype=f4),
        "token": (P * np.arange(NT)[None, :] + np.arange(P)[:, None]).astype(f4),
        "spare": np.arange(2 * N, 2 * N + TILES * P, dtype=np.uint32).view(f4)[:, None],
        "iota": np.arange(TILES, dtype=f4),
        "sixteens": (16.0 ** np.arange(4)).astype(f4),
        "steps": (P * np.arange(NE)).astype(f4),
        "lower": (np.arange(NE)[None, :] < np.arange(NE)[:, None]).astype(f4).reshape(-1),
        "tri": (np.arange(P)[:, None] < np.arange(P)[None, :]).astype(f4),
    }


def lay_out(i):
    g = {k.replace("L0_", ""): np.asarray(v) for k, v in i.items()}
    a = lambda n: [g[f"attn_a_{n}{m}"] for m in "qkvo"]
    sh = [g["ffn_Su"][0], g["ffn_Sg"][0], g["ffn_Sd"][0]]
    up = np.concatenate([np.stack([g["ffn_Wu"], g["ffn_Wg"]], 2).reshape(NE, D, 2 * ED),
                         np.stack([np.concatenate([sh[0][:, k * ED:(k + 1) * ED], sh[1][:, k * ED:(k + 1) * ED]], 1)
                                   for k in range(2)])], 0)
    dn = np.concatenate([g["ffn_Wd"], sh[2].reshape(2, ED, D)], 0)
    return {
        "x": g["attn_a_x"],
        "WT": np.stack([w.T for w in a("W")]), "bias": np.stack(a("b")),
        "biasT": np.stack(a("b")[:3]).reshape(3, DH, P).transpose(2, 0, 1),
        "Bm": np.stack(a("B")), "AmT": np.stack([m.T for m in a("A")]),
        "RwT": np.ascontiguousarray(g["ffn_router_w"].T), "rbias": g["ffn_router_bias"],
        "Wup": up, "Wdn": dn,
        "Wret": np.concatenate([g[f"attn_b_W{m}"] for m in "qkvg"], 1), "WoB": g["attn_b_Wo"],
        "gnw": g["attn_b_g_norm_weight"],
    } | constants()


def kernel(**inputs):
    import concourse.bacc as bacc
    from concourse.bass_utils import run_bass_kernel_spmd

    nc = bacc.Bacc("TRN2", target_bir_lowering=False, num_devices=1)
    arrays = {f"in_{k}": np.ascontiguousarray(v) for k, v in lay_out(inputs).items()}
    io = {k[3:]: nc.dram_tensor(k, v.shape, mybir.dt.from_np(v.dtype), kind="ExternalInput").ap()
          for k, v in arrays.items()}
    out = nc.dram_tensor("out_x", [B, L, D], F32, kind="ExternalOutput").ap()
    build(nc, io, out)
    r = run_bass_kernel_spmd(nc, [arrays], core_ids=[0])
    return r.results[0]["out_x"]
```
